# Optimizing a Trainium2 kernel written in Bass

```python
import numpy as np
import jax
import jax.numpy as jnp

def _softmax(x, axis=-1):
    return jax.nn.softmax(x, axis=axis)

def _gelu(x):
    return jax.nn.gelu(x, approximate=True)

def _silu(x):
    return jax.nn.silu(x)

def _sigmoid(x):
    return jax.nn.sigmoid(x)

def _layernorm(x, axis=-1, eps=1e-05):
    m = jnp.mean(x, axis=axis, keepdims=True)
    v = jnp.var(x, axis=axis, keepdims=True)
    return (x - m) / jnp.sqrt(v + eps)

def _scatter_add(tgt, idx, src, axis=0):
    return tgt.at[idx].add(src)

def _segment_sum(src, seg, n):
    return jax.ops.segment_sum(src, seg, n)
kernel_name = 'mk_decoder_postln_d2_seqx_r4_ba80df'

def setup_inputs(seed: int=0):
    np.random.seed(seed)
    _w = jnp.asarray

    def _rec_inputs():
        import jax
        import jax.numpy as jnp
        _rk = jax.random.key(seed)
        x = 7.22e-05 + 1 * jax.random.normal(jax.random.fold_in(_rk, 1), (4, 512, 256), jnp.float32)
        _lenS = 512 - jax.random.randint(jax.random.fold_in(_rk, 7), (4,), 0, max(1, 512 // 4) + 1, jnp.int32)
        _lenS2 = 512 - jax.random.randint(jax.random.fold_in(_rk, 8), (4,), 0, max(1, 512 // 4) + 1, jnp.int32)
        _ctx_768P = jax.random.normal(jax.random.fold_in(_rk, 11), (4, 16, 192), jnp.float32)
        _ctx_768c = jax.random.dirichlet(jax.random.fold_in(_rk, 511), 0.3 * jnp.ones((16,), jnp.float32), (4, 512))
        _ctx_768t = jnp.einsum('bsk,bkd->bsd', _ctx_768c, _ctx_768P)
        _ctx_768t = _ctx_768t * jax.lax.rsqrt(jnp.mean(jnp.square(_ctx_768t)) + 1e-12) * 0.953939
        ctx_768 = -7.36909e-05 + 0.999899 * (_ctx_768t + 0.3 * jax.random.normal(jax.random.fold_in(_rk, 611), (4, 512, 192), jnp.float32))
        return (x, ctx_768)
    x, ctx_768 = _rec_inputs()

    def _L0_attn_setup():
        import jax, jax.numpy as jnp
        import numpy as np
        B, L, D, ORDER = (2, 2048, 256, 2)
        HID = 64

        def _fft_conv(x, h):
            Ln = x.shape[-1]
            n = 2 * Ln
            xf = jnp.fft.rfft(x, n=n)
            hf = jnp.fft.rfft(h, n=n)
            return jnp.fft.irfft(xf * hf[None], n=n)[..., :Ln]
        key = jax.random.key(seed)
        ks = jax.random.split(key, 7)

        def w(k, shape, fan_in):
            return jax.random.normal(k, shape, jnp.float32) / np.float32(np.sqrt(fan_in))
        return {'x': jax.random.normal(ks[0], (B, L, D), jnp.float32), 'W_in': w(ks[1], ((ORDER + 1) * D, D), D), 'W_out': w(ks[2], (D, D), D), 'f_w1': w(ks[3], (ORDER, HID, 1), 1), 'f_b1': jnp.zeros((ORDER, HID), jnp.float32), 'f_w2': w(ks[4], (ORDER, D, HID), HID), 'f_b2': jnp.zeros((ORDER, D), jnp.float32)}
    _L0_attn_all = _L0_attn_setup()
    _L0_attn_in = {k: v for k, v in _L0_attn_all.items() if k in ('W_in', 'W_out', 'f_w1', 'f_b1', 'f_w2', 'f_b2')}
    del _L0_attn_all

    def _L0_xattn_setup():
        import jax, jax.numpy as jnp
        import numpy as np
        NUM_HEADS = 16
        HEAD_DIM = 64
        INNER = NUM_HEADS * HEAD_DIM
        QUERY_DIM = 256
        CONTEXT_DIM = 192
        SCALE = HEAD_DIM ** (-0.5)
        key = jax.random.key(seed)
        ks = jax.random.split(key, 6)
        B, NQ, NKV = (8, 256, 512)
        query = jax.random.normal(ks[0], (B, NQ, QUERY_DIM), dtype=jnp.float32)
        context = jax.random.normal(ks[1], (B, NKV, CONTEXT_DIM), dtype=jnp.float32)
        w_q = jax.random.normal(ks[2], (QUERY_DIM, INNER), dtype=jnp.float32) * QUERY_DIM ** (-0.5)
        w_kv = jax.random.normal(ks[3], (CONTEXT_DIM, 2 * INNER), dtype=jnp.float32) * CONTEXT_DIM ** (-0.5)
        w_out = jax.random.normal(ks[4], (INNER, QUERY_DIM), dtype=jnp.float32) * INNER ** (-0.5)
        b_out = jax.random.normal(ks[5], (QUERY_DIM,), dtype=jnp.float32) * 0.01
        return {'query': query, 'context': context, 'w_q': w_q, 'w_kv': w_kv, 'w_out': w_out, 'b_out': b_out}
    _L0_xattn_all = _L0_xattn_setup()
    _L0_xattn_in = {k: v for k, v in _L0_xattn_all.items() if k in ('w_q', 'w_kv', 'w_out', 'b_out')}
    del _L0_xattn_all

    def _L0_ffn_setup():
        import jax, jax.numpy as jnp
        import numpy as np
        E = 8
        D = 256
        H = 512
        TOP_K = 2
        key = jax.random.key(seed)
        k_x, k_g, k_w1, k_w2 = jax.random.split(key, 4)
        B, S = (4, 512)
        inp = {'input': jax.random.normal(k_x, (B, S, D), dtype=jnp.float32), 'Wg': jax.random.normal(k_g, (D, E), dtype=jnp.float32) * 0.02, 'W1': jax.random.normal(k_w1, (E, D, H), dtype=jnp.float32) * 0.02, 'b1': jnp.zeros((E, H), dtype=jnp.float32), 'W2': jax.random.normal(k_w2, (E, H, D), dtype=jnp.float32) * 0.02, 'b2': jnp.zeros((E, D), dtype=jnp.float32)}
        return inp
    _L0_ffn_all = _L0_ffn_setup()
    _L0_ffn_in = {k: v for k, v in _L0_ffn_all.items() if k in ('Wg', 'W1', 'b1', 'W2', 'b2')}
    del _L0_ffn_all

    def _L1_attn_setup():
        import jax, jax.numpy as jnp
        import numpy as np
        B, L, D_MODEL, H = (4, 512, 256, 16)
        HD = D_MODEL // H
        EPS = 1e-06
        key = jax.random.key(seed)
        ks = jax.random.split(key, 9)
        s = 1.0 / np.sqrt(D_MODEL)
        return {'x': jax.random.normal(ks[0], (B, L, D_MODEL), dtype=jnp.float32), 'Wq': jax.random.normal(ks[1], (D_MODEL, D_MODEL), dtype=jnp.float32) * s, 'bq': jax.random.normal(ks[2], (D_MODEL,), dtype=jnp.float32) * 0.01, 'Wk': jax.random.normal(ks[3], (D_MODEL, D_MODEL), dtype=jnp.float32) * s, 'bk': jax.random.normal(ks[4], (D_MODEL,), dtype=jnp.float32) * 0.01, 'Wv': jax.random.normal(ks[5], (D_MODEL, D_MODEL), dtype=jnp.float32) * s, 'bv': jax.random.normal(ks[6], (D_MODEL,), dtype=jnp.float32) * 0.01, 'Wo': jax.random.normal(ks[7], (D_MODEL, D_MODEL), dtype=jnp.float32) * s, 'bo': jax.random.normal(ks[8], (D_MODEL,), dtype=jnp.float32) * 0.01}
    _L1_attn_all = _L1_attn_setup()
    _L1_attn_in = {k: v for k, v in _L1_attn_all.items() if k in ('Wq', 'bq', 'Wk', 'bk', 'Wv', 'bv', 'Wo', 'bo')}
    del _L1_attn_all

    def _L1_xattn_setup():
        import jax, jax.numpy as jnp
        import numpy as np
        DIM_Q = 256
        DIM_KV = 192
        N_HEADS = 4

        def _split_heads(x):
            b, l, d = x.shape
            return x.reshape(b, l, N_HEADS, d // N_HEADS).transpose(0, 2, 1, 3)
        key = jax.random.key(seed)
        ks = jax.random.split(key, 7)
        b, lq, lkv = (4, 512, 512)
        q = jax.random.normal(ks[0], (b, lq, DIM_Q), dtype=jnp.float32)
        kv = jax.random.normal(ks[1], (b, lkv, DIM_KV), dtype=jnp.float32)
        s_q = 1.0 / np.sqrt(DIM_Q)
        s_kv = 1.0 / np.sqrt(DIM_KV)
        Wq = jax.random.normal(ks[2], (DIM_Q, DIM_Q), dtype=jnp.float32) * s_q
        Wk = jax.random.normal(ks[3], (DIM_Q, DIM_KV), dtype=jnp.float32) * s_kv
        Wv = jax.random.normal(ks[4], (DIM_Q, DIM_KV), dtype=jnp.float32) * s_kv
        Wo = jax.random.normal(ks[5], (DIM_Q, DIM_Q), dtype=jnp.float32) * s_q
        bo = jax.random.normal(ks[6], (DIM_Q,), dtype=jnp.float32) * 0.01
        return {'q': q, 'kv': kv, 'Wq': Wq, 'Wk': Wk, 'Wv': Wv, 'Wo': Wo, 'bo': bo}
    _L1_xattn_all = _L1_xattn_setup()
    _L1_xattn_in = {k: v for k, v in _L1_xattn_all.items() if k in ('Wq', 'Wk', 'Wv', 'Wo', 'bo')}
    del _L1_xattn_all

    def _L1_ffn_setup():
        import jax, jax.numpy as jnp
        import numpy as np
        B, S, D, F, E, TOP_K = (4, 512, 256, 1024, 8, 2)
        LN_EPS = 1e-05
        key = jax.random.key(seed)
        ks = jax.random.split(key, 4)
        sc = lambda fan_in: 1.0 / np.sqrt(fan_in)
        return {'x': jax.random.normal(ks[0], (B, S, D), jnp.float32), 'W1': jax.random.normal(ks[1], (E, D, F), jnp.float32) * sc(D), 'b1': jnp.zeros((E, F), jnp.float32), 'W2': jax.random.normal(ks[2], (E, F, D), jnp.float32) * sc(F), 'b2': jnp.zeros((E, D), jnp.float32), 'Wr': jax.random.normal(ks[3], (D, E), jnp.float32) * sc(D), 'br': jnp.zeros((E,), jnp.float32), 'gamma': jnp.ones((D,), jnp.float32), 'beta': jnp.zeros((D,), jnp.float32)}
    _L1_ffn_all = _L1_ffn_setup()
    _L1_ffn_in = {k: v for k, v in _L1_ffn_all.items() if k in ('W1', 'b1', 'W2', 'b2', 'Wr', 'br', 'gamma', 'beta')}
    del _L1_ffn_all
    return {'x': x, 'ctx_768': ctx_768, 'L0_attn_W_in': _L0_attn_in['W_in'], 'L0_attn_W_out': _L0_attn_in['W_out'], 'L0_attn_f_w1': _L0_attn_in['f_w1'], 'L0_attn_f_b1': _L0_attn_in['f_b1'], 'L0_attn_f_w2': _L0_attn_in['f_w2'], 'L0_attn_f_b2': _L0_attn_in['f_b2'], 'L0_xattn_w_q': _L0_xattn_in['w_q'], 'L0_xattn_w_kv': _L0_xattn_in['w_kv'], 'L0_xattn_w_out': _L0_xattn_in['w_out'], 'L0_xattn_b_out': _L0_xattn_in['b_out'], 'L0_ffn_Wg': _L0_ffn_in['Wg'], 'L0_ffn_W1': _L0_ffn_in['W1'], 'L0_ffn_b1': _L0_ffn_in['b1'], 'L0_ffn_W2': _L0_ffn_in['W2'], 'L0_ffn_b2': _L0_ffn_in['b2'], 'L1_attn_Wq': _L1_attn_in['Wq'], 'L1_attn_bq': _L1_attn_in['bq'], 'L1_attn_Wk': _L1_attn_in['Wk'], 'L1_attn_bk': _L1_attn_in['bk'], 'L1_attn_Wv': _L1_attn_in['Wv'], 'L1_attn_bv': _L1_attn_in['bv'], 'L1_attn_Wo': _L1_attn_in['Wo'], 'L1_attn_bo': _L1_attn_in['bo'], 'L1_xattn_Wq': _L1_xattn_in['Wq'], 'L1_xattn_Wk': _L1_xattn_in['Wk'], 'L1_xattn_Wv': _L1_xattn_in['Wv'], 'L1_xattn_Wo': _L1_xattn_in['Wo'], 'L1_xattn_bo': _L1_xattn_in['bo'], 'L1_ffn_W1': _L1_ffn_in['W1'], 'L1_ffn_b1': _L1_ffn_in['b1'], 'L1_ffn_W2': _L1_ffn_in['W2'], 'L1_ffn_b2': _L1_ffn_in['b2'], 'L1_ffn_Wr': _L1_ffn_in['Wr'], 'L1_ffn_br': _L1_ffn_in['br'], 'L1_ffn_gamma': _L1_ffn_in['gamma'], 'L1_ffn_beta': _L1_ffn_in['beta']}

def reference(x, ctx_768, L0_attn_W_in, L0_attn_W_out, L0_attn_f_w1, L0_attn_f_b1, L0_attn_f_w2, L0_attn_f_b2, L0_xattn_w_q, L0_xattn_w_kv, L0_xattn_w_out, L0_xattn_b_out, L0_ffn_Wg, L0_ffn_W1, L0_ffn_b1, L0_ffn_W2, L0_ffn_b2, L1_attn_Wq, L1_attn_bq, L1_attn_Wk, L1_attn_bk, L1_attn_Wv, L1_attn_bv, L1_attn_Wo, L1_attn_bo, L1_xattn_Wq, L1_xattn_Wk, L1_xattn_Wv, L1_xattn_Wo, L1_xattn_bo, L1_ffn_W1, L1_ffn_b1, L1_ffn_W2, L1_ffn_b2, L1_ffn_Wr, L1_ffn_br, L1_ffn_gamma, L1_ffn_beta):
    import jax
    import jax.numpy as jnp

    def _L0_attn_ref(x, W_in, W_out, f_w1, f_b1, f_w2, f_b2):
        import jax, jax.numpy as jnp
        import numpy as np
        B, L, D, ORDER = (2, 2048, 256, 2)
        HID = 64

        def _fft_conv(x, h):
            Ln = x.shape[-1]
            n = 2 * Ln
            xf = jnp.fft.rfft(x, n=n)
            hf = jnp.fft.rfft(h, n=n)
            return jnp.fft.irfft(xf * hf[None], n=n)[..., :Ln]
        Bn, Ln, Dn = x.shape
        proj = x @ W_in.T
        splits = jnp.split(proj, ORDER + 1, axis=-1)
        v = jnp.swapaxes(splits[0], 1, 2)
        t = jnp.linspace(0.0, 1.0, Ln, dtype=x.dtype)[:, None]
        for i in range(ORDER):
            h = jax.nn.silu(t @ f_w1[i].T + f_b1[i]) @ f_w2[i].T + f_b2[i]
            v = _fft_conv(v, h.T)
            v = v * jnp.swapaxes(splits[i + 1], 1, 2)
        out = jnp.swapaxes(v, 1, 2)
        return out @ W_out.T

    def _L0_xattn_ref(query, context, w_q, w_kv, w_out, b_out):
        import jax, jax.numpy as jnp
        import numpy as np
        NUM_HEADS = 16
        HEAD_DIM = 64
        INNER = NUM_HEADS * HEAD_DIM
        QUERY_DIM = 256
        CONTEXT_DIM = 192
        SCALE = HEAD_DIM ** (-0.5)
        B, NQ, _ = query.shape
        NKV = context.shape[1]
        q = query @ w_q
        kv = context @ w_kv
        k, v = jnp.split(kv, 2, axis=-1)
        q = q.reshape(B, NQ, NUM_HEADS, HEAD_DIM).transpose(0, 2, 1, 3)
        k = k.reshape(B, NKV, NUM_HEADS, HEAD_DIM).transpose(0, 2, 1, 3)
        v = v.reshape(B, NKV, NUM_HEADS, HEAD_DIM).transpose(0, 2, 1, 3)
        scores = jnp.einsum('bhqd,bhkd->bhqk', q, k) * SCALE
        attn = jax.nn.softmax(scores, axis=-1)
        out = jnp.einsum('bhqk,bhkd->bhqd', attn, v)
        out = out.transpose(0, 2, 1, 3).reshape(B, NQ, INNER)
        return out @ w_out + b_out

    def _L0_ffn_ref(input, Wg, W1, b1, W2, b2):
        import jax, jax.numpy as jnp
        import numpy as np
        E = 8
        D = 256
        H = 512
        TOP_K = 2
        logits = jnp.einsum('bsd,de->bse', input, Wg)
        probs = jax.nn.softmax(logits, axis=-1)
        top_vals, top_idx = jax.lax.top_k(probs, TOP_K)
        top_vals = top_vals / jnp.sum(top_vals, axis=-1, keepdims=True)
        onehot = jax.nn.one_hot(top_idx, E, dtype=input.dtype)
        mask = jnp.sum(onehot, axis=2)
        scores = jnp.sum(onehot * top_vals[..., None], axis=2)
        xm = input[None] * jnp.moveaxis(mask, -1, 0)[..., None]
        h = jnp.einsum('ebsd,edh->ebsh', xm, W1) + b1[:, None, None, :]
        h = jax.nn.relu(h)
        y = jnp.einsum('ebsh,ehd->ebsd', h, W2) + b2[:, None, None, :]
        out = jnp.sum(y * jnp.moveaxis(scores, -1, 0)[..., None], axis=0)
        return out

    def _L1_attn_ref(x, Wq, bq, Wk, bk, Wv, bv, Wo, bo):
        import jax, jax.numpy as jnp
        import numpy as np
        B, L, D_MODEL, H = (4, 512, 256, 16)
        HD = D_MODEL // H
        EPS = 1e-06
        b, l, _ = x.shape
        s = l

        def proj(W, bias):
            return (x @ W.T + bias).reshape(b, l, H, HD).transpose(0, 2, 1, 3)
        q = jax.nn.sigmoid(proj(Wq, bq))
        k = jax.nn.sigmoid(proj(Wk, bk))
        v = proj(Wv, bv)
        sink_incoming = 1.0 / jnp.einsum('nhld,nhd->nhl', q + EPS, k.sum(axis=2) + EPS)
        source_outgoing = 1.0 / jnp.einsum('nhld,nhd->nhl', k + EPS, q.sum(axis=2) + EPS)
        conserved_sink = jnp.einsum('nhld,nhd->nhl', q + EPS, (k * source_outgoing[..., None]).sum(axis=2) + EPS)
        conserved_source = jnp.einsum('nhld,nhd->nhl', k + EPS, (q * sink_incoming[..., None]).sum(axis=2) + EPS)
        conserved_source = jnp.clip(conserved_source, -1.0, 1.0)
        sink_allocation = jax.nn.sigmoid(conserved_sink * (float(l) / float(s)))
        source_competition = jax.nn.softmax(conserved_source, axis=-1) * float(s)
        kv = jnp.einsum('nhld,nhlm->nhdm', k, v * source_competition[..., None])
        out = jnp.einsum('nhld,nhdm->nhlm', q * sink_incoming[..., None], kv)
        out = out * sink_allocation[..., None]
        out = out.transpose(0, 2, 1, 3).reshape(b, l, D_MODEL)
        return out @ Wo.T + bo

    def _L1_xattn_ref(q, kv, Wq, Wk, Wv, Wo, bo):
        import jax, jax.numpy as jnp
        import numpy as np
        DIM_Q = 256
        DIM_KV = 192
        N_HEADS = 4

        def _split_heads(x):
            b, l, d = x.shape
            return x.reshape(b, l, N_HEADS, d // N_HEADS).transpose(0, 2, 1, 3)
        qp = q @ Wq.T
        kp = kv @ Wk.T
        vp = kv @ Wv.T
        qh, kh, vh = (_split_heads(qp), _split_heads(kp), _split_heads(vp))
        scale = (DIM_Q // N_HEADS) ** (-0.5)
        scores = jnp.einsum('bhqd,bhkd->bhqk', qh, kh) * scale
        attn = jax.nn.softmax(scores, axis=-1)
        ctx = jnp.einsum('bhqk,bhkd->bhqd', attn, vh)
        b, h, lq, hd = ctx.shape
        ctx = ctx.transpose(0, 2, 1, 3).reshape(b, lq, h * hd)
        return ctx @ Wo.T + bo

    def _L1_ffn_ref(x, W1, b1, W2, b2, Wr, br, gamma, beta):
        import jax, jax.numpy as jnp
        import numpy as np
        B, S, D, F, E, TOP_K = (4, 512, 256, 1024, 8, 2)
        LN_EPS = 1e-05
        b, s, d = x.shape
        e = Wr.shape[1]
        rw = jax.nn.softmax(x.mean(axis=1) @ Wr + br, axis=-1)
        x_flat = x.reshape(-1, d)
        rw_tok = jnp.repeat(rw, s, axis=0)
        tk_w, tk_i = jax.lax.top_k(rw_tok, TOP_K)
        tk_w = jax.nn.softmax(tk_w, axis=-1)
        h = jax.nn.gelu(jnp.einsum('nd,edf->enf', x_flat, W1) + b1[:, None, :], approximate=False)
        expert_out = jnp.einsum('enf,efd->end', h, W2) + b2[:, None, :]
        onehot = jax.nn.one_hot(tk_i, e, dtype=x.dtype)
        cw = jnp.einsum('nk,nke->ne', tk_w, onehot)
        out = jnp.einsum('ne,end->nd', cw, expert_out).reshape(b, s, d)
        y = out + x
        mu = y.mean(axis=-1, keepdims=True)
        var = y.var(axis=-1, keepdims=True)
        return (y - mu) / jnp.sqrt(var + LN_EPS) * gamma + beta
    x = _layernorm(x + _L0_attn_ref(x, L0_attn_W_in, L0_attn_W_out, L0_attn_f_w1, L0_attn_f_b1, L0_attn_f_w2, L0_attn_f_b2), axis=-1)
    x = _layernorm(x + _L0_xattn_ref(x, ctx_768, L0_xattn_w_q, L0_xattn_w_kv, L0_xattn_w_out, L0_xattn_b_out), axis=-1)
    x = _layernorm(x + _L0_ffn_ref(x, L0_ffn_Wg, L0_ffn_W1, L0_ffn_b1, L0_ffn_W2, L0_ffn_b2), axis=-1)
    x = _layernorm(x + _L1_attn_ref(x, L1_attn_Wq, L1_attn_bq, L1_attn_Wk, L1_attn_bk, L1_attn_Wv, L1_attn_bv, L1_attn_Wo, L1_attn_bo), axis=-1)
    x = _layernorm(x + _L1_xattn_ref(x, ctx_768, L1_xattn_Wq, L1_xattn_Wk, L1_xattn_Wv, L1_xattn_Wo, L1_xattn_bo), axis=-1)
    x = _layernorm(x + _L1_ffn_ref(x, L1_ffn_W1, L1_ffn_b1, L1_ffn_W2, L1_ffn_b2, L1_ffn_Wr, L1_ffn_br, L1_ffn_gamma, L1_ffn_beta), axis=-1)
    return x

_drawn_inputs = setup_inputs


def setup_inputs(seed=0):
    import zlib

    import numpy as np

    out = dict(_drawn_inputs(seed))
    spreads = {'L0_attn_f_b1': (0.0, 0.1),
     'L0_attn_f_b2': (0.0, 0.1),
     'L0_ffn_b1': (0.0, 0.4),
     'L0_ffn_b2': (0.0, 0.1),
     'L1_ffn_b1': (0.0, 0.345),
     'L1_ffn_b2': (0.0, 0.1),
     'L1_ffn_br': (0.0, 0.8),
     'L1_ffn_gamma': (1.0, 0.2),
     'L1_ffn_beta': (0.0, 0.1)}
    factors = {'L0_xattn_b_out': 4.45,
     'L1_attn_Wq': 7.096,
     'L1_attn_bq': 200.0,
     'L1_attn_Wk': 3.872,
     'L1_attn_bk': 200.0,
     'L1_attn_bv': 8.0,
     'L1_attn_bo': 6.88,
     'L1_xattn_bo': 6.151}
    for name, (base, spread) in spreads.items():
        noise = np.random.default_rng([zlib.crc32(name.encode()), seed]).standard_normal(out[name].shape)
        drawn = base * np.exp(spread * noise) if base else spread * noise
        out[name] = jnp.asarray(drawn.astype(out[name].dtype))
    for name, factor in factors.items():
        out[name] = (out[name] * factor).astype(out[name].dtype)
    return out
```

```python
from contextlib import ExitStack

import numpy as np

import concourse.bass as bass
from concourse import mybir

F32 = mybir.dt.float32
I32 = mybir.dt.int32
ALU = mybir.AluOpType
ACT = mybir.ActivationFunctionType
AX = mybir.AxisListType

P = 128
B, L, D = 4, 512, 256
T = B * L
NT = T // P
DK = D // P
DC = 192
E8 = 8
HID = 64
DH = 64
FF0, FF1 = 512, 1024
LN_EPS = 1e-5
FLOW_EPS = 1e-6


def build(nc, I, out):
    with ExitStack() as ctx:
        def sb(name, shape, dt=F32):
            return ctx.enter_context(nc.sbuf_tensor(name, shape, dt))

        def sem(name):
            return ctx.enter_context(nc.semaphore(name))

        x_tok = sb("x_tok", [P, NT, D])
        x_feat = sb("x_feat", [P, DK, T])
        ident = sb("ident", [P, P])
        head_mask = sb("head_mask", [P, P])
        rank8 = sb("rank8", [P, E8])
        bias_row = sb("bias_row", [P, 3, D])
        gb_row = sb("gb_row", [P, 2, D])
        ones = sb("ones", [P, P])
        ln_stat = sb("ln_stat", [P, NT, 6])
        ln_mv = sb("ln_mv", [P, NT, 2])
        ln_std = sb("ln_std", [P, NT])
        ln_rstd = sb("ln_rstd", [P, NT])
        eps_col = sb("eps_col", [P, 1])
        at_negmax = sb("at_negmax", [P, 2])
        at_inv = sb("at_inv", [P, 2])
        arena = sb("arena", [P, 42880])
        psum = ctx.enter_context(nc.psum_tensor("psum", [P, 8, 512], F32))

        class Carve:
            def __init__(self, at=0):
                self.at = at

            def __call__(self, *dims):
                n = int(np.prod(dims))
                a = arena[:, self.at:self.at + n]
                self.at += n
                assert self.at <= 42880, self.at
                if len(dims) > 1:
                    names = "abcdef"[:len(dims)]
                    a = a.rearrange(f"p ({' '.join(names)}) -> p {' '.join(names)}",
                                    **{k: v for k, v in zip(names, dims)})
                return a

        c = Carve()
        hy_gate1 = c(4, B, D)
        hy_v = c(4, B, D)
        hy_gate2 = c(DK, T)
        hy_x = c(2, 2, 512)
        hy_a = c(2, 2, 512)
        hy_b = c(2, 2, 512)
        hy_odd = c(2, 512)
        hy_sd = c(2, 2, 2, 2, 512)
        hy_spec = c(2, 2, 2, 512)
        hy_fwd = c(4, 4, P)
        hy_inv = c(2, 2, 2, D)
        hy_win = c(DK, 3 * D)
        hy_wout = c(DK, D)
        hy_end = c.at
        c = Carve(2 * 4096 + 4096 + 3 * 2048 + 1024)
        hy_time = c(L)
        hy_phi = c(2, L)
        hy_sig = c(2, L)
        hy_w1 = c(2)
        hy_b1 = c(2)
        hy_w2 = c(2, D)
        hy_h = c(4, 2 * D)

        ctx_feat = Carve(0)(DK, T)
        c = Carve(4096)
        at_wout = c(8, D)
        at_w = c(6, P)
        at_q = c(2, B, L)
        at_k = c(B, L)
        at_v = c(B, 4, 130)
        at_p = c(2, L)
        at_pt = c(2, L)
        at_o = c(2, P)
        at_ot = c(2, P)
        at_end = c.at

        c = Carve(at_end)
        mo_w1 = c(2, DK * FF0 + 4)
        mo_w2 = c(2, 4, D)
        mo_h = c(2, 4, 512)
        mo_wg = c(DK, E8)
        mo_b2 = c(D)
        mo_logit = c(NT, E8)
        mo_z = c(NT, E8)
        mo_e = c(NT, E8)
        mo_pr = c(NT, E8)
        mo_oh1 = c(NT, E8)
        mo_oh2 = c(NT, E8)
        mo_t = c(NT, E8)
        mo_m = c(6, NT)
        mo_score = c(NT, P)
        mo_scol = c(2, NT)
        mo_st = c(NT * P)
        mo_end = c.at

        c = Carve(4096)
        fl_w = c(4, DK, D)
        fl_bias = c(3, DK)
        fl_k = c(DK, T)
        fl_q = c(DK, T)
        fl_v = c(DK, T)
        fl_ke = c(DK, T)
        fl_qe = c(DK, T)
        fl_alloc = c(DK, T)
        fl_mask = c(8, 4, P)
        fl_sum = c(8, 4)
        fl_sume = c(8, 4)
        fl_tmp = c(2, 512)
        fl_clip = c(2, 512)
        fl_col = c(8, 4)
        fl_ktok = c(2, 512)
        fl_vtok = c(2, 512)
        fl_kv = c(2, P)
        c = Carve(0)
        se_h = c(2, 8, 512)
        c = Carve(at_end)
        se_w1 = c(2, DK * FF1 + 8)
        se_w2 = c(2, 8 * D + D)
        se_wr = c(DK, E8)
        se_br = c(E8)
        se_mean = c(DK, B)
        se_logit = c(B, E8)
        se_z = c(B, E8)
        se_e = c(B, E8)
        se_pr = c(B, E8)
        se_oh1 = c(B, E8)
        se_oh2 = c(B, E8)
        se_t = c(B, E8)
        se_m = c(8, B)
        se_pick = c(B, 2)
        se_picki = sb("se_picki", [P, B * 2], I32)
        se_cw = c(B, 2)
        se_cwb = c(B, 2)
        se_bias = c(2, D)
        se_t4 = c(DK, B)
        se_keep = c(NT, D)
        se_cwc = c(2)

        ld_const, ld_x, ld_hy, ld_ctx, ld_bias = (sem(n) for n in ("ld_const", "ld_x", "ld_hy", "ld_ctx", "ld_bias"))
        S = {}

        def sems(stage, names):
            for n in names.split():
                S[stage, n] = sem(f"{stage}_{n}")

        sems("hy", "time phi filt filtcopy proj projcopy gate2 gate2copy dft odd dve dvex inv gated1 sd gated2 outmm added step")
        sems("ln", "stat aggr sqrt rstd norm turn feat")
        ln_done = lambda n: NT * (n + 1)
        for n in (1, 4):
            sems(f"at{n}", "w wout wused q qcopy k kcopy v vcopy s max exp turn pt ov inv o oturn ot y add ones bias")
        sems("mo", "wg w0 w1 rl step exp score st stcopy b2mm base h relu y add scol")
        sems("fl", "w step q sig k v den recip vec col con alloc clip max smx rsum comp turn kcopy vcopy kv kvm out gated outmm bias added")
        sems("se", "small w0 w1 step mean rl exp pick cwmm cwc h gelu y bias add gamma beta")
        store = sem("store")

        block = ctx.enter_context(nc.Block())


        def sync_hyena(sp):
            sp.dma_start(x_feat[:, :, :], I["x_feat"]).then_inc(ld_x, 16)
            sp.dma_start(hy_win, I["hy_win"]).then_inc(ld_x, 16)
            sp.dma_start(hy_time, I["time"]).then_inc(ld_hy, 16)
            for dst, name in ((hy_w1, "f_w1"), (hy_b1, "f_b1")):
                sp.dma_start(dst[0:HID, :], I[name]).then_inc(ld_hy, 16)
            sp.dma_start(hy_w2[0:HID + 1], I["f_w2b"]).then_inc(ld_hy, 16)
            sp.dma_start(hy_fwd, I["dft_fwd"]).then_inc(ld_const, 16)
            sp.dma_start(hy_inv, I["dft_inv"]).then_inc(ld_const, 16)
            sp.dma_start(x_tok[:, :, :], I["x_tok"]).then_inc(ld_const, 16)
            sp.dma_start(hy_wout, I["hy_wout"]).then_inc(ld_const, 16)
            sp.dma_start(ident[:, :], I["ident"]).then_inc(ld_const, 16)
            sp.dma_start(head_mask[:, :], I["head_mask"]).then_inc(ld_const, 16)
            sp.dma_start(rank8[:, :], I["rank8"]).then_inc(ld_const, 16)
            sp.dma_start(bias_row[:, :, :], I["bias_row"]).then_inc(ld_bias, 16)
            sp.dma_start(gb_row[:, :, :], I["gb_row"]).then_inc(ld_bias, 16)
            sp.wait_ge(S["hy", "gated1"], 8)
            sp.dma_start(ctx_feat, I["ctx_feat"]).then_inc(ld_ctx, 16)

        ALL_CONST = 7 * 16

        def sync_attention(sp, n, w, wout, pairs, freed):
            s = lambda k: S[f"at{n}", k]
            freed(sp)
            sp.dma_start(at_w, w[0]).then_inc(s("w"), 16)
            sp.dma_start(at_wout[:, 0:pairs, :], wout).then_inc(s("wout"), 16)
            with sp.Fori(1, pairs) as i:
                sp.wait_ge(s("wused"), i)
                sp.dma_start(at_w, w[i]).then_inc(s("w"), 16)

        def norm_group(v, g, c0, r0, added=lambda v, t: None):
            s = lambda k: S["ln", k]
            tiles = range(4 * g, 4 * g + 4)
            for t in tiles:
                added(v, t)
                v.bn_stats(ln_stat[:, t, :], x_tok[:, t, :]).then_inc(s("stat"), 1)
            for t in tiles:
                v.wait_ge(s("stat"), c0 + t % 4 + 1)
                v.bn_aggr(ln_mv[:, t, :], ln_stat[:, t, :]).then_inc(s("aggr"), 1)
            v.wait_ge(s("sqrt"), r0 + 1)
            v.reciprocal(ln_rstd[:, 4 * g:4 * g + 4], ln_std[:, 4 * g:4 * g + 4]).then_inc(s("rstd"), 1)
            v.wait_ge(s("rstd"), r0 + 1)
            for t in tiles:
                v.tensor_scalar(x_tok[:, t, :], x_tok[:, t, :], ln_mv[:, t, 0:1], ln_rstd[:, t:t + 1],
                                ALU.subtract, ALU.mult).then_inc(s("norm"), 1)

        def norm_vector(v, n, added=lambda v, t: None):
            for g in range(NT // 4):
                norm_group(v, g, NT * n + 4 * g, 4 * n + g, added)

        def norm_tensor(pe, n, g):
            s = lambda k: S["ln", k]
            c0 = NT * n
            for t in range(4 * g, 4 * g + 4):
                pe.wait_ge(s("norm"), c0 + t + 1)
                if t >= 2:
                    pe.wait_ge(s("feat"), c0 + t - 1)
                for k in range(DK):
                    mm = pe.transpose(psum[:, 6 + t % 2, k * P:(k + 1) * P], x_tok[:, t, k * P:(k + 1) * P], ident[:, :])
                mm.then_inc(s("turn"), 1)

        def norm_scalar(a, n):
            s = lambda k: S["ln", k]
            c0 = NT * n

            def root(g):
                a.wait_ge(s("aggr"), c0 + 4 * g + 4)
                a.activation(ln_std[:, 4 * g:4 * g + 4], ln_mv[:, 4 * g:4 * g + 4, 1], ACT.Sqrt,
                             bias=eps_col[:, 0:1]).then_inc(s("sqrt"), 1)

            root(0)
            for g in range(NT // 4):
                if g < 3:
                    root(g + 1)
                for t in range(4 * g, 4 * g + 4):
                    a.wait_ge(s("turn"), c0 + t + 1)
                    a.activation(x_feat[:, :, t * P:(t + 1) * P],
                                 psum[:, 6 + t % 2, 0:D].rearrange("p (k c) -> p k c", k=DK), ACT.Copy).then_inc(s("feat"), 1)

        def hyena_tensor(pe):
            s = lambda k: S["hy", k]
            pe.wait_ge(ld_hy, 64)
            pe.wait_ge(s("phi"), 3)
            for ej in range(4):
                for o in range(2):
                    mm = pe.matmul(psum[:, ej, o * D:(o + 1) * D], hy_phi[0:HID + 1, o, ej * P:(ej + 1) * P],
                                   hy_w2[0:HID + 1, o, :], start=True, stop=True)
                mm.then_inc(s("filt"), 1)
            pe.wait_ge(ld_x, 32)
            for t in range(NT):
                if t >= 4:
                    pe.wait_ge(s("projcopy"), t - 3)
                for k in range(DK):
                    mm = pe.matmul(psum[:, 4 + t % 4, :], x_feat[:, k, t * P:(t + 1) * P], hy_win[:, k, 0:512],
                                   start=k == 0, stop=k == DK - 1)
                mm.then_inc(s("proj"), 1)
            for j in range(8):
                m, b = j // 4, j % 4
                pe.wait_ge(s("filtcopy"), 4)
                if j >= 4:
                    pe.wait_ge(s("gate2copy"), j - 3)
                for k in range(DK):
                    mm = pe.matmul(psum[:, j % 4, :], hy_win[:, k, 512 + m * P:512 + (m + 1) * P],
                                   x_feat[:, k, b * L:(b + 1) * L], start=k == 0, stop=k == DK - 1)
                mm.then_inc(s("gate2"), 1)
            pe.wait_ge(ld_const, ALL_CONST)
            pe.wait_ge(s("gate2copy"), 8)
            pe.wait_ge(s("projcopy"), NT)

            def forward(job, src, g):
                bank = 4 * (job % 2)
                if job >= 2:
                    pe.wait_ge(s("dvex"), job - 1)
                for e in range(2):
                    for part in range(2):
                        for j in range(2):
                            mm = pe.matmul(psum[:, bank + 2 * e + part, :], hy_fwd[:, 2 * e + j, 2 * g + part, :],
                                           src(2 * e + j), start=j == 0, stop=j == 1)
                mm.then_inc(s("dft"), 1)

            for g in range(2):
                forward(g, lambda ej: hy_h[:, ej, :], g)
            job = 2
            for o in range(2):
                for half in range(2):
                    for g in range(2):
                        if o == 1:
                            pe.wait_ge(s("gated1"), 4 if half + g == 0 else 8)
                        forward(job, lambda ej: hy_v[:, ej, 2 * half:2 * half + 2, :], g)
                        job += 1
                if o == 0:
                    for half in range(2):
                        pe.wait_ge(s("sd"), 2 * half + 2)
                        if half == 0:
                            pe.wait_ge(s("dvex"), job)
                        for ej in range(4):
                            n = 4 * half + ej
                            e, j = ej // 2, ej % 2
                            if n >= 4:
                                pe.wait_ge(s("gated1"), n - 3)
                            for g in range(2):
                                for part in range(2):
                                    mm = pe.matmul(psum[:, 4 + n % 4, :], hy_inv[:, e, g, part, j * P:(j + 1) * P],
                                                   hy_sd[:, half, e, g, part, :], start=g + part == 0, stop=g + part == 2)
                            mm.then_inc(s("inv"), 1)
                else:
                    for half in range(2):
                        pe.wait_ge(s("sd"), 4 + 2 * half + 2)
                        if half == 0:
                            pe.wait_ge(s("dvex"), job)
                        for b2 in range(2):
                            for m in range(DK):
                                n = 4 * half + 2 * b2 + m
                                if n >= 4:
                                    pe.wait_ge(s("gated2"), n - 3)
                                col = b2 * D + m * P
                                for e in range(2):
                                    for g in range(2):
                                        for part in range(2):
                                            mm = pe.matmul(psum[:, n % 4, e * D:(e + 1) * D],
                                                           hy_sd[:, half, e, g, part, col:col + P],
                                                           hy_inv[:, e, g, part, :], start=g + part == 0, stop=g + part == 2)
                                mm.then_inc(s("inv"), 1)
            for g in range(4):
                for t in range(4 * g, 4 * g + 4):
                    pe.wait_ge(s("gated2"), 2 * (t // 4) + 2)
                    if t >= 2:
                        pe.wait_ge(s("added"), t - 1)
                    for k in range(DK):
                        mm = pe.matmul(psum[:, 4 + t % 2, 0:D], hy_gate2[:, k, t * P:(t + 1) * P], hy_wout[:, k, :],
                                       start=k == 0, stop=k == DK - 1)
                    mm.then_inc(s("outmm"), 1)
                if g >= 1:
                    norm_tensor(pe, 0, g - 1)
            norm_tensor(pe, 0, 3)

        def hyena_scalar(a):
            s = lambda k: S["hy", k]
            a.wait_ge(ld_hy, 64)
            for o in range(2):
                a.activation(hy_phi[0:HID, o, :], hy_time[0:HID], ACT.Identity, bias=hy_b1[0:HID, o:o + 1],
                             scale=hy_w1[0:HID, o:o + 1]).then_inc(s("time"), 1)
                a.activation(hy_sig[0:HID, o, :], hy_time[0:HID], ACT.Sigmoid, bias=hy_b1[0:HID, o:o + 1],
                             scale=hy_w1[0:HID, o:o + 1]).then_inc(s("time"), 1)
            for ej in range(4):
                a.wait_ge(s("filt"), ej + 1)
                a.activation(hy_h[:, ej, :], psum[:, ej, :], ACT.Copy).then_inc(s("filtcopy"), 1)
            for j in range(8):
                a.wait_ge(s("gate2"), j + 1)
                a.activation(hy_gate2[:, j // 4, (j % 4) * L:(j % 4 + 1) * L], psum[:, j % 4, :],
                             ACT.Copy).then_inc(s("gate2copy"), 1)
            for job in range(10):
                a.wait_ge(s("dft"), job + 1)
                if job >= 1:
                    a.wait_ge(s("dvex"), job)
                bank = 4 * (job % 2)
                a.activation(hy_odd, psum[:, bank + 2:bank + 4, :], ACT.Copy).then_inc(s("odd"), 1)
            norm_scalar(a, 0)

        def hyena_vector(v):
            s = lambda k: S["hy", k]
            steps = [0]

            def step(ins):
                steps[0] += 1
                ins.then_inc(s("step"), 1)
                v.wait_ge(s("step"), steps[0])

            v.memset(eps_col[:, :], LN_EPS)
            v.memset(ones[:, :], 1.0).then_inc(s("dve"), 1)
            v.memset(hy_phi[HID:HID + 1, :, :], 1.0).then_inc(s("phi"), 1)
            for o in range(2):
                v.wait_ge(s("time"), 2 * o + 2)
                v.tensor_tensor(hy_phi[0:HID, o, :], hy_phi[0:HID, o, :], hy_sig[0:HID, o, :], ALU.mult).then_inc(s("phi"), 1)
            for t in range(NT):
                v.wait_ge(s("proj"), t + 1)
                b, ej = t // 4, t % 4
                v.tensor_copy(hy_v[:, ej, b, :], psum[:, 4 + t % 4, 0:D])
                v.tensor_copy(hy_gate1[:, ej, b, :], psum[:, 4 + t % 4, D:2 * D]).then_inc(s("projcopy"), 1)

            def spectrum(job, dst):
                bank = 4 * (job % 2)
                v.wait_ge(s("odd"), job + 1)
                v.tensor_tensor(dst[:, 0], psum[:, bank:bank + 2, :], hy_odd, ALU.add)
                v.tensor_tensor(dst[:, 1], psum[:, bank:bank + 2, :], hy_odd, ALU.subtract).then_inc(s("dvex"), 1)
                v.wait_ge(s("dvex"), job + 1)

            for g in range(2):
                spectrum(g, hy_spec[:, g])
            job = 2
            v.wait_ge(s("dft"), 2)
            for o in range(2):
                for half in range(2):
                    for g in range(2):
                        spectrum(job, hy_x)
                        job += 1
                        xs = [hy_x[:, i].rearrange("p r (b c) -> p r b c", b=2) for i in range(2)]
                        aa = [hy_a[:, i].rearrange("p r (b c) -> p r b c", b=2) for i in range(2)]
                        bb = [hy_b[:, i].rearrange("p r (b c) -> p r b c", b=2) for i in range(2)]
                        for i in range(2):
                            hr = hy_spec[:, g, i, 0, o * D:(o + 1) * D].unsqueeze(1).broadcast_to([P, 2, D])
                            hi = hy_spec[:, g, i, 1, o * D:(o + 1) * D].unsqueeze(1).broadcast_to([P, 2, D])
                            for r in range(2):
                                v.tensor_tensor(aa[i][:, r], xs[i][:, r], hr, ALU.mult)
                                v.tensor_tensor(bb[i][:, r], xs[i][:, 1 - r], hi, ALU.mult).then_inc(s("dve"), 1)
                        n = 1 + 4 * (job - 2)
                        v.wait_ge(s("dve"), n)
                        v.tensor_tensor(hy_x[:, :, 0], hy_a[:, :, 0], hy_b[:, :, 0], ALU.subtract)
                        step(v.tensor_tensor(hy_x[:, :, 1], hy_a[:, :, 1], hy_b[:, :, 1], ALU.add))
                        if o == 1:
                            v.wait_ge(s("inv"), 8)
                        v.tensor_tensor(hy_sd[:, half, 0, g], hy_x[:, 0], hy_x[:, 1], ALU.add)
                        v.tensor_tensor(hy_sd[:, half, 1, g], hy_x[:, 0], hy_x[:, 1], ALU.subtract).then_inc(s("sd"), 1)
                        v.wait_ge(s("sd"), job - 2)
                for n in range(8):
                    v.wait_ge(s("inv"), 8 * o + n + 1)
                    if o == 0:
                        half, ej = n // 4, n % 4
                        v.tensor_tensor(hy_v[:, ej, 2 * half:2 * half + 2, :],
                                        psum[:, 4 + n % 4, :].rearrange("p (b c) -> p b c", b=2),
                                        hy_gate1[:, ej, 2 * half:2 * half + 2, :], ALU.mult).then_inc(s("gated1"), 1)
                    else:
                        b, m = n // 2, n % 2
                        z = hy_gate2[:, m, b * L:(b + 1) * L]
                        v.tensor_tensor(z, psum[:, n % 4, :], z, ALU.mult).then_inc(s("gated2"), 1)
            v.wait_ge(ld_const, ALL_CONST)

            def added(v, t):
                if t % 4:
                    return
                for u in range(t, t + 4):
                    v.wait_ge(s("outmm"), u + 1)
                    v.tensor_tensor(x_tok[:, u, :], psum[:, 4 + u % 2, 0:D], x_tok[:, u, :],
                                    ALU.add).then_inc(s("added"), 1)
                v.wait_ge(s("added"), t + 4)

            norm_vector(v, 0, added)

        def attention_tensor(pe, n, pairs):
            s = lambda k: S[f"at{n}", k]
            pe.wait_ge(S["ln", "feat"], ln_done(n - 1))
            pe.wait_ge(ld_ctx, 16)
            pe.wait_ge(s("ones"), 5)
            pe.wait_ge(s("wout"), 16)
            with pe.Fori(0, pairs) as i:
                pe.wait_ge(s("w"), 16 * i + 16)
                for b in range(B):
                    if b >= 2:
                        pe.wait_ge(s("qcopy"), B * i + b - 1)
                    for k in range(DK):
                        mm = pe.matmul(psum[:, b % 2, :], at_w[:, k, :], x_feat[:, k, b * L:(b + 1) * L],
                                       start=k == 0, stop=k == DK - 1)
                    mm.then_inc(s("q"), 1)
                    if b >= 1:
                        pe.wait_ge(s("kcopy"), B * i + b)
                    for k in range(DK):
                        mm = pe.matmul(psum[:, 2, :], at_w[:, 2 + k, :], ctx_feat[:, k, b * L:(b + 1) * L],
                                       start=k == 0, stop=k == DK - 1)
                    mm.then_inc(s("k"), 1)
                    if b >= 1:
                        pe.wait_ge(s("vcopy"), B * i + b)
                    for kt in range(4):
                        for k in range(DK):
                            mm = pe.matmul(psum[:, 3, kt * P:(kt + 1) * P],
                                           ctx_feat[:, k, b * L + kt * P:b * L + (kt + 1) * P], at_w[:, 4 + k, :],
                                           start=k == 0, stop=k == DK - 1)
                    mm.then_inc(s("v"), 1)
                pe.wait_ge(s("v"), B * i + B)
                pe.sem_inc(s("wused"), 1)
                pe.wait_ge(s("qcopy"), B * i + B)
                pe.wait_ge(s("kcopy"), B * i + B)
                pe.wait_ge(s("vcopy"), B * i + B)
                for step in range(32 + 6):
                    m = step
                    if m < 32:
                        b, qt, h = m // 8, m // 2 % 4, m % 2
                        if m >= 2:
                            pe.wait_ge(s("exp"), 32 * i + m - 1)
                        pe.matmul(psum[:, m % 2, :], at_q[:, h, b, qt * P:(qt + 1) * P], at_k[:, b, :],
                                  start=True, stop=True).then_inc(s("s"), 1)
                    m = step - 2
                    if 0 <= m < 32:
                        pe.wait_ge(s("exp"), 32 * i + m + 1)
                        if m >= 2:
                            pe.wait_ge(s("pt"), 32 * i + m - 1)
                        for kt in range(4):
                            mm = pe.transpose(psum[:, 2 + m % 2, kt * P:(kt + 1) * P], at_p[:, m % 2, kt * P:(kt + 1) * P],
                                              ident[:, :])
                        mm.then_inc(s("turn"), 1)
                    m = step - 3
                    if 0 <= m < 32:
                        b = m // 8
                        pe.wait_ge(s("pt"), 32 * i + m + 1)
                        if m >= 2:
                            pe.wait_ge(s("o"), 32 * i + m - 1)
                        for kt in range(4):
                            mm = pe.matmul(psum[:, 4 + m % 2, 0:130], at_pt[:, m % 2, kt * P:(kt + 1) * P],
                                           at_v[:, b, kt, :], start=kt == 0, stop=kt == 3)
                        mm.then_inc(s("ov"), 1)
                    m = step - 4
                    if 0 <= m < 32 and m % 2:
                        q = m // 2
                        pe.wait_ge(s("o"), 32 * i + m + 1)
                        if q >= 1:
                            pe.wait_ge(s("ot"), 16 * i + q)
                        pe.transpose(psum[:, 6, 0:P], at_o[:, q % 2, :], ident[:, :]).then_inc(s("oturn"), 1)
                    m = step - 5
                    if 0 <= m < 32 and m % 2:
                        q = m // 2
                        pe.wait_ge(s("ot"), 16 * i + q + 1)
                        if q >= 1:
                            pe.wait_ge(s("add"), 16 * i + q)
                        pe.matmul(psum[:, 7, 0:D], at_ot[:, q % 2, :], at_wout[:, bass.ds(i, 1), :],
                                  start=True, stop=True).then_inc(s("y"), 1)
                pe.wait_ge(s("add"), 16 * i + 16)
            for g in range(4):
                norm_tensor(pe, n, g)

        def attention_scalar(a, n, pairs):
            s = lambda k: S[f"at{n}", k]
            with a.Fori(0, pairs) as i:
                for b in range(B):
                    a.wait_ge(s("k"), B * i + b + 1)
                    a.activation(at_k[:, b, :], psum[:, 2, :], ACT.Copy).then_inc(s("kcopy"), 1)
                    a.wait_ge(s("v"), B * i + b + 1)
                    if b == 0:
                        a.wait_ge(s("ones"), 5)
                    a.activation(at_v[:, b].rearrange("p t (h d) -> p t h d", h=2)[:, :, :, 0:DH],
                                 psum[:, 3, :].rearrange("p (t h d) -> p t h d", t=4, h=2), ACT.Copy).then_inc(s("vcopy"), 1)
                for step in range(32 + 5):
                    m = step
                    if m < 32:
                        a.wait_ge(s("max"), 32 * i + m + 1)
                        if m >= 2:
                            a.wait_ge(s("turn"), 32 * i + m - 1)
                        a.activation(at_p[:, m % 2, :], psum[:, m % 2, :], ACT.Exp,
                                     bias=at_negmax[:, m % 2:m % 2 + 1]).then_inc(s("exp"), 1)
                    m = step - 1
                    if 0 <= m < 32:
                        a.wait_ge(s("turn"), 32 * i + m + 1)
                        if m >= 2:
                            a.wait_ge(s("ov"), 32 * i + m - 1)
                        a.activation(at_pt[:, m % 2, :], psum[:, 2 + m % 2, :], ACT.Copy).then_inc(s("pt"), 1)
                    m = step - 4
                    if 0 <= m < 32 and m % 2:
                        q = m // 2
                        a.wait_ge(s("oturn"), 16 * i + q + 1)
                        if q >= 2:
                            a.wait_ge(s("y"), 16 * i + q - 1)
                        a.activation(at_ot[:, q % 2, :], psum[:, 6, 0:P], ACT.Copy).then_inc(s("ot"), 1)
            norm_scalar(a, n)

        def attention_vector(v, n, pairs):
            s = lambda k: S[f"at{n}", k]
            v.wait_ge(S["ln", "feat"], ln_done(n - 1))
            v.memset(at_q[DH:P, 0, :, :], 0.0).then_inc(s("ones"), 1)
            v.memset(at_q[0:DH, 1, :, :], 0.0).then_inc(s("ones"), 1)
            v.memset(at_v[:, :, :, DH:DH + 1], 1.0).then_inc(s("ones"), 1)
            v.memset(at_v[:, :, :, 2 * DH + 1:2 * DH + 2], 1.0).then_inc(s("ones"), 1)
            v.wait_ge(ld_bias, 32)
            v.tensor_tensor(x_tok[:, :, :], x_tok[:, :, :],
                            bias_row[:, 0 if n == 1 else 2, :].unsqueeze(1).broadcast_to([P, NT, D]),
                            ALU.add).then_inc(s("ones"), 1)
            v.wait_ge(s("ones"), 5)
            with v.Fori(0, pairs) as i:
                for b in range(B):
                    v.wait_ge(s("q"), B * i + b + 1)
                    v.tensor_scalar(at_q[0:DH, 0, b, :], psum[0:DH, b % 2, :], DH ** -0.5, None, ALU.mult)
                    v.tensor_scalar(at_q[DH:P, 1, b, :], psum[DH:P, b % 2, :], DH ** -0.5, None, ALU.mult).then_inc(s("qcopy"), 1)
                for step in range(32 + 6):
                    m = step
                    if m < 32:
                        v.wait_ge(s("s"), 32 * i + m + 1)
                        if m >= 2:
                            v.wait_ge(s("exp"), 32 * i + m - 1)
                        v.tensor_reduce(at_negmax[:, m % 2:m % 2 + 1], psum[:, m % 2, :], AX.X, ALU.max,
                                        negate=True).then_inc(s("max"), 1)
                    m = step - 3
                    if 0 <= m < 32:
                        q, h = m // 2, m % 2
                        v.wait_ge(s("ov"), 32 * i + m + 1)
                        if m >= 4:
                            v.wait_ge(s("oturn"), 16 * i + q - 1)
                        c0 = h * (DH + 1)
                        v.reciprocal(at_inv[:, m % 2:m % 2 + 1],
                                     psum[:, 4 + m % 2, c0 + DH:c0 + DH + 1]).then_inc(s("inv"), 1)
                        v.wait_ge(s("inv"), 32 * i + m + 1)
                        v.tensor_scalar(at_o[:, q % 2, h * DH:(h + 1) * DH], psum[:, 4 + m % 2, c0:c0 + DH],
                                        at_inv[:, m % 2:m % 2 + 1], None, ALU.mult).then_inc(s("o"), 1)
                    m = step - 5
                    if 0 <= m < 32 and m % 2:
                        q = m // 2
                        v.wait_ge(s("y"), 16 * i + q + 1)
                        t = q // 4 * 4 + q % 4
                        v.tensor_tensor(x_tok[:, t, :], psum[:, 7, 0:D], x_tok[:, t, :], ALU.add).then_inc(s("add"), 1)
                v.wait_ge(s("add"), 16 * i + 16)
            norm_vector(v, n)

        def top2_vector(v, stage, rows, G, logit, z, e, pr, oh1, oh2, t, m):
            n = [0]

            def step(ins):
                n[0] += 1
                ins.then_inc(S[stage, "step"], 1)
                v.wait_ge(S[stage, "step"], n[0])

            r = lambda x: x[rows]
            over = lambda x: x[rows].unsqueeze(2).broadcast_to([x[rows].shape[0], G, E8])
            rank = rank8[rows].unsqueeze(1).broadcast_to([rank8[rows].shape[0], G, E8])
            m = [m[:, i, :] for i in range(m.shape[1])]
            step(v.tensor_reduce(r(m[0]), r(logit), AX.X, ALU.max))
            step(v.tensor_tensor(r(z), r(logit), over(m[0]), ALU.subtract))
            v.wait_ge(S[stage, "exp"], 1)
            step(v.tensor_reduce(r(m[1]), r(e), AX.X, ALU.add))
            step(v.reciprocal(r(m[2]), r(m[1])))
            step(v.tensor_tensor(r(pr), r(e), over(m[2]), ALU.mult))
            for k, oh in enumerate((oh1, oh2)):
                step(v.tensor_reduce(r(m[k]), r(pr), AX.X, ALU.max))
                step(v.tensor_tensor(r(t), r(pr), over(m[k]), ALU.is_equal))
                step(v.tensor_tensor(r(t), r(t), rank, ALU.mult))
                step(v.tensor_reduce(r(m[2 + k]), r(t), AX.X, ALU.max))
                step(v.tensor_tensor(r(oh), rank, over(m[2 + k]), ALU.is_equal))
                if k == 0:
                    step(v.scalar_tensor_tensor(r(pr), r(oh), -2.0, r(pr), ALU.mult, ALU.add))
            return step

        def tokens_sync(sp):
            s = lambda k: S["mo", k]
            sp.dma_start(mo_wg, I["mo_wg"]).then_inc(s("wg"), 16)
            sp.dma_start(mo_b2, I["mo_b2"]).then_inc(s("wg"), 16)
            for slot in range(2):
                sp.dma_start(mo_w1[:, slot], I["mo_w1"][slot]).then_inc(s(f"w{slot}"), 16)
                sp.dma_start(mo_w2[:, slot], I["mo_w2"][slot]).then_inc(s(f"w{slot}"), 16)
            with sp.Fori(1, E8 // 2) as i:
                for slot in range(2):
                    sp.wait_ge(s("y"), 32 * i + 16 * (slot - 1))
                    sp.dma_start(mo_w1[:, slot], I["mo_w1"][2 * i + slot]).then_inc(s(f"w{slot}"), 16)
                    sp.dma_start(mo_w2[:, slot], I["mo_w2"][2 * i + slot]).then_inc(s(f"w{slot}"), 16)

        def tokens_tensor(pe):
            s = lambda k: S["mo", k]
            pe.wait_ge(S["ln", "feat"], ln_done(1))
            pe.wait_ge(s("wg"), 32)
            for t in range(NT):
                for k in range(DK):
                    mm = pe.matmul(psum[:, 0, t * E8:(t + 1) * E8], x_feat[:, k, t * P:(t + 1) * P], mo_wg[:, k, :],
                                   start=k == 0, stop=k == DK - 1)
            mm.then_inc(s("rl"), 1)
            pe.wait_ge(s("score"), 2)
            for t in range(NT):
                mm = pe.transpose(psum[:, 1 + t // 4, t % 4 * P:(t % 4 + 1) * P], mo_score[:, t, :], ident[:, :])
                if t % 4 == 3:
                    mm.then_inc(s("st"), 1)
            for t in range(NT):
                pe.wait_ge(s("stcopy"), t // 4 + 1)
                if t >= 2:
                    pe.wait_ge(s("base"), t - 1)
                pe.matmul(psum[:, 6 + t % 2, 0:D], mo_st[:, t * P:(t + 1) * P], mo_b2, start=True, stop=True).then_inc(s("b2mm"), 1)
            pe.wait_ge(s("stcopy"), 4)
            pe.wait_ge(s("base"), NT)
            with pe.Fori(0, E8 // 2) as i:
                for step in range(9):
                    if step < 8:
                        slot, ch = step // 4, step % 4
                        if ch == 0:
                            pe.wait_ge(s(f"w{slot}"), 32 * i + 32)
                        for ht in range(4):
                            if step >= 1:
                                pe.wait_ge(s("relu"), 32 * i + 4 * step + ht - 3)
                            for k in range(DK):
                                mm = pe.matmul(psum[:, ht, :], mo_w1[:, slot, k * FF0 + ht * P:k * FF0 + (ht + 1) * P],
                                               x_feat[:, k, ch * L:(ch + 1) * L], start=k == 0, stop=k == DK - 1)
                            mm.then_inc(s("h"), 1)
                    if step >= 1:
                        m = step - 1
                        pe.wait_ge(s("relu"), 32 * i + 4 * m + 4)
                        for tt in range(4):
                            if m >= 1:
                                pe.wait_ge(s("add"), 32 * i + 4 * m + tt - 3)
                            for ht in range(4):
                                mm = pe.matmul(psum[:, 4 + tt, 0:D], mo_h[:, m % 2, ht, tt * P:(tt + 1) * P],
                                               mo_w2[:, m // 4, ht, :], start=ht == 0, stop=ht == 3)
                            mm.then_inc(s("y"), 1)
                pe.wait_ge(s("add"), 32 * i + 32)
            for g in range(4):
                norm_tensor(pe, 2, g)

        def tokens_scalar(a):
            s = lambda k: S["mo", k]
            a.wait_ge(s("step"), 2)
            a.activation(mo_e, mo_z, ACT.Exp).then_inc(s("exp"), 1)
            for q in range(4):
                a.wait_ge(s("st"), q + 1)
                a.activation(mo_st[:, q * 512:(q + 1) * 512], psum[:, 1 + q, :], ACT.Copy).then_inc(s("stcopy"), 1)
            with a.Fori(0, E8 // 2) as i:
                for step in range(8):
                    for ht in range(4):
                        a.wait_ge(s("h"), 32 * i + 4 * step + ht + 1)
                        if step >= 2:
                            a.wait_ge(s("y"), 32 * i + 4 * step - 4)
                        b1 = mo_w1[:, step // 4, DK * FF0 + ht:DK * FF0 + ht + 1]
                        a.activation(mo_h[:, step % 2, ht, :], psum[:, ht, :], ACT.Relu, bias=b1).then_inc(s("relu"), 1)
                a.wait_ge(s("y"), 32 * i + 32)
            norm_scalar(a, 2)

        def tokens_vector(v):
            s = lambda k: S["mo", k]
            v.memset(mo_score, 0.0).then_inc(s("score"), 1)
            v.wait_ge(s("rl"), 1)
            v.tensor_copy(mo_logit, psum[:, 0, 0:NT * E8].rearrange("p (t e) -> p t e", e=E8)).then_inc(s("scol"), 1)
            v.wait_ge(s("scol"), 1)
            step = top2_vector(v, "mo", slice(0, P), NT, mo_logit, mo_z, mo_e, mo_pr, mo_oh1, mo_oh2, mo_t, mo_m)
            over = lambda x: x.unsqueeze(2).broadcast_to([P, NT, E8])
            step(v.tensor_tensor(mo_m[:, 4, :], mo_m[:, 0, :], mo_m[:, 1, :], ALU.add))
            step(v.reciprocal(mo_m[:, 5, :], mo_m[:, 4, :]))
            step(v.tensor_tensor(mo_oh1, mo_oh1, over(mo_m[:, 0, :]), ALU.mult))
            step(v.tensor_tensor(mo_oh2, mo_oh2, over(mo_m[:, 1, :]), ALU.mult))
            step(v.tensor_tensor(mo_t, mo_oh1, mo_oh2, ALU.add))
            v.wait_ge(s("score"), 1)
            v.tensor_tensor(mo_score[:, :, 0:E8], mo_t, over(mo_m[:, 5, :]), ALU.mult).then_inc(s("score"), 1)
            for t in range(NT):
                v.wait_ge(s("b2mm"), t + 1)
                v.tensor_tensor(x_tok[:, t, :], psum[:, 6 + t % 2, 0:D], x_tok[:, t, :], ALU.add).then_inc(s("base"), 1)
            v.wait_ge(s("base"), NT)
            v.wait_ge(s("score"), 2)
            with v.Fori(0, E8 // 2) as i:
                for slot in range(2):
                    v.tensor_copy(mo_scol[:, slot, :], mo_score[:, :, bass.ds(2 * i + slot, 1)].rearrange("p t e -> p (t e)")
                                  ).then_inc(s("scol"), 1)
                v.wait_ge(s("scol"), 2 * i + 3)
                for step in range(8):
                    for tt in range(4):
                        t = 4 * (step % 4) + tt
                        v.wait_ge(s("y"), 32 * i + 4 * step + tt + 1)
                        if step >= 4:
                            v.wait_ge(s("add"), 32 * i + 4 * step + tt - 15)
                        v.scalar_tensor_tensor(x_tok[:, t, :], psum[:, 4 + tt, 0:D], mo_scol[:, step // 4, t:t + 1],
                                               x_tok[:, t, :], ALU.mult, ALU.add).then_inc(s("add"), 1)
                v.wait_ge(s("add"), 32 * i + 32)
            norm_vector(v, 2)

        COMBOS = [(m, b) for m in range(DK) for b in range(B)]

        def flow_sync(sp):
            s = lambda k: S["fl", k]
            sp.wait_ge(S["ln", "feat"], ln_done(2))
            sp.dma_start(fl_w, I["fl_w"]).then_inc(s("w"), 16)
            sp.dma_start(fl_bias, I["fl_bias"]).then_inc(s("w"), 16)

        def flow_tensor(pe):
            s = lambda k: S["fl", k]
            pe.wait_ge(s("w"), 32)
            for j, (m, b) in enumerate(COMBOS):
                for n, name in enumerate(("q", "k", "v")):
                    if j >= 2:
                        pe.wait_ge(s("sig"), 3 * (j - 2) + n + 1)
                    for k in range(DK):
                        mm = pe.matmul(psum[:, 2 * n + j % 2, :], fl_w[:, n, k, m * P:(m + 1) * P],
                                       x_feat[:, k, b * L:(b + 1) * L], start=k == 0, stop=k == DK - 1)
                    mm.then_inc(s(name), 1)
            pe.wait_ge(s("sig"), 24)
            for j, (m, b) in enumerate(COMBOS):
                pe.wait_ge(s("vec"), 2 * j + 2)
                if j >= 2:
                    pe.wait_ge(s("recip"), 2 * j - 2)
                cols = slice(b * L, (b + 1) * L)
                pe.matmul(psum[:, j % 2, :], fl_mask[:, j, 0, :], fl_qe[:, m, cols], start=True, stop=True).then_inc(s("den"), 1)
                pe.matmul(psum[:, 2 + j % 2, :], fl_mask[:, j, 1, :], fl_ke[:, m, cols], start=True, stop=True).then_inc(s("den"), 1)
            for j, (m, b) in enumerate(COMBOS):
                pe.wait_ge(s("col"), j + 1)
                if j >= 2:
                    pe.wait_ge(s("alloc"), j - 1)
                    pe.wait_ge(s("clip"), j - 1)
                cols = slice(b * L, (b + 1) * L)
                pe.matmul(psum[:, 4 + j % 2, :], fl_mask[:, j, 2, :], fl_qe[:, m, cols], start=True, stop=True).then_inc(s("con"), 1)
                pe.matmul(psum[:, 6 + j % 2, :], fl_mask[:, j, 3, :], fl_ke[:, m, cols], start=True, stop=True).then_inc(s("con"), 1)
            pe.wait_ge(s("recip"), 16)
            for j in range(9):
                if j < 8:
                    m, b = COMBOS[j]
                    pe.wait_ge(s("comp"), j + 1)
                    if j >= 1:
                        pe.wait_ge(s("kcopy"), j)
                        pe.wait_ge(s("vcopy"), j)
                    for n, src in enumerate((fl_k, fl_v)):
                        for tt in range(4):
                            mm = pe.transpose(psum[:, n, tt * P:(tt + 1) * P],
                                              src[:, m, b * L + tt * P:b * L + (tt + 1) * P], ident[:, :])
                        mm.then_inc(s("turn"), 1)
                if j >= 1:
                    i = j - 1
                    m, b = COMBOS[i]
                    pe.wait_ge(s("kcopy"), i + 1)
                    pe.wait_ge(s("vcopy"), i + 1)
                    if i >= 1:
                        pe.wait_ge(s("kvm"), i)
                    for tt in range(4):
                        mm = pe.matmul(psum[:, 2, 0:P], fl_ktok[:, i % 2, tt * P:(tt + 1) * P],
                                       fl_vtok[:, i % 2, tt * P:(tt + 1) * P], start=tt == 0, stop=tt == 3)
                    mm.then_inc(s("kv"), 1)
                    pe.wait_ge(s("kvm"), i + 1)
                    if i >= 1:
                        pe.wait_ge(s("gated"), i)
                    pe.matmul(psum[:, 3, :], fl_kv[:, i % 2, :], fl_q[:, m, b * L:(b + 1) * L],
                              start=True, stop=True).then_inc(s("out"), 1)
            pe.wait_ge(s("gated"), 8)
            for g in range(4):
                for t in range(4 * g, 4 * g + 4):
                    if t >= 2:
                        pe.wait_ge(s("added"), t - 1)
                    for k in range(DK):
                        mm = pe.matmul(psum[:, 4 + t % 2, 0:D], fl_v[:, k, t * P:(t + 1) * P], fl_w[:, 3, k, :],
                                       start=k == 0, stop=k == DK - 1)
                    mm.then_inc(s("outmm"), 1)
                if g >= 1:
                    norm_tensor(pe, 3, g - 1)
            norm_tensor(pe, 3, 3)

        def flow_scalar(a):
            s = lambda k: S["fl", k]
            a.wait_ge(s("w"), 32)
            for j, (m, b) in enumerate(COMBOS):
                cols = slice(b * L, (b + 1) * L)
                a.wait_ge(s("q"), j + 1)
                a.activation(fl_q[:, m, cols], psum[:, j % 2, :], ACT.Sigmoid, bias=fl_bias[:, 0, m:m + 1],
                             accum_out=fl_sum[:, j, 1:2]).then_inc(s("sig"), 1)
                a.wait_ge(s("k"), j + 1)
                a.activation(fl_k[:, m, cols], psum[:, 2 + j % 2, :], ACT.Sigmoid, bias=fl_bias[:, 1, m:m + 1],
                             accum_out=fl_sum[:, j, 0:1]).then_inc(s("sig"), 1)
                a.wait_ge(s("v"), j + 1)
                a.activation(fl_v[:, m, cols], psum[:, 4 + j % 2, :], ACT.Identity,
                             bias=fl_bias[:, 2, m:m + 1]).then_inc(s("sig"), 1)
            for j, (m, b) in enumerate(COMBOS):
                cols = slice(b * L, (b + 1) * L)
                a.wait_ge(s("con"), 2 * j + 1)
                a.activation(fl_alloc[:, m, cols], psum[:, 4 + j % 2, :], ACT.Sigmoid).then_inc(s("alloc"), 1)
            for j, (m, b) in enumerate(COMBOS):
                cols = slice(b * L, (b + 1) * L)
                a.wait_ge(s("max"), j + 1)
                a.activation(fl_ke[:, m, cols], fl_ke[:, m, cols], ACT.Exp, bias=fl_col[:, j, 0:1],
                             accum_out=fl_col[:, j, 1:2]).then_inc(s("smx"), 1)
            for j in range(8):
                a.wait_ge(s("turn"), 2 * j + 1)
                if j >= 2:
                    a.wait_ge(s("kv"), j - 1)
                a.activation(fl_ktok[:, j % 2, :], psum[:, 0, :], ACT.Copy).then_inc(s("kcopy"), 1)
            norm_scalar(a, 3)

        def flow_vector(v):
            s = lambda k: S["fl", k]
            v.wait_ge(S["ln", "turn"], ln_done(2))
            v.tensor_tensor(x_tok[:, :, :], x_tok[:, :, :], bias_row[:, 1, :].unsqueeze(1).broadcast_to([P, NT, D]),
                            ALU.add).then_inc(s("bias"), 1)
            for j, (m, b) in enumerate(COMBOS):
                cols = slice(b * L, (b + 1) * L)
                v.wait_ge(s("sig"), 3 * j + 3)
                v.tensor_scalar(fl_sume[:, j, 0:2], fl_sum[:, j, 0:2], FLOW_EPS, None, ALU.add).then_inc(s("step"), 1)
                v.tensor_scalar(fl_qe[:, m, cols], fl_q[:, m, cols], FLOW_EPS, None, ALU.add)
                v.tensor_scalar(fl_ke[:, m, cols], fl_k[:, m, cols], FLOW_EPS, None, ALU.add)
                v.wait_ge(s("step"), j + 1)
                for n in range(2):
                    v.tensor_scalar(fl_mask[:, j, n, :], head_mask[:, :], fl_sume[:, j, n:n + 1], None,
                                    ALU.mult).then_inc(s("vec"), 1)
            for j, (m, b) in enumerate(COMBOS):
                cols = slice(b * L, (b + 1) * L)
                v.wait_ge(s("den"), 2 * j + 1)
                v.reciprocal(fl_tmp[:, 0, :], psum[:, j % 2, :]).then_inc(s("recip"), 1)
                v.wait_ge(s("den"), 2 * j + 2)
                v.reciprocal(fl_tmp[:, 1, :], psum[:, 2 + j % 2, :]).then_inc(s("recip"), 1)
                v.wait_ge(s("recip"), 2 * j + 2)
                v.tensor_tensor_reduce(fl_q[:, m, cols], fl_q[:, m, cols], fl_tmp[:, 0, :], 1.0, 0.0, ALU.mult, ALU.add,
                                       fl_sum[:, j, 3:4]).then_inc(s("step"), 1)
                v.tensor_tensor_reduce(fl_clip[:, j % 2, :], fl_k[:, m, cols], fl_tmp[:, 1, :], 1.0, 0.0, ALU.mult, ALU.add,
                                       fl_sum[:, j, 2:3]).then_inc(s("step"), 1)
                v.wait_ge(s("step"), 8 + 3 * j + 2)
                v.tensor_scalar(fl_sume[:, j, 2:4], fl_sum[:, j, 2:4], FLOW_EPS, None, ALU.add).then_inc(s("step"), 1)
                v.wait_ge(s("step"), 8 + 3 * j + 3)
                v.tensor_scalar(fl_mask[:, j, 2, :], head_mask[:, :], fl_sume[:, j, 2:3], None, ALU.mult)
                v.tensor_scalar(fl_mask[:, j, 3, :], head_mask[:, :], fl_sume[:, j, 3:4], None, ALU.mult).then_inc(s("col"), 1)
            for j, (m, b) in enumerate(COMBOS):
                cols = slice(b * L, (b + 1) * L)
                v.wait_ge(s("con"), 2 * j + 2)
                v.tensor_scalar(fl_ke[:, m, cols], psum[:, 6 + j % 2, :], 1.0, -1.0, ALU.min, ALU.max).then_inc(s("clip"), 1)
                v.wait_ge(s("clip"), j + 1)
                v.tensor_reduce(fl_col[:, j, 0:1], fl_ke[:, m, cols], AX.X, ALU.max, negate=True).then_inc(s("max"), 1)
            for j, (m, b) in enumerate(COMBOS):
                cols = slice(b * L, (b + 1) * L)
                v.wait_ge(s("smx"), j + 1)
                v.reciprocal(fl_col[:, j, 2:3], fl_col[:, j, 1:2]).then_inc(s("rsum"), 1)
                v.wait_ge(s("rsum"), 2 * j + 1)
                v.tensor_scalar(fl_col[:, j, 3:4], fl_col[:, j, 2:3], float(L), None, ALU.mult).then_inc(s("rsum"), 1)
                v.wait_ge(s("rsum"), 2 * j + 2)
                v.scalar_tensor_tensor(fl_v[:, m, cols], fl_ke[:, m, cols], fl_col[:, j, 3:4], fl_v[:, m, cols],
                                       ALU.mult, ALU.mult).then_inc(s("comp"), 1)
            for j in range(9):
                if j < 8:
                    v.wait_ge(s("turn"), 2 * j + 2)
                    if j >= 2:
                        v.wait_ge(s("kv"), j - 1)
                    v.tensor_copy(fl_vtok[:, j % 2, :], psum[:, 1, :]).then_inc(s("vcopy"), 1)
                if j >= 1:
                    i = j - 1
                    m, b = COMBOS[i]
                    cols = slice(b * L, (b + 1) * L)
                    v.wait_ge(s("kv"), i + 1)
                    if i >= 2:
                        v.wait_ge(s("out"), i - 1)
                    v.tensor_tensor(fl_kv[:, i % 2, :], psum[:, 2, 0:P], head_mask[:, :], ALU.mult).then_inc(s("kvm"), 1)
                    v.wait_ge(s("out"), i + 1)
                    v.wait_ge(s("alloc"), i + 1)
                    v.tensor_tensor(fl_v[:, m, cols], psum[:, 3, :], fl_alloc[:, m, cols], ALU.mult).then_inc(s("gated"), 1)
            v.wait_ge(s("bias"), 1)

            def added(v, t):
                if t % 4:
                    return
                for u in range(t, t + 4):
                    v.wait_ge(s("outmm"), u + 1)
                    v.tensor_tensor(x_tok[:, u, :], psum[:, 4 + u % 2, 0:D], x_tok[:, u, :], ALU.add).then_inc(s("added"), 1)
                v.wait_ge(s("added"), t + 4)

            norm_vector(v, 3, added)

        def sequence_sync(sp):
            s = lambda k: S["se", k]
            sp.wait_ge(S["ln", "feat"], ln_done(3))
            sp.dma_start(se_wr, I["se_wr"]).then_inc(s("small"), 16)
            sp.dma_start(se_br, I["se_br"]).then_inc(s("small"), 16)
            sp.wait_ge(s("pick"), 1)

            def load(b, slot):
                e = sp.value_load(se_picki[0:1, bass.ds(2 * b + slot, 1)], min_val=0, max_val=E8 - 1)
                sp.dma_start(se_w1[:, slot], I["se_w1"][bass.ds(e, 1)].rearrange("o p n -> (o p) n")).then_inc(s(f"w{slot}"), 16)
                sp.dma_start(se_w2[:, slot], I["se_w2"][bass.ds(e, 1)].rearrange("o p n -> (o p) n")).then_inc(s(f"w{slot}"), 16)

            for slot in range(2):
                load(0, slot)
            with sp.Fori(1, B) as b:
                sp.wait_ge(s("bias"), 2 * b)
                for slot in range(2):
                    sp.wait_ge(s("y"), 8 * b - 4 + 4 * slot)
                    load(b, slot)

        def sequence_tensor(pe):
            s = lambda k: S["se", k]
            pe.wait_ge(S["ln", "feat"], ln_done(4))
            pe.wait_ge(s("small"), 32)
            pe.wait_ge(s("mean"), 2)
            for b in range(B):
                for k in range(DK):
                    mm = pe.matmul(psum[0:1, 0, b * E8:(b + 1) * E8], se_mean[:, k, b:b + 1], se_wr[:, k, :],
                                   start=k == 0, stop=k == DK - 1)
            mm.then_inc(s("rl"), 1)
            pe.wait_ge(s("pick"), 2)
            pe.matmul(psum[:, 1, 0:2 * B], ones[0:1, :], se_cw[0:1].rearrange("p b s -> p (b s)"),
                      start=True, stop=True).then_inc(s("cwmm"), 1)
            pe.wait_ge(s("bias"), 1)
            with pe.Fori(0, B) as b:
                for step in range(3):
                    if step < 2:
                        pe.wait_ge(s(f"w{step}"), 32 * b + 32)
                        for ft in range(8):
                            if step + ft // 4 >= 1:
                                pe.wait_ge(s("gelu"), 16 * b + 8 * step + ft - 3)
                            for k in range(DK):
                                mm = pe.matmul(psum[:, ft % 4, :], se_w1[:, step, k * FF1 + ft * P:k * FF1 + (ft + 1) * P],
                                               x_feat[:, k, bass.ds(b * L, L)], start=k == 0, stop=k == DK - 1)
                            mm.then_inc(s("h"), 1)
                    if step >= 1:
                        m = step - 1
                        pe.wait_ge(s("gelu"), 16 * b + 8 * m + 8)
                        for tt in range(4):
                            if m >= 1:
                                pe.wait_ge(s("add"), 12 * b + 4 + tt + 1)
                            for ft in range(8):
                                mm = pe.matmul(psum[:, 4 + tt, 0:D], se_h[:, m, ft, tt * P:(tt + 1) * P],
                                               se_w2[:, m, ft * D:(ft + 1) * D], start=ft == 0, stop=ft == 7)
                            mm.then_inc(s("y"), 1)
                pe.wait_ge(s("add"), 12 * b + 12)

        def sequence_scalar(a):
            s = lambda k: S["se", k]
            a.wait_ge(s("step"), 2)
            a.activation(se_e[0:1], se_z[0:1], ACT.Exp).then_inc(s("exp"), 1)
            a.wait_ge(s("pick"), 1)
            a.activation(se_m[0:1, 5, :], se_m[0:1, 4, :], ACT.Exp).then_inc(s("exp"), 1)
            with a.Fori(0, B) as b:
                for m in range(2):
                    for ft in range(8):
                        a.wait_ge(s("h"), 16 * b + 8 * m + ft + 1)
                        b1 = se_w1[:, m, DK * FF1 + ft:DK * FF1 + ft + 1]
                        a.activation(se_h[:, m, ft, :], psum[:, ft % 4, :], ACT.Gelu, bias=b1).then_inc(s("gelu"), 1)
                a.wait_ge(s("y"), 8 * b + 8)

            for g in range(4):
                for n in (5, 6):
                    a.wait_ge(S["ln", "aggr"], NT * 5 + 8 * g + 4 * (n - 4))
                    a.activation(ln_std[:, 4 * g:4 * g + 4], ln_mv[:, 4 * g:4 * g + 4, 1], ACT.Sqrt,
                                 bias=eps_col[:, 0:1]).then_inc(S["ln", "sqrt"], 1)

        def sequence_vector(v):
            s = lambda k: S["se", k]
            v.wait_ge(S["ln", "feat"], ln_done(4))
            v.tensor_reduce(se_t4, x_feat[:, :, :].rearrange("p k (b l) -> p k b l", b=B), AX.X, ALU.add).then_inc(s("mean"), 1)
            v.wait_ge(s("mean"), 1)
            v.tensor_scalar(se_mean, se_t4, 1.0 / L, None, ALU.mult).then_inc(s("mean"), 1)
            v.wait_ge(s("rl"), 1)
            one = slice(0, 1)
            v.tensor_tensor(se_logit[one], psum[0:1, 0, 0:B * E8].rearrange("p (b e) -> p b e", e=E8),
                            se_br[one].unsqueeze(1).broadcast_to([1, B, E8]), ALU.add).then_inc(s("mean"), 1)
            v.wait_ge(s("mean"), 3)
            v.tensor_tensor(se_keep, x_tok[:, :, :], gb_row[:, 1, :].unsqueeze(1).broadcast_to([P, NT, D]),
                            ALU.add).then_inc(s("mean"), 1)
            step = top2_vector(v, "se", one, B, se_logit, se_z, se_e, se_pr, se_oh1, se_oh2, se_t, se_m)
            step(v.tensor_scalar(se_pick[one, :, 0], se_m[one, 2, :], -1.0, float(E8), ALU.mult, ALU.add))
            step(v.tensor_scalar(se_pick[one, :, 1], se_m[one, 3, :], -1.0, float(E8), ALU.mult, ALU.add))
            step(v.tensor_tensor(se_m[one, 4, :], se_m[one, 1, :], se_m[one, 0, :], ALU.subtract))
            v.tensor_copy(se_picki[0:1, :], se_pick[one].rearrange("p b s -> p (b s)")).then_inc(s("pick"), 1)
            v.wait_ge(s("exp"), 2)
            step(v.tensor_scalar(se_m[one, 6, :], se_m[one, 5, :], 1.0, None, ALU.add))
            step(v.reciprocal(se_cw[one, :, 0], se_m[one, 6, :]))
            v.tensor_tensor(se_cw[one, :, 1], se_cw[one, :, 0], se_m[one, 5, :], ALU.mult).then_inc(s("pick"), 1)
            v.wait_ge(s("cwmm"), 1)
            v.tensor_copy(se_cwb, psum[:, 1, 0:2 * B].rearrange("p (b s) -> p b s", s=2)).then_inc(s("bias"), 1)
            v.wait_ge(s("bias"), 1)
            with v.Fori(0, B) as b:
                v.wait_ge(s("w0"), 32 * b + 32)
                v.wait_ge(s("w1"), 32 * b + 32)
                v.tensor_copy(se_cwc, se_cwb[:, bass.ds(b, 1), :].rearrange("p o s -> p (o s)")).then_inc(s("cwc"), 1)
                v.wait_ge(s("cwc"), 3 * b + 1)
                v.tensor_scalar(se_bias[:, 0, :], se_w2[:, 0, 8 * D:9 * D], se_cwc[:, 0:1], None, ALU.mult).then_inc(s("cwc"), 1)
                v.wait_ge(s("cwc"), 3 * b + 2)
                v.scalar_tensor_tensor(se_bias[:, 1, :], se_w2[:, 1, 8 * D:9 * D], se_cwc[:, 1:2], se_bias[:, 0, :],
                                       ALU.mult, ALU.add).then_inc(s("cwc"), 1)
                v.wait_ge(s("cwc"), 3 * b + 3)
                v.sem_inc(s("bias"), 2)
                xb = lambda tt: x_tok[:, bass.ds(4 * b + tt, 1), :].rearrange("p o d -> p (o d)")
                v.wait_ge(s("mean"), 4)
                for tt in range(4):
                    v.tensor_tensor(xb(tt), xb(tt), se_bias[:, 1, :], ALU.add).then_inc(s("add"), 1)
                for m in range(2):
                    for tt in range(4):
                        v.wait_ge(s("y"), 8 * b + 4 * m + tt + 1)
                        v.wait_ge(s("add"), 12 * b + 4 * m + tt + 1)
                        v.scalar_tensor_tensor(xb(tt), psum[:, 4 + tt, 0:D], se_cwc[:, m:m + 1], xb(tt),
                                               ALU.mult, ALU.add).then_inc(s("add"), 1)
                v.wait_ge(s("add"), 12 * b + 12)
            for g in range(4):
                norm_group(v, g, NT * 5 + 8 * g, 4 * 5 + 2 * g)
                for t in range(4 * g, 4 * g + 4):
                    v.wait_ge(S["ln", "norm"], NT * 5 + 8 * g + t % 4 + 1)
                    v.tensor_tensor(x_tok[:, t, :], x_tok[:, t, :], gb_row[:, 0, :], ALU.mult).then_inc(s("gamma"), 1)
                for t in range(4 * g, 4 * g + 4):
                    v.wait_ge(s("gamma"), t + 1)
                    v.tensor_tensor(x_tok[:, t, :], x_tok[:, t, :], se_keep[:, t, :], ALU.add).then_inc(s("beta"), 1)
                v.wait_ge(s("beta"), 4 * g + 4)
                norm_group(v, g, NT * 5 + 8 * g + 4, 4 * 5 + 2 * g + 1)

        stop = STOP

        @block.sync
        def _(sp):
            sync_hyena(sp)
            if stop >= 1:
                sync_attention(sp, 1, I["at1_w"], I["at1_wout"], 8, lambda sp: sp.wait_ge(S["ln", "feat"], ln_done(0)))
            if stop >= 2:
                tokens_sync(sp)
            if stop >= 3:
                flow_sync(sp)
            if stop >= 4:
                sync_attention(sp, 4, I["at4_w"], I["at4_wout"], 2, lambda sp: sp.wait_ge(S["ln", "feat"], ln_done(3)))
            if stop >= 5:
                sequence_sync(sp)
            for b in range(B):
                if stop == 5:
                    sp.wait_ge(S["ln", "norm"], NT * 5 + 8 * b + 8)
                else:
                    sp.wait_ge(S["ln", "norm"], NT * stop + 4 * b + 4)
                for e in range(2):
                    sp.dma_start(out[b].rearrange("(j p e) d -> e p j d", j=2, e=2)[e],
                                 x_tok[:, 4 * b + 2 * e:4 * b + 2 * e + 2, :]).then_inc(store, 16)
            sp.wait_ge(store, 16 * 2 * B)

        @block.tensor
        def _(pe):
            hyena_tensor(pe)
            if stop >= 1:
                attention_tensor(pe, 1, 8)
            if stop >= 2:
                tokens_tensor(pe)
            if stop >= 3:
                flow_tensor(pe)
            if stop >= 4:
                attention_tensor(pe, 4, 2)
            if stop >= 5:
                sequence_tensor(pe)

        @block.scalar
        def _(a):
            hyena_scalar(a)
            if stop >= 1:
                attention_scalar(a, 1, 8)
            if stop >= 2:
                tokens_scalar(a)
            if stop >= 3:
                flow_scalar(a)
            if stop >= 4:
                attention_scalar(a, 4, 2)
            if stop >= 5:
                sequence_scalar(a)

        @block.vector
        def _(v):
            hyena_vector(v)
            if stop >= 1:
                attention_vector(v, 1, 8)
            if stop >= 2:
                tokens_vector(v)
            if stop >= 3:
                flow_vector(v)
            if stop >= 4:
                attention_vector(v, 4, 2)
            if stop >= 5:
                sequence_vector(v)


STOP = 5


def _transforms():
    f = np.arange(256)
    t = np.arange(512)
    ang = 2 * np.pi * (((2 * f[:, None] + 1) * t[None, :]) % 2048) / 2048.0
    cos, sin = np.cos(ang), np.sin(ang)
    fwd = np.zeros((P, 4, 4, P), np.float32)
    inv = np.zeros((P, 2, 2, 2, 256), np.float32)
    for e in range(2):
        for j in range(2):
            tt = 2 * (128 * j + np.arange(P)) + e
            for g in range(2):
                fwd[:, 2 * e + j, 2 * g, :] = cos[g * P:(g + 1) * P, tt].T
                fwd[:, 2 * e + j, 2 * g + 1, :] = -sin[g * P:(g + 1) * P, tt].T
        tt = 2 * np.arange(256) + e
        for g in range(2):
            inv[:, e, g, 0, :] = cos[g * P:(g + 1) * P, tt] / 512.0
            inv[:, e, g, 1, :] = -sin[g * P:(g + 1) * P, tt] / 512.0
    return fwd, inv


def _rows(w, pad=None):
    w = np.asarray(w)
    if pad and w.shape[0] < pad:
        w = np.concatenate([w, np.zeros((pad - w.shape[0],) + w.shape[1:], w.dtype)])
    return np.ascontiguousarray(w.reshape(-1, P, *w.shape[1:]).swapaxes(0, 1))


def _attention(wq, wk, wv, wout):
    pairs = wq.shape[1] // P
    w = np.zeros((pairs, P, 6, P), np.float32)
    for n, m in enumerate((wq, wk, wv)):
        r = _rows(m, 256)
        w[:, :, 2 * n:2 * n + 2, :] = r.reshape(P, 2, pairs, P).transpose(2, 0, 1, 3)
    return w, _rows(wout)


def _experts(w1, b1, w2):
    e, _, f = w1.shape
    one = w1.reshape(e, DK, P, f).transpose(0, 2, 1, 3).reshape(e, P, DK * f)
    bias = b1.reshape(e, f // P, P).transpose(0, 2, 1)
    two = w2.reshape(e, f // P, P, D).transpose(0, 2, 1, 3)
    return np.ascontiguousarray(np.concatenate([one, bias], 2)), np.ascontiguousarray(two)


def layouts(x, ctx_768, **W):
    a = {}
    order = np.concatenate([np.arange(0, L, 2), np.arange(1, L, 2)])
    xo = np.asarray(x)[:, order, :].reshape(T, D)
    a["x_tok"] = np.ascontiguousarray(xo.reshape(NT, P, D).transpose(1, 0, 2))
    a["x_feat"] = _rows(xo.T)
    a["ctx_feat"] = _rows(np.asarray(ctx_768).reshape(T, DC).T, 256)
    a["hy_win"] = _rows(W["L0_attn_W_in"].T)
    a["hy_wout"] = _rows(W["L0_attn_W_out"].T)
    time = np.linspace(0.0, 1.0, L, dtype=np.float32)[order]
    a["time"] = np.ascontiguousarray(np.broadcast_to(time, (P, L)))
    a["f_w1"] = np.ascontiguousarray(W["L0_attn_f_w1"][:, :, 0].T)
    a["f_b1"] = np.ascontiguousarray(W["L0_attn_f_b1"].T)
    a["f_w2b"] = np.ascontiguousarray(np.concatenate(
        [W["L0_attn_f_w2"].transpose(2, 0, 1), W["L0_attn_f_b2"][None]]))
    a["dft_fwd"], a["dft_inv"] = _transforms()
    a["ident"] = np.eye(P, dtype=np.float32)
    a["head_mask"] = np.kron(np.eye(8), np.ones((16, 16))).astype(np.float32)
    a["rank8"] = np.ascontiguousarray(np.broadcast_to(8 - np.arange(8, dtype=np.float32), (P, 8)))
    a["bias_row"] = np.ascontiguousarray(np.broadcast_to(np.stack(
        [W["L0_xattn_b_out"], W["L1_attn_bo"], W["L1_xattn_bo"]]), (P, 3, D)))
    a["gb_row"] = np.ascontiguousarray(np.broadcast_to(np.stack(
        [W["L1_ffn_gamma"], W["L1_ffn_beta"]]), (P, 2, D)))
    kv = W["L0_xattn_w_kv"]
    a["at1_w"], a["at1_wout"] = _attention(W["L0_xattn_w_q"], kv[:, :1024], kv[:, 1024:], W["L0_xattn_w_out"])
    a["at4_w"], a["at4_wout"] = _attention(W["L1_xattn_Wq"].T, W["L1_xattn_Wk"].T, W["L1_xattn_Wv"].T,
                                           W["L1_xattn_Wo"].T)
    a["mo_wg"] = _rows(W["L0_ffn_Wg"])
    a["mo_b2"] = np.ascontiguousarray(np.concatenate([W["L0_ffn_b2"], np.zeros((P - E8, D), np.float32)]))
    a["mo_w1"], a["mo_w2"] = _experts(W["L0_ffn_W1"], W["L0_ffn_b1"], W["L0_ffn_W2"])
    a["fl_w"] = np.ascontiguousarray(np.stack([_rows(W[f"L1_attn_W{n}"].T) for n in "qkvo"], 1))
    a["fl_bias"] = np.ascontiguousarray(np.stack([W[f"L1_attn_b{n}"].reshape(DK, P).T for n in "qkv"], 1))
    a["se_wr"] = _rows(W["L1_ffn_Wr"])
    a["se_br"] = np.ascontiguousarray(np.broadcast_to(W["L1_ffn_br"], (P, E8)))
    a["se_w1"], w2 = _experts(W["L1_ffn_W1"], W["L1_ffn_b1"], W["L1_ffn_W2"])
    a["se_w2"] = np.ascontiguousarray(np.concatenate(
        [w2.reshape(E8, P, -1), np.broadcast_to(W["L1_ffn_b2"][:, None, :], (E8, P, D))], 2))
    return a


def program(nc, arrays):
    I = {n: nc.dram_tensor("in_" + n, a.shape, mybir.dt.from_np(a.dtype), kind="ExternalInput").ap() for n, a in arrays.items()}
    out = nc.dram_tensor("out", (B, L, D), F32, kind="ExternalOutput").ap()
    build(nc, I, out)


def kernel(**inputs):
    import concourse.bacc as _bacc
    from concourse.bass_utils import run_bass_kernel_spmd as _run

    nc = _bacc.Bacc("TRN2", target_bir_lowering=False, num_devices=1)
    arrays = layouts(**{k: np.asarray(v) for k, v in inputs.items()})
    program(nc, arrays)
    r = _run(nc, [{"in_" + k: v for k, v in arrays.items()}], core_ids=[0])
    return r.results[0]["out"]
```

```python
from contextlib import ExitStack

import numpy as np

import concourse.bass as bass
from concourse import mybir

F32 = mybir.dt.float32
F32R = mybir.dt.float32r
I32 = mybir.dt.int32
ALU = mybir.AluOpType
ACT = mybir.ActivationFunctionType
AX = mybir.AxisListType

P = 128
B, L, D = 4, 512, 256
T = B * L
NT = T // P
DK = D // P
DC = 192
E8 = 8
HID = 64
DH = 64
FF0, FF1 = 512, 1024
SLOT_TILES = 2 * T // P + E8
LN_EPS = 1e-5
FLOW_EPS = 1e-6


def build(nc, I, out):
    with ExitStack() as ctx:
        def sb(name, shape, dt=F32):
            return ctx.enter_context(nc.sbuf_tensor(name, shape, dt))

        def sem(name):
            return ctx.enter_context(nc.semaphore(name))

        x_tok = sb("x_tok", [P, NT, D])
        x_feat = sb("x_feat", [P, DK, T])
        ident = sb("ident", [P, P])
        head_mask = sb("head_mask", [P, P])
        rank8 = sb("rank8", [P, E8])
        bias_row = sb("bias_row", [P, 3, D])
        gb_row = sb("gb_row", [P, 2, D])
        ones = sb("ones", [P, P])
        ln_stat = sb("ln_stat", [P, NT, 6])
        ln_mv = sb("ln_mv", [P, NT, 2])
        ln_std = sb("ln_std", [P, NT])
        ln_rstd = sb("ln_rstd", [P, NT])
        eps_col = sb("eps_col", [P, 1])
        at_negmax = sb("at_negmax", [P, 2])
        se_wr = sb("se_wr", [P, DK, E8])
        se_br = sb("se_br", [P, E8])
        REGION, SHARED, SPLIT = 42720, 24288, 18432
        base = -(-nc.sbuf_base // 64) * 64
        sb("region", [P, REGION + 16])

        def place(name, at, shape, dt=F32):
            return nc.alloc_sbuf_tensor_at(name, shape, dt, offset=base + 4 * at)

        hyena_mem = place("hyena_mem", 0, [P, 38144])
        shared_mem = place("shared_mem", 0, [P, SHARED])
        late_mem = place("late_mem", SHARED, [P, SPLIT])
        tail_mem = place("tail_mem", 4096, [P, REGION - 4096])
        psum = ctx.enter_context(nc.psum_tensor("psum", [P, 8, 512], F32))

        class Carve:
            def __init__(self, mem, at=0):
                self.mem, self.at = mem, at

            def __call__(self, *dims):
                n = int(np.prod(dims))
                a = self.mem[:, self.at:self.at + n]
                self.at += n
                assert self.at <= self.mem.shape[1], self.at
                if len(dims) > 1:
                    names = "abcdef"[:len(dims)]
                    a = a.rearrange(f"p ({' '.join(names)}) -> p {' '.join(names)}",
                                    **{k: v for k, v in zip(names, dims)})
                return a

        c = Carve(hyena_mem)
        hy_gate1 = c(4, B, D)
        hy_v = c(4, B, D)
        hy_gate2 = c(DK, T)
        hy_x = c(2, 2, 512)
        hy_a = c(2, 2, 512)
        hy_b = c(2, 2, 512)
        hy_odd = c(2, 512)
        hy_sd = c(2, 2, 2, 2, 512)
        hy_spec = c(2, 2, 2, 512)
        hy_fwd = c(4, 4, P)
        hy_inv = c(2, 2, 2, D)
        hy_win = c(DK, 3 * D)
        hy_wout = c(DK, D)
        hy_end = c.at
        c = Carve(hyena_mem, 3 * 4096 + 3 * 2048 + 1024)
        hy_time = c(L)
        hy_phi = c(2, L)
        hy_sig = c(2, L)
        hy_w1 = c(2)
        hy_b1 = c(2)
        hy_w2 = c(2, D)
        hy_h = c(4, 2 * D)

        ctx_feat = Carve(shared_mem)(DK, T)
        c = Carve(shared_mem, 4096)
        at_wout = c(8, D)
        at_w = c(6, P)
        at_p = c(4, L)
        at_ot = c(2, L)
        at_oc = c(L)
        at_sum = c(16)
        at_rinv = c(16)
        at_end = c.at
        spl = [SHARED]

        def split_mem(name, *dims):
            n = int(np.prod(dims))
            t = place(name, spl[0], [P, *dims], F32R)
            spl[0] += n
            assert spl[0] <= REGION
            return t

        at_qn = split_mem("at_qn", 2, L)
        at_kn = split_mem("at_kn", 2, L)
        at_qd = split_mem("at_qd", 2, 2, L)
        at_kd = split_mem("at_kd", 2, 2, 2, L)
        at_vd = split_mem("at_vd", 2, 4, 4, DH)
        at_ph = split_mem("at_ph", 2, 4, L)
        at_pl = split_mem("at_pl", 2, 4, L)

        c = Carve(shared_mem, at_end)
        mo_w1 = c(E8, DK * FF0)
        mo_b1 = c(E8, FF0)
        mo_wg = c(DK, E8)
        mo_lt8 = c(E8, E8)
        mo_step128 = c(16)
        mo_iota = c(SLOT_TILES)
        c = Carve(late_mem)
        mo_w2 = c(E8, 4 * D)
        mo_b2 = c(E8, D)
        mo_x = c(2, D)
        mo_xt = c(2, D)
        mo_h = c(2, FF0)
        mo_ht = c(2, FF0)
        mo_y = c(2, D)
        mo_yg = c(2, 4, D)
        zero_row = Carve(hyena_mem, 38144 - D)(D)
        c = Carve(shared_mem, 4096)
        mo_before = c(P)
        mo_logit = c(NT, E8)
        mo_z = c(NT, E8)
        mo_e = c(NT, E8)
        mo_pr = c(NT, E8)
        mo_oh1 = c(NT, E8)
        mo_oh2 = c(NT, E8)
        mo_t = c(NT, E8)
        mo_both_pad = c(2 * NT, E8)
        mo_both = mo_both_pad[:, NT:2 * NT, :]
        mo_pos = c(NT, E8)
        mo_m = c(6, NT)
        mo_s = c(2, NT)
        mo_mine = c(E8)
        mo_cmp = c(E8, 16)
        mo_tiles = c(E8)
        mo_ltt = c(E8, E8)
        mo_base = c(E8)
        mo_end8 = c(E8)
        mo_base128 = c(E8)
        mo_geq = c(SLOT_TILES, E8)
        mo_te = c(SLOT_TILES)
        mo_posf = c(2, NT)
        assert c.at <= at_end
        mo_tei = sb("mo_tei", [P, SLOT_TILES], I32)
        mo_posi = sb("mo_posi", [P, 2, NT], I32)

        c = Carve(tail_mem)
        fl_w = c(4, DK, D)
        fl_bias = c(3, DK)
        fl_k = c(DK, T)
        fl_q = c(DK, T)
        fl_v = c(DK, T)
        fl_ke = c(DK, T)
        fl_qe = c(DK, T)
        fl_alloc = c(DK, T)
        fl_mask = c(8, 4, P)
        fl_sum = c(8, 4)
        fl_sume = c(8, 4)
        fl_tmp = c(2, 512)
        fl_clip = c(2, 512)
        fl_col = c(8, 4)
        fl_ktok = c(2, 512)
        fl_vtok = c(2, 512)
        fl_kv = c(2, P)
        c = Carve(tail_mem)
        se_h = c(2, 8, 512)
        se_w1 = c(2, DK * FF1 + 8)
        se_w2 = c(2, 8 * D + D)
        se_mean = c(DK, B)
        se_logit = c(B, E8)
        se_z = c(B, E8)
        se_e = c(B, E8)
        se_pr = c(B, E8)
        se_oh1 = c(B, E8)
        se_oh2 = c(B, E8)
        se_t = c(B, E8)
        se_m = c(8, B)
        se_pick = c(B, 2)
        se_picki = sb("se_picki", [P, B * 2], I32)
        se_cw = c(B, 2)
        se_cwb = c(B, 2)
        se_bias = c(2, D)
        se_t4 = c(DK, B)
        se_keep = c(NT, D)
        se_cwc = c(2)

        ld_const, ld_x, ld_hy, ld_ctx, ld_bias = (sem(n) for n in ("ld_const", "ld_x", "ld_hy", "ld_ctx", "ld_bias"))
        S = {}

        def sems(stage, names):
            for n in names.split():
                S[stage, n] = sem(f"{stage}_{n}")

        sems("hy", "time phi filt filtcopy proj projcopy gate2 gate2copy dft odd dve dvex inv gated1 sd gated2 outmm added step")
        sems("ln", "stat aggr sqrt rstd norm turn feat")
        ln_done = lambda n: NT * (n + 1)
        for n in (1, 4):
            sems(f"at{n}", "w wout q k v qh kh vh ql kl vl qd kd s max exp rinv pn turn ph pl av oc ot y add")
        sems("mo", "zero fill w wlate rl step exp both rank place scatter x0 x1 xturn xt h hb hturn relu y y2 ys0 ys1 g0 g1 g2 g3 mix")
        sems("fl", "w step q sig k v den recip vec col con alloc clip max smx rsum comp turn kcopy vcopy kv kvm out gated outmm added")
        sems("se", "small w0 w1 step mean rl exp pick cwmm cwc h gelu y bias add gamma beta")
        biased = sem("biased")
        store = sem("store")

        block = ctx.enter_context(nc.Block())

        sorted_x = nc.dram_tensor("sorted_x", (SLOT_TILES * P, D), F32).ap()


        def sync_hyena(sp):
            sp.dma_start(x_feat[:, :, :], I["x_feat"]).then_inc(ld_x, 16)
            sp.dma_start(hy_win, I["hy_win"]).then_inc(ld_x, 16)
            sp.dma_start(hy_time, I["time"]).then_inc(ld_hy, 16)
            for dst, name in ((hy_w1, "f_w1"), (hy_b1, "f_b1")):
                sp.dma_start(dst[0:HID, :], I[name]).then_inc(ld_hy, 16)
            sp.dma_start(hy_w2[0:HID + 1], I["f_w2b"]).then_inc(ld_hy, 16)
            sp.dma_start(hy_fwd, I["dft_fwd"]).then_inc(ld_const, 16)
            sp.dma_start(hy_inv, I["dft_inv"]).then_inc(ld_const, 16)
            sp.dma_start(x_tok[:, :, :], I["x_tok"]).then_inc(ld_const, 16)
            sp.dma_start(hy_wout, I["hy_wout"]).then_inc(ld_const, 16)
            sp.dma_start(ident[:, :], I["ident"]).then_inc(ld_const, 16)
            sp.dma_start(head_mask[:, :], I["head_mask"]).then_inc(ld_const, 16)
            sp.dma_start(rank8[:, :], I["rank8"]).then_inc(ld_const, 16)
            sp.dma_start(bias_row[:, :, :], I["bias_row"]).then_inc(ld_bias, 16)
            sp.dma_start(gb_row[:, :, :], I["gb_row"]).then_inc(ld_bias, 16)
            sp.wait_ge(S["mo", "zero"], 1)
            sp.dma_start(sorted_x.rearrange("(i p) d -> p i d", p=P),
                         zero_row.unsqueeze(1).broadcast_to([P, SLOT_TILES, D])).then_inc(S["mo", "fill"], 16)
            sp.wait_ge(S["hy", "gated1"], 8)
            sp.dma_start(ctx_feat, I["ctx_feat"]).then_inc(ld_ctx, 16)

        ALL_CONST = 7 * 16

        def hold(eng, sem, count):
            if not isinstance(count, int) or count > 0:
                eng.wait_ge(sem, count)

        TAIL = 17
        PARTS = {"q": 2, "k": 2, "v": 8}
        PROJECT = {0: ("k", [0]), 1: ("k", [1]), 3: ("q", [0]), 4: ("q", [1]), 6: ("v", [0, 1, 2, 3]), 7: ("v", [4, 5, 6, 7])}

        def over_pairs(eng, pairs, steps):
            steps(0, range(32), True, False)
            with eng.Fori(1, pairs) as i:
                steps(i, range(32), False, False)
            steps(pairs, range(TAIL), False, True)

        def back(s, by, first, last):
            m = s - by
            return None if (first and m < 0) or (last and m >= 0) else m

        def attention_sync(sp, n, pairs):
            s = lambda k: S[f"at{n}", k]

            def stack(u, slot):
                sp.wait_ge(s("kl"), u + 1)
                for h in range(2):
                    for half in range(2):
                        sp.dma_start(at_kd[half * DH:(half + 1) * DH, slot, h, :, :].bitcast(F32),
                                     at_kn[h * DH:(h + 1) * DH, :, :].bitcast(F32)).then_inc(s("kd"), 16)
                sp.wait_ge(s("ql"), u + 1)
                for h in range(2):
                    for part in range(2):
                        sp.dma_start(at_qd[part * DH:(part + 1) * DH, slot, h, :].bitcast(F32),
                                     at_qn[h * DH:(h + 1) * DH, part, :].bitcast(F32)).then_inc(s("qd"), 16)

            stack(0, 0)
            with sp.Fori(0, pairs) as i:
                for b in range(B):
                    stack(4 * i + (b + 1), (b + 1) % 2)
            sp.wait_ge(s("qd"), 64 * (4 * pairs + 1))
            sp.wait_ge(s("kd"), 64 * (4 * pairs + 1))

        def attention_gpsimd(gp, n, w, wout, pairs):
            s = lambda k: S[f"at{n}", k]
            gp.wait_ge(S["ln", "feat"], ln_done(n - 1))
            gp.dma_start(at_w, w[0]).then_inc(s("w"), 16)
            gp.dma_start(at_wout[:, 0:pairs, :], wout).then_inc(s("wout"), 16)

            def steps(i, span, first, last):
                for st in span:
                    m = back(st, 2, first, last)
                    if m is not None:
                        gp.wait_ge(s("rinv"), 32 * i + (m + 1))
                        gp.tensor_tensor(at_p[:, m % 4, :], at_p[:, m % 4, :], at_rinv[:, m % 16:m % 16 + 1].broadcast_to([P, L]),
                                         ALU.mult).then_inc(s("pn"), 1)
                    if not last and st == 24:
                        gp.wait_ge(s("v"), 4 * i + 4)
                        gp.dma_start(at_w, w[i + 1]).then_inc(s("w"), 16)

            over_pairs(gp, pairs, steps)

        def norm_group(v, g, c0, r0, added=lambda v, t: None):
            s = lambda k: S["ln", k]
            tiles = range(4 * g, 4 * g + 4)
            for t in tiles:
                added(v, t)
                v.bn_stats(ln_stat[:, t, :], x_tok[:, t, :]).then_inc(s("stat"), 1)
            for t in tiles:
                v.wait_ge(s("stat"), c0 + t % 4 + 1)
                v.bn_aggr(ln_mv[:, t, :], ln_stat[:, t, :]).then_inc(s("aggr"), 1)
            v.wait_ge(s("sqrt"), r0 + 1)
            v.reciprocal(ln_rstd[:, 4 * g:4 * g + 4], ln_std[:, 4 * g:4 * g + 4]).then_inc(s("rstd"), 1)
            v.wait_ge(s("rstd"), r0 + 1)
            for t in tiles:
                v.tensor_scalar(x_tok[:, t, :], x_tok[:, t, :], ln_mv[:, t, 0:1], ln_rstd[:, t:t + 1],
                                ALU.subtract, ALU.mult).then_inc(s("norm"), 1)

        def norm_vector(v, n, added=lambda v, t: None):
            for g in range(NT // 4):
                norm_group(v, g, NT * n + 4 * g, 4 * n + g, added)

        def norm_tensor(pe, n, g):
            s = lambda k: S["ln", k]
            c0 = NT * n
            for t in range(4 * g, 4 * g + 4):
                pe.wait_ge(s("norm"), c0 + t + 1)
                if t >= 2:
                    pe.wait_ge(s("feat"), c0 + t - 1)
                for k in range(DK):
                    mm = pe.transpose(psum[:, 6 + t % 2, k * P:(k + 1) * P], x_tok[:, t, k * P:(k + 1) * P], ident[:, :])
                mm.then_inc(s("turn"), 1)

        def norm_scalar(a, n):
            s = lambda k: S["ln", k]
            c0 = NT * n

            def root(g):
                a.wait_ge(s("aggr"), c0 + 4 * g + 4)
                a.activation(ln_std[:, 4 * g:4 * g + 4], ln_mv[:, 4 * g:4 * g + 4, 1], ACT.Sqrt,
                             bias=eps_col[:, 0:1]).then_inc(s("sqrt"), 1)

            root(0)
            for g in range(NT // 4):
                if g < 3:
                    root(g + 1)
                for t in range(4 * g, 4 * g + 4):
                    a.wait_ge(s("turn"), c0 + t + 1)
                    a.activation(x_feat[:, :, t * P:(t + 1) * P],
                                 psum[:, 6 + t % 2, 0:D].rearrange("p (k c) -> p k c", k=DK), ACT.Copy).then_inc(s("feat"), 1)

        def hyena_tensor(pe):
            s = lambda k: S["hy", k]
            pe.wait_ge(ld_hy, 64)
            pe.wait_ge(s("phi"), 3)
            for ej in range(4):
                for o in range(2):
                    mm = pe.matmul(psum[:, ej, o * D:(o + 1) * D], hy_phi[0:HID + 1, o, ej * P:(ej + 1) * P],
                                   hy_w2[0:HID + 1, o, :], start=True, stop=True)
                mm.then_inc(s("filt"), 1)
            pe.wait_ge(ld_x, 32)
            for t in range(NT):
                if t >= 4:
                    pe.wait_ge(s("projcopy"), t - 3)
                for k in range(DK):
                    mm = pe.matmul(psum[:, 4 + t % 4, :], x_feat[:, k, t * P:(t + 1) * P], hy_win[:, k, 0:512],
                                   start=k == 0, stop=k == DK - 1)
                mm.then_inc(s("proj"), 1)
            for j in range(8):
                m, b = j // 4, j % 4
                pe.wait_ge(s("filtcopy"), 4)
                if j >= 4:
                    pe.wait_ge(s("gate2copy"), j - 3)
                for k in range(DK):
                    mm = pe.matmul(psum[:, j % 4, :], hy_win[:, k, 512 + m * P:512 + (m + 1) * P],
                                   x_feat[:, k, b * L:(b + 1) * L], start=k == 0, stop=k == DK - 1)
                mm.then_inc(s("gate2"), 1)
            pe.wait_ge(ld_const, ALL_CONST)
            pe.wait_ge(s("gate2copy"), 8)
            pe.wait_ge(s("projcopy"), NT)

            def forward(job, src, g):
                bank = 4 * (job % 2)
                if job >= 2:
                    pe.wait_ge(s("dvex"), job - 1)
                for e in range(2):
                    for part in range(2):
                        for j in range(2):
                            mm = pe.matmul(psum[:, bank + 2 * e + part, :], hy_fwd[:, 2 * e + j, 2 * g + part, :],
                                           src(2 * e + j), start=j == 0, stop=j == 1)
                mm.then_inc(s("dft"), 1)

            for g in range(2):
                forward(g, lambda ej: hy_h[:, ej, :], g)
            job = 2
            for o in range(2):
                for half in range(2):
                    for g in range(2):
                        if o == 1:
                            pe.wait_ge(s("gated1"), 4 if half + g == 0 else 8)
                        forward(job, lambda ej: hy_v[:, ej, 2 * half:2 * half + 2, :], g)
                        job += 1
                if o == 0:
                    for half in range(2):
                        pe.wait_ge(s("sd"), 2 * half + 2)
                        if half == 0:
                            pe.wait_ge(s("dvex"), job)
                        for ej in range(4):
                            n = 4 * half + ej
                            e, j = ej // 2, ej % 2
                            if n >= 4:
                                pe.wait_ge(s("gated1"), n - 3)
                            for g in range(2):
                                for part in range(2):
                                    mm = pe.matmul(psum[:, 4 + n % 4, :], hy_inv[:, e, g, part, j * P:(j + 1) * P],
                                                   hy_sd[:, half, e, g, part, :], start=g + part == 0, stop=g + part == 2)
                            mm.then_inc(s("inv"), 1)
                else:
                    for half in range(2):
                        pe.wait_ge(s("sd"), 4 + 2 * half + 2)
                        if half == 0:
                            pe.wait_ge(s("dvex"), job)
                        for b2 in range(2):
                            for m in range(DK):
                                n = 4 * half + 2 * b2 + m
                                if n >= 4:
                                    pe.wait_ge(s("gated2"), n - 3)
                                col = b2 * D + m * P
                                for e in range(2):
                                    for g in range(2):
                                        for part in range(2):
                                            mm = pe.matmul(psum[:, n % 4, e * D:(e + 1) * D],
                                                           hy_sd[:, half, e, g, part, col:col + P],
                                                           hy_inv[:, e, g, part, :], start=g + part == 0, stop=g + part == 2)
                                mm.then_inc(s("inv"), 1)
            for g in range(4):
                for t in range(4 * g, 4 * g + 4):
                    pe.wait_ge(s("gated2"), 2 * (t // 4) + 2)
                    if t >= 2:
                        pe.wait_ge(s("added"), t - 1)
                    for k in range(DK):
                        mm = pe.matmul(psum[:, 4 + t % 2, 0:D], hy_gate2[:, k, t * P:(t + 1) * P], hy_wout[:, k, :],
                                       start=k == 0, stop=k == DK - 1)
                    mm.then_inc(s("outmm"), 1)
                if g >= 1:
                    norm_tensor(pe, 0, g - 1)
            norm_tensor(pe, 0, 3)

        def hyena_scalar(a):
            s = lambda k: S["hy", k]
            a.wait_ge(ld_hy, 64)
            for o in range(2):
                a.activation(hy_phi[0:HID, o, :], hy_time[0:HID], ACT.Identity, bias=hy_b1[0:HID, o:o + 1],
                             scale=hy_w1[0:HID, o:o + 1]).then_inc(s("time"), 1)
                a.activation(hy_sig[0:HID, o, :], hy_time[0:HID], ACT.Sigmoid, bias=hy_b1[0:HID, o:o + 1],
                             scale=hy_w1[0:HID, o:o + 1]).then_inc(s("time"), 1)
            for ej in range(4):
                a.wait_ge(s("filt"), ej + 1)
                a.activation(hy_h[:, ej, :], psum[:, ej, :], ACT.Copy).then_inc(s("filtcopy"), 1)
            for j in range(8):
                a.wait_ge(s("gate2"), j + 1)
                a.activation(hy_gate2[:, j // 4, (j % 4) * L:(j % 4 + 1) * L], psum[:, j % 4, :],
                             ACT.Copy).then_inc(s("gate2copy"), 1)
            for job in range(10):
                a.wait_ge(s("dft"), job + 1)
                if job >= 1:
                    a.wait_ge(s("dvex"), job)
                bank = 4 * (job % 2)
                a.activation(hy_odd, psum[:, bank + 2:bank + 4, :], ACT.Copy).then_inc(s("odd"), 1)
            norm_scalar(a, 0)

        def hyena_vector(v):
            s = lambda k: S["hy", k]
            steps = [0]

            def step(ins):
                steps[0] += 1
                ins.then_inc(s("step"), 1)
                v.wait_ge(s("step"), steps[0])

            v.memset(zero_row, 0.0).then_inc(S["mo", "zero"], 1)
            v.memset(eps_col[:, :], LN_EPS)
            v.memset(ones[:, :], 1.0).then_inc(s("dve"), 1)
            v.memset(hy_phi[HID:HID + 1, :, :], 1.0).then_inc(s("phi"), 1)
            for o in range(2):
                v.wait_ge(s("time"), 2 * o + 2)
                v.tensor_tensor(hy_phi[0:HID, o, :], hy_phi[0:HID, o, :], hy_sig[0:HID, o, :], ALU.mult).then_inc(s("phi"), 1)
            for t in range(NT):
                v.wait_ge(s("proj"), t + 1)
                b, ej = t // 4, t % 4
                v.tensor_copy(hy_v[:, ej, b, :], psum[:, 4 + t % 4, 0:D])
                v.tensor_copy(hy_gate1[:, ej, b, :], psum[:, 4 + t % 4, D:2 * D]).then_inc(s("projcopy"), 1)

            def spectrum(job, dst):
                bank = 4 * (job % 2)
                v.wait_ge(s("odd"), job + 1)
                v.tensor_tensor(dst[:, 0], psum[:, bank:bank + 2, :], hy_odd, ALU.add)
                v.tensor_tensor(dst[:, 1], psum[:, bank:bank + 2, :], hy_odd, ALU.subtract).then_inc(s("dvex"), 1)
                v.wait_ge(s("dvex"), job + 1)

            for g in range(2):
                spectrum(g, hy_spec[:, g])
            job = 2
            v.wait_ge(s("dft"), 2)
            for o in range(2):
                for half in range(2):
                    for g in range(2):
                        spectrum(job, hy_x)
                        job += 1
                        xs = [hy_x[:, i].rearrange("p r (b c) -> p r b c", b=2) for i in range(2)]
                        aa = [hy_a[:, i].rearrange("p r (b c) -> p r b c", b=2) for i in range(2)]
                        bb = [hy_b[:, i].rearrange("p r (b c) -> p r b c", b=2) for i in range(2)]
                        for i in range(2):
                            hr = hy_spec[:, g, i, 0, o * D:(o + 1) * D].unsqueeze(1).broadcast_to([P, 2, D])
                            hi = hy_spec[:, g, i, 1, o * D:(o + 1) * D].unsqueeze(1).broadcast_to([P, 2, D])
                            for r in range(2):
                                v.tensor_tensor(aa[i][:, r], xs[i][:, r], hr, ALU.mult)
                                v.tensor_tensor(bb[i][:, r], xs[i][:, 1 - r], hi, ALU.mult).then_inc(s("dve"), 1)
                        n = 1 + 4 * (job - 2)
                        v.wait_ge(s("dve"), n)
                        v.tensor_tensor(hy_x[:, :, 0], hy_a[:, :, 0], hy_b[:, :, 0], ALU.subtract)
                        step(v.tensor_tensor(hy_x[:, :, 1], hy_a[:, :, 1], hy_b[:, :, 1], ALU.add))
                        if o == 1:
                            v.wait_ge(s("inv"), 8)
                        v.tensor_tensor(hy_sd[:, half, 0, g], hy_x[:, 0], hy_x[:, 1], ALU.add)
                        v.tensor_tensor(hy_sd[:, half, 1, g], hy_x[:, 0], hy_x[:, 1], ALU.subtract).then_inc(s("sd"), 1)
                        v.wait_ge(s("sd"), job - 2)
                for n in range(8):
                    v.wait_ge(s("inv"), 8 * o + n + 1)
                    if o == 0:
                        half, ej = n // 4, n % 4
                        v.tensor_tensor(hy_v[:, ej, 2 * half:2 * half + 2, :],
                                        psum[:, 4 + n % 4, :].rearrange("p (b c) -> p b c", b=2),
                                        hy_gate1[:, ej, 2 * half:2 * half + 2, :], ALU.mult).then_inc(s("gated1"), 1)
                    else:
                        b, m = n // 2, n % 2
                        z = hy_gate2[:, m, b * L:(b + 1) * L]
                        v.tensor_tensor(z, psum[:, n % 4, :], z, ALU.mult).then_inc(s("gated2"), 1)
            v.wait_ge(ld_const, ALL_CONST)

            def added(v, t):
                if t % 4:
                    return
                for u in range(t, t + 4):
                    v.wait_ge(s("outmm"), u + 1)
                    v.tensor_tensor(x_tok[:, u, :], psum[:, 4 + u % 2, 0:D], x_tok[:, u, :],
                                    ALU.add).then_inc(s("added"), 1)
                v.wait_ge(s("added"), t + 4)

            norm_vector(v, 0, added)

        def attention_tensor(pe, n, pairs):
            s = lambda k: S[f"at{n}", k]

            def project(what, u, b, parts):
                cols = slice(b * L, (b + 1) * L)
                if parts[0] == 0:
                    if what == "k":
                        pe.wait_ge(s("w"), 16 * ((u + (4 - b)) // 4) if isinstance(u, int) else u * 4 + (16 - 4 * b))
                        hold(pe, s("vl"), u)
                    else:
                        pe.wait_ge(s("kl" if what == "q" else "ql"), u + 1)
                for part in parts:
                    if what == "q":
                        mm = pe.matmul(psum[:, 5, :], at_w[:, part, :], x_feat[:, part, cols], start=part == 0, stop=part == 1)
                    elif what == "k":
                        mm = pe.matmul(psum[:, 5, :], at_w[:, 2 + part, :], ctx_feat[:, part, cols],
                                       start=part == 0, stop=part == 1)
                    else:
                        kt, k = part // 2, part % 2
                        mm = pe.matmul(psum[:, 5, kt * P:(kt + 1) * P],
                                       ctx_feat[:, k, b * L + kt * P:b * L + (kt + 1) * P], at_w[:, 4 + k, :],
                                       start=k == 0, stop=k == 1)
                if parts[-1] == PARTS[what] - 1:
                    mm.then_inc(s(what), 1)

            def steps(i, span, first, last):
                for st in span:
                    m = back(st, 0, first, last)
                    if m is not None:
                        b, h, qt = m // 8, m // 4 % 2, m % 4
                        if m % 8 == 0:
                            pe.wait_ge(s("qd"), 64 * 4 * i + 64 * (b + 1))
                            pe.wait_ge(s("kd"), 64 * 4 * i + 64 * (b + 1))
                        hold(pe, s("exp"), 32 * i + (m - 1))
                        for part in range(2):
                            mm = pe.matmul(psum[:, m % 2, :], at_qd[:, b % 2, h, qt * P:(qt + 1) * P],
                                           at_kd[:, b % 2, h, part, :], start=part == 0, stop=part == 1)
                        mm.then_inc(s("s"), 1)
                    g = st // 4 - 2
                    if st % 4 < 3 and not (first and g < 0) and not (last and g >= 0):
                        h = g % 2
                        bank = 7 if h else 4
                        if st % 4 == 0:
                            pe.wait_ge(s("pl"), 32 * i + (4 * g + 4))
                            pe.wait_ge(s("vl"), 4 * i + (g // 2 + 1))
                            hold(pe, s("ot"), 8 * i + (g - 1))
                        for n8 in ((0, 1, 2), (3, 4, 5), (6, 7))[st % 4]:
                            kt, part = n8 // 2, (at_ph, at_pl)[n8 % 2]
                            mm = pe.matmul(psum[:, bank, :],
                                           at_vd[:, g // 2 % 2, kt, 2 * h:2 * h + 2, :].rearrange("p a d -> p (a d)"),
                                           part[:, h, kt, :], start=n8 == 0, stop=n8 == 7)
                        if st % 4 == 2:
                            mm.then_inc(s("av"), 1)
                    u = st // 8 - 2
                    if st % 4 == 3 and not (first and u < 0) and not (last and u >= 0):
                        half = st // 4 % 2
                        pe.wait_ge(s("ot"), 8 * i + (2 * u + 2))
                        hold(pe, s("add"), 8 * i + (2 * u + half))
                        pair = i if u >= 0 else i - 1
                        rhs = at_wout[:, pair, :] if isinstance(pair, int) else at_wout[:, bass.ds(pair, 1), :]
                        for n2 in range(2):
                            qt = 2 * half + n2
                            mm = pe.matmul(psum[:, 6, n2 * D:(n2 + 1) * D], at_ot[:, u % 2, qt * P:(qt + 1) * P], rhs,
                                           start=True, stop=True)
                        mm.then_inc(s("y"), 1)
                    if not last and st % 8 in PROJECT:
                        what, parts = PROJECT[st % 8]
                        project(what, 4 * i + (st // 8 + 1), (st // 8 + 1) % 4, parts)
                    m = back(st, 3, first, last)
                    if m is not None:
                        pe.wait_ge(s("pn"), 32 * i + (m + 1))
                        hold(pe, s("pl"), 32 * i + (m - 1))
                        for kt in range(4):
                            mm = pe.transpose(psum[:, 2 + m % 2, kt * P:(kt + 1) * P], at_p[:, m % 4, kt * P:(kt + 1) * P],
                                              ident[:, :])
                        mm.then_inc(s("turn"), 1)

            pe.wait_ge(S["ln", "feat"], ln_done(n - 1))
            pe.wait_ge(ld_ctx, 16)
            for what in "kqv":
                project(what, 0, 0, range(PARTS[what]))
            pe.wait_ge(s("wout"), 16)
            over_pairs(pe, pairs, steps)
            for g in range(4):
                norm_tensor(pe, n, g)

        def attention_scalar(a, n, pairs):
            s = lambda k: S[f"at{n}", k]

            def high(what, u, slot, used):
                a.wait_ge(s(what), u + 1)
                if what == "q":
                    hold(a, s("qd"), 64 * u)
                    a.activation(at_qn[:, 0, :], psum[:, 5, :], ACT.Copy, scale=DH ** -0.5).then_inc(s("qh"), 1)
                elif what == "k":
                    hold(a, s("kd"), 64 * u)
                    a.activation(at_kn[:, 0, :], psum[:, 5, :], ACT.Copy).then_inc(s("kh"), 1)
                else:
                    hold(a, s("av"), used)
                    a.activation(at_vd[:, slot, :, 0:4:3, :], psum[:, 5, :].rearrange("p (t h d) -> p t h d", t=4, h=2),
                                 ACT.Copy).then_inc(s("vh"), 1)

            def steps(i, span, first, last):
                for st in span:
                    m = back(st, 0, first, last)
                    if m is not None:
                        a.wait_ge(s("max"), 32 * i + (m + 1))
                        hold(a, s("turn"), 32 * i + (m - 3))
                        hold(a, s("rinv"), 32 * i + (m - 15))
                        a.activation(at_p[:, m % 4, :], psum[:, m % 2, :], ACT.Exp, bias=at_negmax[:, m % 2:m % 2 + 1],
                                     accum_out=at_sum[:, m % 16:m % 16 + 1]).then_inc(s("exp"), 1)
                    m = back(st, 3, first, last)
                    if m is not None:
                        qt = m % 4
                        a.wait_ge(s("turn"), 32 * i + (m + 1))
                        hold(a, s("av"), 8 * i + (m // 4 - 1))
                        a.activation(at_ph[:, m // 4 % 2, :, qt * P:(qt + 1) * P],
                                     psum[:, 2 + m % 2, :].rearrange("p (t q) -> p t q", t=4), ACT.Copy).then_inc(s("ph"), 1)
                    if not last and st % 8 in (1, 4, 7):
                        u = st // 8 + 1
                        high({1: "k", 4: "q", 7: "v"}[st % 8], 4 * i + u, u % 2, 8 * i + 2 * (u - 1))
                    m = back(st, 11, first, last)
                    if m is not None and m % 4 == 0:
                        g = m // 4
                        h = g % 2
                        a.wait_ge(s("av"), 8 * i + (g + 1))
                        hold(a, s("ot"), 8 * i + (g - 1))
                        a.activation(at_oc[h * DH:(h + 1) * DH, :], psum[(1 - h) * DH:(2 - h) * DH, 7 if h else 4, :],
                                     ACT.Copy).then_inc(s("oc"), 1)

            if n == 1:
                a.wait_ge(S["mo", "fill"], 16)
            for what in "kqv":
                high(what, 0, 0, 0)
            over_pairs(a, pairs, steps)
            norm_scalar(a, n)

        def attention_vector(v, n, pairs):
            s = lambda k: S[f"at{n}", k]

            def low(what, u, slot):
                v.wait_ge(s(what + "h"), u + 1)
                if what == "q":
                    v.scalar_tensor_tensor(at_qn[:, 1, :], psum[:, 5, :], DH ** -0.5, at_qn[:, 0, :],
                                           ALU.mult, ALU.subtract).then_inc(s("ql"), 1)
                elif what == "k":
                    v.tensor_tensor(at_kn[:, 1, :], psum[:, 5, :], at_kn[:, 0, :], ALU.subtract).then_inc(s("kl"), 1)
                else:
                    v.tensor_tensor(at_vd[:, slot, :, 1:3, :], psum[:, 5, :].rearrange("p (t h d) -> p t h d", t=4, h=2),
                                    at_vd[:, slot, :, 0:4:3, :], ALU.subtract).then_inc(s("vl"), 1)

            def steps(i, span, first, last):
                for st in span:
                    if not last and st % 8 == 0:
                        low("v", 4 * i + st // 8, st // 8 % 2)
                    m = back(st, 0, first, last)
                    if m is not None:
                        v.wait_ge(s("s"), 32 * i + (m + 1))
                        hold(v, s("exp"), 32 * i + (m - 1))
                        v.tensor_reduce(at_negmax[:, m % 2:m % 2 + 1], psum[:, m % 2, :], AX.X, ALU.max,
                                        negate=True).then_inc(s("max"), 1)
                    if not last and st % 8 in (2, 5):
                        low({2: "k", 5: "q"}[st % 8], 4 * i + (st // 8 + 1), 0)
                    m = back(st, 1, first, last)
                    if m is not None:
                        v.wait_ge(s("exp"), 32 * i + (m + 1))
                        c = slice(m % 16, m % 16 + 1)
                        hold(v, s("pn"), 32 * i + (m - 15))
                        v.reciprocal(at_rinv[:, c], at_sum[:, c]).then_inc(s("rinv"), 1)
                    m = back(st, 4, first, last)
                    if m is not None:
                        qt = m % 4
                        v.wait_ge(s("ph"), 32 * i + (m + 1))
                        p = (slice(None), m // 4 % 2, slice(None), slice(qt * P, (qt + 1) * P))
                        v.tensor_tensor(at_pl[p], psum[:, 2 + m % 2, :].rearrange("p (t q) -> p t q", t=4), at_ph[p],
                                        ALU.subtract).then_inc(s("pl"), 1)
                    m = back(st, 12, first, last)
                    if m is not None and m % 4 == 0:
                        g = m // 4
                        rows = slice(g % 2 * DH, (g % 2 + 1) * DH)
                        v.wait_ge(s("oc"), 8 * i + (g + 1))
                        hold(v, s("y"), 8 * i + 2 * (g // 2 - 1))
                        v.tensor_tensor(at_ot[rows, g // 2 % 2, :], psum[rows, 7 if g % 2 else 4, :], at_oc[rows, :],
                                        ALU.add).then_inc(s("ot"), 1)
                    u, half = (st // 8 - 2, 0) if st % 8 == 4 else (st // 8 - 3, 1)
                    if st % 4 == 0 and not (first and u < 0) and not (last and u >= 0):
                        v.wait_ge(s("y"), 8 * i + (2 * u + half + 1))
                        t = 4 * (u % 4) + 2 * half
                        v.tensor_tensor(x_tok[:, t:t + 2, :], psum[:, 6, :].rearrange("p (t d) -> p t d", t=2),
                                        x_tok[:, t:t + 2, :], ALU.add).then_inc(s("add"), 1)

            v.wait_ge(S["ln", "turn"], ln_done(n - 1))
            v.wait_ge(ld_bias, 32)
            v.tensor_tensor(x_tok[:, :, :], x_tok[:, :, :],
                            bias_row[:, 0 if n == 1 else 2, :].unsqueeze(1).broadcast_to([P, NT, D]),
                            ALU.add).then_inc(biased, 1)
            for what in "kq":
                low(what, 0, 0)
            v.wait_ge(biased, 1 if n == 1 else 3)
            over_pairs(v, pairs, steps)
            v.wait_ge(s("add"), 8 * pairs)
            norm_vector(v, n)

        def top2_vector(v, stage, rows, G, logit, z, e, pr, oh1, oh2, t, m):
            n = [0]

            def step(ins):
                n[0] += 1
                ins.then_inc(S[stage, "step"], 1)
                v.wait_ge(S[stage, "step"], n[0])

            r = lambda x: x[rows]
            over = lambda x: x[rows].unsqueeze(2).broadcast_to([x[rows].shape[0], G, E8])
            rank = rank8[rows].unsqueeze(1).broadcast_to([rank8[rows].shape[0], G, E8])
            m = [m[:, i, :] for i in range(m.shape[1])]
            step(v.tensor_reduce(r(m[0]), r(logit), AX.X, ALU.max))
            step(v.tensor_tensor(r(z), r(logit), over(m[0]), ALU.subtract))
            v.wait_ge(S[stage, "exp"], 1)
            step(v.tensor_reduce(r(m[1]), r(e), AX.X, ALU.add))
            step(v.reciprocal(r(m[2]), r(m[1])))
            step(v.tensor_tensor(r(pr), r(e), over(m[2]), ALU.mult))
            for k, oh in enumerate((oh1, oh2)):
                step(v.tensor_reduce(r(m[k]), r(pr), AX.X, ALU.max))
                step(v.tensor_tensor(r(t), r(pr), over(m[k]), ALU.is_equal))
                step(v.tensor_tensor(r(t), r(t), rank, ALU.mult))
                step(v.tensor_reduce(r(m[2 + k]), r(t), AX.X, ALU.max))
                step(v.tensor_tensor(r(oh), rank, over(m[2 + k]), ALU.is_equal))
                if k == 0:
                    step(v.scalar_tensor_tensor(r(pr), r(oh), -2.0, r(pr), ALU.mult, ALU.add))
            return step

        sorted_y = nc.dram_tensor("sorted_y", (SLOT_TILES * P, D), F32).ap()
        ITERS, UNROLL = 4, SLOT_TILES // 4

        def tokens_sync(sp):
            s = lambda k: S["mo", k]
            for dst, name in ((mo_wg, "mo_wg"), (mo_lt8, "mo_lt8"), (mo_step128, "mo_step128"), (mo_iota, "mo_iota"),
                              (mo_w1, "mo_w1"), (mo_b1, "mo_b1")):
                sp.dma_start(dst, I[name]).then_inc(s("w"), 16)
            sp.wait_ge(S["ln", "feat"], ln_done(1))
            for dst, name in ((mo_before, "mo_before"), (mo_b2, "mo_b2"), (mo_w2, "mo_w2")):
                sp.dma_start(dst, I[name]).then_inc(s("wlate"), 16)
            sp.wait_ge(s("scatter"), 2 * NT * 16)
            for q in range(2):
                sp.dma_start(mo_x[:, q, :], sorted_x[q * P:(q + 1) * P, :]).then_inc(s(f"x{q}"), 16)
            with sp.Fori(1, SLOT_TILES // 2) as m:
                for q in range(2):
                    sp.wait_ge(s("xturn"), 2 * m + (q - 1))
                    sp.dma_start(mo_x[:, q, :], sorted_x[bass.ds(m * (2 * P) + q * P, P), :]).then_inc(s(f"x{q}"), 16)

        def tokens_gpsimd(gp):
            s = lambda k: S["mo", k]
            gp.wait_ge(s("place"), 1)
            gp.wait_ge(s("fill"), 16)
            for t in range(NT):
                for k in range(2):
                    gp.indirect_dma_start(out=sorted_x, out_offset=bass.IndirectOffsetOnAxis(mo_posi[:, k, t:t + 1], 0),
                                          in_=x_tok[:, t, :], in_offset=None).then_inc(s("scatter"), 16)
            with gp.Fori(0, SLOT_TILES // 2) as m:
                for q in range(2):
                    gp.wait_ge(s("y2"), 2 * m + (q + 1))
                    gp.dma_start(sorted_y[bass.ds(m * (2 * P) + q * P, P), :], mo_y[:, q, :]).then_inc(s(f"ys{q}"), 16)
            for q in range(2):
                gp.wait_ge(s(f"ys{q}"), 8 * SLOT_TILES)
            for t in range(NT):
                if t >= 4:
                    gp.wait_ge(s("mix"), 2 * (t - 3))
                for k in range(2):
                    gp.indirect_dma_start(out=mo_yg[:, k, t % 4, :], out_offset=None, in_=sorted_y,
                                          in_offset=bass.IndirectOffsetOnAxis(mo_posi[:, k, t:t + 1], 0)
                                          ).then_inc(s(f"g{t % 4}"), 16)

        def tokens_tensor(pe):
            s = lambda k: S["mo", k]
            pe.wait_ge(S["ln", "feat"], ln_done(1))
            pe.wait_ge(s("w"), 6 * 16)
            for t in range(NT):
                for k in range(DK):
                    mm = pe.matmul(psum[:, 0, t * E8:(t + 1) * E8], x_feat[:, k, t * P:(t + 1) * P], mo_wg[:, k, :],
                                   start=k == 0, stop=k == DK - 1)
            mm.then_inc(s("rl"), 1)
            pe.wait_ge(s("wlate"), 3 * 16)
            pe.wait_ge(s("both"), 2)
            pad = mo_both_pad.rearrange("p t e -> p (t e)")
            pe.matmul(psum[:, 1, 0:P], mo_before, pad[:, P:2 * P], start=True, stop=False)
            for d in range(1, NT):
                mm = pe.matmul(psum[:, 1, 0:P], ones[:, :], pad[:, P - d * E8:2 * P - d * E8],
                               start=False, stop=d == NT - 1)
            mm.then_inc(s("rank"), 1)
            pe.matmul(psum[:, 2, 0:E8], ones[:, :], mo_mine, start=True, stop=True).then_inc(s("rank"), 1)
            pe.wait_ge(s("place"), 1)
            with pe.Fori(0, ITERS) as i:
                for step in range(UNROLL + 3):
                    m = step
                    if m < UNROLL:
                        pe.wait_ge(s(f"x{m % 2}"), 8 * UNROLL * i + 8 * (m - m % 2) + 16)
                        if m >= 2:
                            pe.wait_ge(s("xt"), UNROLL * i + m - 1)
                        for k in range(DK):
                            mm = pe.transpose(psum[:, m % 2, k * P:(k + 1) * P], mo_x[:, m % 2, k * P:(k + 1) * P], ident[:, :])
                        mm.then_inc(s("xturn"), 1)
                    m = step - 1
                    if 0 <= m < UNROLL:
                        e = pe.value_load(mo_tei[0:1, bass.ds(UNROLL * i + m, 1)], min_val=0, max_val=E8 - 1)
                        pe.wait_ge(s("xt"), UNROLL * i + m + 1)
                        if m >= 2:
                            pe.wait_ge(s("hb"), UNROLL * i + m - 1)
                        for k in range(DK):
                            mm = pe.matmul(psum[:, 2 + m % 2, :], mo_xt[:, m % 2, k * P:(k + 1) * P],
                                           mo_w1[:, bass.ds(e, 1), k * FF0:(k + 1) * FF0], start=k == 0, stop=k == DK - 1)
                        mm.then_inc(s("h"), 1)
                    m = step - 2
                    if 0 <= m < UNROLL:
                        pe.wait_ge(s("hb"), UNROLL * i + m + 1)
                        if m >= 2:
                            pe.wait_ge(s("relu"), UNROLL * i + m - 1)
                        for ht in range(4):
                            mm = pe.transpose(psum[:, 4 + m % 2, ht * P:(ht + 1) * P], mo_h[:, m % 2, ht * P:(ht + 1) * P],
                                              ident[:, :])
                        mm.then_inc(s("hturn"), 1)
                    m = step - 3
                    if 0 <= m < UNROLL:
                        e = pe.value_load(mo_tei[0:1, bass.ds(UNROLL * i + m, 1)], min_val=0, max_val=E8 - 1)
                        pe.wait_ge(s("relu"), UNROLL * i + m + 1)
                        if m >= 2:
                            pe.wait_ge(s("y2"), UNROLL * i + m - 1)
                        for ht in range(4):
                            mm = pe.matmul(psum[:, 6 + m % 2, 0:D], mo_ht[:, m % 2, ht * P:(ht + 1) * P],
                                           mo_w2[:, bass.ds(e, 1), ht * D:(ht + 1) * D], start=ht == 0, stop=ht == 3)
                        mm.then_inc(s("y"), 1)
                pe.wait_ge(s("y2"), UNROLL * i + UNROLL)
            for g in range(4):
                norm_tensor(pe, 2, g)

        def tokens_scalar(a):
            s = lambda k: S["mo", k]
            a.wait_ge(s("step"), 2)
            a.activation(mo_e, mo_z, ACT.Exp).then_inc(s("exp"), 1)
            with a.Fori(0, ITERS) as i:
                for step in range(UNROLL + 2):
                    m = step
                    if m < UNROLL:
                        a.wait_ge(s("xturn"), UNROLL * i + m + 1)
                        if m >= 2:
                            a.wait_ge(s("h"), UNROLL * i + m - 1)
                        a.activation(mo_xt[:, m % 2, :], psum[:, m % 2, 0:D], ACT.Copy).then_inc(s("xt"), 1)
                    m = step - 2
                    if 0 <= m < UNROLL:
                        a.wait_ge(s("hturn"), UNROLL * i + m + 1)
                        if m >= 2:
                            a.wait_ge(s("y"), UNROLL * i + m - 1)
                        a.activation(mo_ht[:, m % 2, :], psum[:, 4 + m % 2, :], ACT.Relu).then_inc(s("relu"), 1)
                a.wait_ge(s("y"), UNROLL * i + UNROLL)
            norm_scalar(a, 2)

        def tokens_vector(v):
            s = lambda k: S["mo", k]
            v.wait_ge(s("rl"), 1)
            v.memset(mo_both_pad[:, 0:NT, :], 0.0)
            v.tensor_copy(mo_logit, psum[:, 0, 0:NT * E8].rearrange("p (t e) -> p t e", e=E8)).then_inc(s("both"), 1)
            v.wait_ge(s("both"), 1)
            step = top2_vector(v, "mo", slice(0, P), NT, mo_logit, mo_z, mo_e, mo_pr, mo_oh1, mo_oh2, mo_t, mo_m)
            step(v.tensor_tensor(mo_both, mo_oh1, mo_oh2, ALU.add))
            v.tensor_reduce(mo_mine, mo_both.rearrange("p t e -> p e t"), AX.X, ALU.add).then_inc(s("both"), 1)
            step(v.tensor_tensor(mo_m[:, 4, :], mo_m[:, 0, :], mo_m[:, 1, :], ALU.add))
            step(v.reciprocal(mo_m[:, 5, :], mo_m[:, 4, :]))
            for k in range(2):
                step(v.tensor_tensor(mo_s[:, k, :], mo_m[:, k, :], mo_m[:, 5, :], ALU.mult))
            v.wait_ge(s("rank"), 2)
            step(v.tensor_tensor(mo_cmp, psum[:, 2, 0:E8].unsqueeze(2).broadcast_to([P, E8, 16]),
                                 mo_step128.unsqueeze(1).broadcast_to([P, E8, 16]), ALU.is_gt))
            step(v.tensor_reduce(mo_tiles, mo_cmp, AX.X, ALU.add))
            step(v.tensor_tensor(mo_ltt, mo_lt8, mo_tiles.unsqueeze(1).broadcast_to([P, E8, E8]), ALU.mult))
            step(v.tensor_reduce(mo_base, mo_ltt, AX.X, ALU.add))
            step(v.tensor_tensor(mo_end8, mo_base, mo_tiles, ALU.add))
            step(v.tensor_scalar(mo_base128, mo_base, float(P), None, ALU.mult))
            step(v.tensor_tensor(mo_geq, mo_iota.unsqueeze(2).broadcast_to([P, SLOT_TILES, E8]),
                                 mo_end8.unsqueeze(1).broadcast_to([P, SLOT_TILES, E8]), ALU.is_ge))
            step(v.tensor_reduce(mo_te, mo_geq, AX.X, ALU.add))
            v.tensor_scalar(mo_tei[:, :], mo_te, float(E8 - 1), None, ALU.min)
            step(v.tensor_tensor(mo_pos, psum[:, 1, 0:P].rearrange("p (t e) -> p t e", e=E8),
                                 mo_base128.unsqueeze(1).broadcast_to([P, NT, E8]), ALU.add))
            for k, oh in enumerate((mo_oh1, mo_oh2)):
                step(v.tensor_tensor(oh, oh, mo_pos, ALU.mult))
                step(v.tensor_reduce(mo_posf[:, k, :], oh, AX.X, ALU.add))
            v.tensor_copy(mo_posi[:, :, :], mo_posf).then_inc(s("place"), 1)
            with v.Fori(0, ITERS) as i:
                for step in range(UNROLL + 3):
                    m = step - 1
                    if 0 <= m < UNROLL:
                        e = v.value_load(mo_tei[0:1, bass.ds(UNROLL * i + m, 1)], min_val=0, max_val=E8 - 1)
                        v.wait_ge(s("h"), UNROLL * i + m + 1)
                        if m >= 2:
                            v.wait_ge(s("hturn"), UNROLL * i + m - 1)
                        v.tensor_tensor(mo_h[:, m % 2, :], psum[:, 2 + m % 2, :],
                                        mo_b1[:, bass.ds(e, 1), :].rearrange("p o n -> p (o n)"), ALU.add).then_inc(s("hb"), 1)
                    m = step - 3
                    if 0 <= m < UNROLL:
                        e = v.value_load(mo_tei[0:1, bass.ds(UNROLL * i + m, 1)], min_val=0, max_val=E8 - 1)
                        v.wait_ge(s("y"), UNROLL * i + m + 1)
                        if m >= 2:
                            v.wait_ge(s(f"ys{m % 2}"), 8 * UNROLL * i + 8 * (m - m % 2))
                        v.tensor_tensor(mo_y[:, m % 2, :], psum[:, 6 + m % 2, 0:D],
                                        mo_b2[:, bass.ds(e, 1), :].rearrange("p o n -> p (o n)"), ALU.add).then_inc(s("y2"), 1)
                for q in range(2):
                    v.wait_ge(s(f"ys{q}"), 8 * UNROLL * i + 8 * UNROLL)
            for t in range(NT):
                for k in range(2):
                    v.wait_ge(s(f"g{t % 4}"), 32 * (t // 4) + 32)
                    if k:
                        v.wait_ge(s("mix"), 2 * t + 1)
                    v.scalar_tensor_tensor(x_tok[:, t, :], mo_yg[:, k, t % 4, :], mo_s[:, k, t:t + 1], x_tok[:, t, :],
                                           ALU.mult, ALU.add).then_inc(s("mix"), 1)

            def added(v, t):
                v.wait_ge(s("mix"), 2 * t + 2)

            norm_vector(v, 2, added)

        COMBOS = [(m, b) for m in range(DK) for b in range(B)]

        def flow_sync(sp):
            s = lambda k: S["fl", k]
            sp.wait_ge(S["ln", "feat"], ln_done(2))
            sp.dma_start(fl_w, I["fl_w"]).then_inc(s("w"), 16)
            sp.dma_start(fl_bias, I["fl_bias"]).then_inc(s("w"), 16)

        def flow_tensor(pe):
            s = lambda k: S["fl", k]
            pe.wait_ge(s("w"), 32)
            for j, (m, b) in enumerate(COMBOS):
                for n, name in enumerate(("q", "k", "v")):
                    if j >= 2:
                        pe.wait_ge(s("sig"), 3 * (j - 2) + n + 1)
                    for k in range(DK):
                        mm = pe.matmul(psum[:, 2 * n + j % 2, :], fl_w[:, n, k, m * P:(m + 1) * P],
                                       x_feat[:, k, b * L:(b + 1) * L], start=k == 0, stop=k == DK - 1)
                    mm.then_inc(s(name), 1)
            pe.wait_ge(s("sig"), 24)
            for j, (m, b) in enumerate(COMBOS):
                pe.wait_ge(s("vec"), 2 * j + 2)
                if j >= 2:
                    pe.wait_ge(s("recip"), 2 * j - 2)
                cols = slice(b * L, (b + 1) * L)
                pe.matmul(psum[:, j % 2, :], fl_mask[:, j, 0, :], fl_qe[:, m, cols], start=True, stop=True).then_inc(s("den"), 1)
                pe.matmul(psum[:, 2 + j % 2, :], fl_mask[:, j, 1, :], fl_ke[:, m, cols], start=True, stop=True).then_inc(s("den"), 1)
            for j, (m, b) in enumerate(COMBOS):
                pe.wait_ge(s("col"), j + 1)
                if j >= 2:
                    pe.wait_ge(s("alloc"), j - 1)
                    pe.wait_ge(s("clip"), j - 1)
                cols = slice(b * L, (b + 1) * L)
                pe.matmul(psum[:, 4 + j % 2, :], fl_mask[:, j, 2, :], fl_qe[:, m, cols], start=True, stop=True).then_inc(s("con"), 1)
                pe.matmul(psum[:, 6 + j % 2, :], fl_mask[:, j, 3, :], fl_ke[:, m, cols], start=True, stop=True).then_inc(s("con"), 1)
            pe.wait_ge(s("recip"), 16)
            for j in range(9):
                if j < 8:
                    m, b = COMBOS[j]
                    pe.wait_ge(s("comp"), j + 1)
                    if j >= 1:
                        pe.wait_ge(s("kcopy"), j)
                        pe.wait_ge(s("vcopy"), j)
                    for n, src in enumerate((fl_k, fl_v)):
                        for tt in range(4):
                            mm = pe.transpose(psum[:, n, tt * P:(tt + 1) * P],
                                              src[:, m, b * L + tt * P:b * L + (tt + 1) * P], ident[:, :])
                        mm.then_inc(s("turn"), 1)
                if j >= 1:
                    i = j - 1
                    m, b = COMBOS[i]
                    pe.wait_ge(s("kcopy"), i + 1)
                    pe.wait_ge(s("vcopy"), i + 1)
                    if i >= 1:
                        pe.wait_ge(s("kvm"), i)
                    for tt in range(4):
                        mm = pe.matmul(psum[:, 2, 0:P], fl_ktok[:, i % 2, tt * P:(tt + 1) * P],
                                       fl_vtok[:, i % 2, tt * P:(tt + 1) * P], start=tt == 0, stop=tt == 3)
                    mm.then_inc(s("kv"), 1)
                    pe.wait_ge(s("kvm"), i + 1)
                    if i >= 1:
                        pe.wait_ge(s("gated"), i)
                    pe.matmul(psum[:, 3, :], fl_kv[:, i % 2, :], fl_q[:, m, b * L:(b + 1) * L],
                              start=True, stop=True).then_inc(s("out"), 1)
            pe.wait_ge(s("gated"), 8)
            for g in range(4):
                for t in range(4 * g, 4 * g + 4):
                    if t >= 2:
                        pe.wait_ge(s("added"), t - 1)
                    for k in range(DK):
                        mm = pe.matmul(psum[:, 4 + t % 2, 0:D], fl_v[:, k, t * P:(t + 1) * P], fl_w[:, 3, k, :],
                                       start=k == 0, stop=k == DK - 1)
                    mm.then_inc(s("outmm"), 1)
                if g >= 1:
                    norm_tensor(pe, 3, g - 1)
            norm_tensor(pe, 3, 3)

        def flow_scalar(a):
            s = lambda k: S["fl", k]
            a.wait_ge(s("w"), 32)
            for j, (m, b) in enumerate(COMBOS):
                cols = slice(b * L, (b + 1) * L)
                a.wait_ge(s("q"), j + 1)
                a.activation(fl_q[:, m, cols], psum[:, j % 2, :], ACT.Sigmoid, bias=fl_bias[:, 0, m:m + 1],
                             accum_out=fl_sum[:, j, 1:2]).then_inc(s("sig"), 1)
                a.wait_ge(s("k"), j + 1)
                a.activation(fl_k[:, m, cols], psum[:, 2 + j % 2, :], ACT.Sigmoid, bias=fl_bias[:, 1, m:m + 1],
                             accum_out=fl_sum[:, j, 0:1]).then_inc(s("sig"), 1)
                a.wait_ge(s("v"), j + 1)
                a.activation(fl_v[:, m, cols], psum[:, 4 + j % 2, :], ACT.Identity,
                             bias=fl_bias[:, 2, m:m + 1]).then_inc(s("sig"), 1)
            for j, (m, b) in enumerate(COMBOS):
                cols = slice(b * L, (b + 1) * L)
                a.wait_ge(s("con"), 2 * j + 1)
                a.activation(fl_alloc[:, m, cols], psum[:, 4 + j % 2, :], ACT.Sigmoid).then_inc(s("alloc"), 1)
            for j, (m, b) in enumerate(COMBOS):
                cols = slice(b * L, (b + 1) * L)
                a.wait_ge(s("max"), j + 1)
                a.activation(fl_ke[:, m, cols], fl_ke[:, m, cols], ACT.Exp, bias=fl_col[:, j, 0:1],
                             accum_out=fl_col[:, j, 1:2]).then_inc(s("smx"), 1)
            for j in range(8):
                a.wait_ge(s("turn"), 2 * j + 1)
                if j >= 2:
                    a.wait_ge(s("kv"), j - 1)
                a.activation(fl_ktok[:, j % 2, :], psum[:, 0, :], ACT.Copy).then_inc(s("kcopy"), 1)
            norm_scalar(a, 3)

        def flow_vector(v):
            s = lambda k: S["fl", k]
            v.wait_ge(S["ln", "turn"], ln_done(2))
            v.tensor_tensor(x_tok[:, :, :], x_tok[:, :, :], bias_row[:, 1, :].unsqueeze(1).broadcast_to([P, NT, D]),
                            ALU.add).then_inc(biased, 1)
            for j, (m, b) in enumerate(COMBOS):
                cols = slice(b * L, (b + 1) * L)
                v.wait_ge(s("sig"), 3 * j + 3)
                v.tensor_scalar(fl_sume[:, j, 0:2], fl_sum[:, j, 0:2], FLOW_EPS, None, ALU.add).then_inc(s("step"), 1)
                v.tensor_scalar(fl_qe[:, m, cols], fl_q[:, m, cols], FLOW_EPS, None, ALU.add)
                v.tensor_scalar(fl_ke[:, m, cols], fl_k[:, m, cols], FLOW_EPS, None, ALU.add)
                v.wait_ge(s("step"), j + 1)
                for n in range(2):
                    v.tensor_scalar(fl_mask[:, j, n, :], head_mask[:, :], fl_sume[:, j, n:n + 1], None,
                                    ALU.mult).then_inc(s("vec"), 1)
            for j, (m, b) in enumerate(COMBOS):
                cols = slice(b * L, (b + 1) * L)
                v.wait_ge(s("den"), 2 * j + 1)
                v.reciprocal(fl_tmp[:, 0, :], psum[:, j % 2, :]).then_inc(s("recip"), 1)
                v.wait_ge(s("den"), 2 * j + 2)
                v.reciprocal(fl_tmp[:, 1, :], psum[:, 2 + j % 2, :]).then_inc(s("recip"), 1)
                v.wait_ge(s("recip"), 2 * j + 2)
                v.tensor_tensor_reduce(fl_q[:, m, cols], fl_q[:, m, cols], fl_tmp[:, 0, :], 1.0, 0.0, ALU.mult, ALU.add,
                                       fl_sum[:, j, 3:4]).then_inc(s("step"), 1)
                v.tensor_tensor_reduce(fl_clip[:, j % 2, :], fl_k[:, m, cols], fl_tmp[:, 1, :], 1.0, 0.0, ALU.mult, ALU.add,
                                       fl_sum[:, j, 2:3]).then_inc(s("step"), 1)
                v.wait_ge(s("step"), 8 + 3 * j + 2)
                v.tensor_scalar(fl_sume[:, j, 2:4], fl_sum[:, j, 2:4], FLOW_EPS, None, ALU.add).then_inc(s("step"), 1)
                v.wait_ge(s("step"), 8 + 3 * j + 3)
                v.tensor_scalar(fl_mask[:, j, 2, :], head_mask[:, :], fl_sume[:, j, 2:3], None, ALU.mult)
                v.tensor_scalar(fl_mask[:, j, 3, :], head_mask[:, :], fl_sume[:, j, 3:4], None, ALU.mult).then_inc(s("col"), 1)
            for j, (m, b) in enumerate(COMBOS):
                cols = slice(b * L, (b + 1) * L)
                v.wait_ge(s("con"), 2 * j + 2)
                v.tensor_scalar(fl_ke[:, m, cols], psum[:, 6 + j % 2, :], 1.0, -1.0, ALU.min, ALU.max).then_inc(s("clip"), 1)
                v.wait_ge(s("clip"), j + 1)
                v.tensor_reduce(fl_col[:, j, 0:1], fl_ke[:, m, cols], AX.X, ALU.max, negate=True).then_inc(s("max"), 1)
            for j, (m, b) in enumerate(COMBOS):
                cols = slice(b * L, (b + 1) * L)
                v.wait_ge(s("smx"), j + 1)
                v.reciprocal(fl_col[:, j, 2:3], fl_col[:, j, 1:2]).then_inc(s("rsum"), 1)
                v.wait_ge(s("rsum"), 2 * j + 1)
                v.tensor_scalar(fl_col[:, j, 3:4], fl_col[:, j, 2:3], float(L), None, ALU.mult).then_inc(s("rsum"), 1)
                v.wait_ge(s("rsum"), 2 * j + 2)
                v.scalar_tensor_tensor(fl_v[:, m, cols], fl_ke[:, m, cols], fl_col[:, j, 3:4], fl_v[:, m, cols],
                                       ALU.mult, ALU.mult).then_inc(s("comp"), 1)
            for j in range(9):
                if j < 8:
                    v.wait_ge(s("turn"), 2 * j + 2)
                    if j >= 2:
                        v.wait_ge(s("kv"), j - 1)
                    v.tensor_copy(fl_vtok[:, j % 2, :], psum[:, 1, :]).then_inc(s("vcopy"), 1)
                if j >= 1:
                    i = j - 1
                    m, b = COMBOS[i]
                    cols = slice(b * L, (b + 1) * L)
                    v.wait_ge(s("kv"), i + 1)
                    if i >= 2:
                        v.wait_ge(s("out"), i - 1)
                    v.tensor_tensor(fl_kv[:, i % 2, :], psum[:, 2, 0:P], head_mask[:, :], ALU.mult).then_inc(s("kvm"), 1)
                    v.wait_ge(s("out"), i + 1)
                    v.wait_ge(s("alloc"), i + 1)
                    v.tensor_tensor(fl_v[:, m, cols], psum[:, 3, :], fl_alloc[:, m, cols], ALU.mult).then_inc(s("gated"), 1)
            v.wait_ge(biased, 2)

            def added(v, t):
                if t % 4:
                    return
                for u in range(t, t + 4):
                    v.wait_ge(s("outmm"), u + 1)
                    v.tensor_tensor(x_tok[:, u, :], psum[:, 4 + u % 2, 0:D], x_tok[:, u, :], ALU.add).then_inc(s("added"), 1)
                v.wait_ge(s("added"), t + 4)

            norm_vector(v, 3, added)

        def sequence_sync(sp):
            s = lambda k: S["se", k]
            sp.wait_ge(S["ln", "feat"], ln_done(3))
            sp.dma_start(se_wr[:, :, :], I["se_wr"]).then_inc(s("small"), 16)
            sp.dma_start(se_br[:, :], I["se_br"]).then_inc(s("small"), 16)
            sp.wait_ge(s("pick"), 1)

            def load(b, slot):
                e = sp.value_load(se_picki[0:1, bass.ds(2 * b + slot, 1)], min_val=0, max_val=E8 - 1)
                sp.dma_start(se_w1[:, slot], I["se_w1"][bass.ds(e, 1)].rearrange("o p n -> (o p) n")).then_inc(s(f"w{slot}"), 16)
                sp.dma_start(se_w2[:, slot], I["se_w2"][bass.ds(e, 1)].rearrange("o p n -> (o p) n")).then_inc(s(f"w{slot}"), 16)

            for slot in range(2):
                load(0, slot)
            with sp.Fori(1, B) as b:
                sp.wait_ge(s("bias"), 2 * b)
                for slot in range(2):
                    sp.wait_ge(s("y"), 8 * b - 4 + 4 * slot)
                    load(b, slot)

        def sequence_tensor(pe):
            s = lambda k: S["se", k]
            pe.wait_ge(S["ln", "feat"], ln_done(4))
            pe.wait_ge(s("small"), 32)
            pe.wait_ge(s("mean"), 2)
            for b in range(B):
                for k in range(DK):
                    mm = pe.matmul(psum[0:1, 0, b * E8:(b + 1) * E8], se_mean[:, k, b:b + 1], se_wr[:, k, :],
                                   start=k == 0, stop=k == DK - 1)
            mm.then_inc(s("rl"), 1)
            pe.wait_ge(s("pick"), 2)
            pe.matmul(psum[:, 1, 0:2 * B], ones[0:1, :], se_cw[0:1].rearrange("p b s -> p (b s)"),
                      start=True, stop=True).then_inc(s("cwmm"), 1)
            pe.wait_ge(s("bias"), 1)
            with pe.Fori(0, B) as b:
                for step in range(3):
                    if step < 2:
                        pe.wait_ge(s(f"w{step}"), 32 * b + 32)
                        for ft in range(8):
                            if step + ft // 4 >= 1:
                                pe.wait_ge(s("gelu"), 16 * b + 8 * step + ft - 3)
                            for k in range(DK):
                                mm = pe.matmul(psum[:, ft % 4, :], se_w1[:, step, k * FF1 + ft * P:k * FF1 + (ft + 1) * P],
                                               x_feat[:, k, bass.ds(b * L, L)], start=k == 0, stop=k == DK - 1)
                            mm.then_inc(s("h"), 1)
                    if step >= 1:
                        m = step - 1
                        pe.wait_ge(s("gelu"), 16 * b + 8 * m + 8)
                        for tt in range(4):
                            if m >= 1:
                                pe.wait_ge(s("add"), 12 * b + 4 + tt + 1)
                            for ft in range(8):
                                mm = pe.matmul(psum[:, 4 + tt, 0:D], se_h[:, m, ft, tt * P:(tt + 1) * P],
                                               se_w2[:, m, ft * D:(ft + 1) * D], start=ft == 0, stop=ft == 7)
                            mm.then_inc(s("y"), 1)
                pe.wait_ge(s("add"), 12 * b + 12)

        def sequence_scalar(a):
            s = lambda k: S["se", k]
            a.wait_ge(s("step"), 2)
            a.activation(se_e[0:1], se_z[0:1], ACT.Exp).then_inc(s("exp"), 1)
            a.wait_ge(s("pick"), 1)
            a.activation(se_m[0:1, 5, :], se_m[0:1, 4, :], ACT.Exp).then_inc(s("exp"), 1)
            with a.Fori(0, B) as b:
                for m in range(2):
                    for ft in range(8):
                        a.wait_ge(s("h"), 16 * b + 8 * m + ft + 1)
                        b1 = se_w1[:, m, DK * FF1 + ft:DK * FF1 + ft + 1]
                        a.activation(se_h[:, m, ft, :], psum[:, ft % 4, :], ACT.Gelu, bias=b1).then_inc(s("gelu"), 1)
                a.wait_ge(s("y"), 8 * b + 8)

            for g in range(4):
                for n in (5, 6):
                    a.wait_ge(S["ln", "aggr"], NT * 5 + 8 * g + 4 * (n - 4))
                    a.activation(ln_std[:, 4 * g:4 * g + 4], ln_mv[:, 4 * g:4 * g + 4, 1], ACT.Sqrt,
                                 bias=eps_col[:, 0:1]).then_inc(S["ln", "sqrt"], 1)

        def sequence_vector(v):
            s = lambda k: S["se", k]
            v.wait_ge(S["ln", "feat"], ln_done(4))
            v.tensor_reduce(se_t4, x_feat[:, :, :].rearrange("p k (b l) -> p k b l", b=B), AX.X, ALU.add).then_inc(s("mean"), 1)
            v.wait_ge(s("mean"), 1)
            v.tensor_scalar(se_mean, se_t4, 1.0 / L, None, ALU.mult).then_inc(s("mean"), 1)
            v.wait_ge(s("rl"), 1)
            one = slice(0, 1)
            v.tensor_tensor(se_logit[one], psum[0:1, 0, 0:B * E8].rearrange("p (b e) -> p b e", e=E8),
                            se_br[one].unsqueeze(1).broadcast_to([1, B, E8]), ALU.add).then_inc(s("mean"), 1)
            v.wait_ge(s("mean"), 3)
            v.tensor_tensor(se_keep, x_tok[:, :, :], gb_row[:, 1, :].unsqueeze(1).broadcast_to([P, NT, D]),
                            ALU.add).then_inc(s("mean"), 1)
            step = top2_vector(v, "se", one, B, se_logit, se_z, se_e, se_pr, se_oh1, se_oh2, se_t, se_m)
            step(v.tensor_scalar(se_pick[one, :, 0], se_m[one, 2, :], -1.0, float(E8), ALU.mult, ALU.add))
            step(v.tensor_scalar(se_pick[one, :, 1], se_m[one, 3, :], -1.0, float(E8), ALU.mult, ALU.add))
            step(v.tensor_tensor(se_m[one, 4, :], se_m[one, 1, :], se_m[one, 0, :], ALU.subtract))
            v.tensor_copy(se_picki[0:1, :], se_pick[one].rearrange("p b s -> p (b s)")).then_inc(s("pick"), 1)
            v.wait_ge(s("exp"), 2)
            step(v.tensor_scalar(se_m[one, 6, :], se_m[one, 5, :], 1.0, None, ALU.add))
            step(v.reciprocal(se_cw[one, :, 0], se_m[one, 6, :]))
            v.tensor_tensor(se_cw[one, :, 1], se_cw[one, :, 0], se_m[one, 5, :], ALU.mult).then_inc(s("pick"), 1)
            v.wait_ge(s("cwmm"), 1)
            v.tensor_copy(se_cwb, psum[:, 1, 0:2 * B].rearrange("p (b s) -> p b s", s=2)).then_inc(s("bias"), 1)
            v.wait_ge(s("bias"), 1)
            with v.Fori(0, B) as b:
                v.wait_ge(s("w0"), 32 * b + 32)
                v.wait_ge(s("w1"), 32 * b + 32)
                v.tensor_copy(se_cwc, se_cwb[:, bass.ds(b, 1), :].rearrange("p o s -> p (o s)")).then_inc(s("cwc"), 1)
                v.wait_ge(s("cwc"), 3 * b + 1)
                v.tensor_scalar(se_bias[:, 0, :], se_w2[:, 0, 8 * D:9 * D], se_cwc[:, 0:1], None, ALU.mult).then_inc(s("cwc"), 1)
                v.wait_ge(s("cwc"), 3 * b + 2)
                v.scalar_tensor_tensor(se_bias[:, 1, :], se_w2[:, 1, 8 * D:9 * D], se_cwc[:, 1:2], se_bias[:, 0, :],
                                       ALU.mult, ALU.add).then_inc(s("cwc"), 1)
                v.wait_ge(s("cwc"), 3 * b + 3)
                v.sem_inc(s("bias"), 2)
                xb = lambda tt: x_tok[:, bass.ds(4 * b + tt, 1), :].rearrange("p o d -> p (o d)")
                v.wait_ge(s("mean"), 4)
                for tt in range(4):
                    v.tensor_tensor(xb(tt), xb(tt), se_bias[:, 1, :], ALU.add).then_inc(s("add"), 1)
                for m in range(2):
                    for tt in range(4):
                        v.wait_ge(s("y"), 8 * b + 4 * m + tt + 1)
                        v.wait_ge(s("add"), 12 * b + 4 * m + tt + 1)
                        v.scalar_tensor_tensor(xb(tt), psum[:, 4 + tt, 0:D], se_cwc[:, m:m + 1], xb(tt),
                                               ALU.mult, ALU.add).then_inc(s("add"), 1)
                v.wait_ge(s("add"), 12 * b + 12)
            for g in range(4):
                norm_group(v, g, NT * 5 + 8 * g, 4 * 5 + 2 * g)
                for t in range(4 * g, 4 * g + 4):
                    v.wait_ge(S["ln", "norm"], NT * 5 + 8 * g + t % 4 + 1)
                    v.tensor_tensor(x_tok[:, t, :], x_tok[:, t, :], gb_row[:, 0, :], ALU.mult).then_inc(s("gamma"), 1)
                for t in range(4 * g, 4 * g + 4):
                    v.wait_ge(s("gamma"), t + 1)
                    v.tensor_tensor(x_tok[:, t, :], x_tok[:, t, :], se_keep[:, t, :], ALU.add).then_inc(s("beta"), 1)
                v.wait_ge(s("beta"), 4 * g + 4)
                norm_group(v, g, NT * 5 + 8 * g + 4, 4 * 5 + 2 * g + 1)

        stop = STOP

        @block.sync
        def _(sp):
            sync_hyena(sp)
            if stop >= 1:
                attention_sync(sp, 1, 8)
            if stop >= 2:
                tokens_sync(sp)
            if stop >= 3:
                flow_sync(sp)
            if stop >= 4:
                attention_sync(sp, 4, 2)
            if stop >= 5:
                sequence_sync(sp)
            for b in range(B):
                if stop == 5:
                    sp.wait_ge(S["ln", "norm"], NT * 5 + 8 * b + 8)
                else:
                    sp.wait_ge(S["ln", "norm"], NT * stop + 4 * b + 4)
                for e in range(2):
                    sp.dma_start(out[b].rearrange("(j p e) d -> e p j d", j=2, e=2)[e],
                                 x_tok[:, 4 * b + 2 * e:4 * b + 2 * e + 2, :]).then_inc(store, 16)
            sp.wait_ge(store, 16 * 2 * B)

        @block.tensor
        def _(pe):
            hyena_tensor(pe)
            if stop >= 1:
                attention_tensor(pe, 1, 8)
            if stop >= 2:
                tokens_tensor(pe)
            if stop >= 3:
                flow_tensor(pe)
            if stop >= 4:
                attention_tensor(pe, 4, 2)
            if stop >= 5:
                sequence_tensor(pe)

        @block.gpsimd
        def _(gp):
            if stop >= 1:
                attention_gpsimd(gp, 1, I["at1_w"], I["at1_wout"], 8)
            if stop >= 2:
                tokens_gpsimd(gp)
            if stop >= 4:
                attention_gpsimd(gp, 4, I["at4_w"], I["at4_wout"], 2)

        @block.scalar
        def _(a):
            hyena_scalar(a)
            if stop >= 1:
                attention_scalar(a, 1, 8)
            if stop >= 2:
                tokens_scalar(a)
            if stop >= 3:
                flow_scalar(a)
            if stop >= 4:
                attention_scalar(a, 4, 2)
            if stop >= 5:
                sequence_scalar(a)

        @block.vector
        def _(v):
            hyena_vector(v)
            if stop >= 1:
                attention_vector(v, 1, 8)
            if stop >= 2:
                tokens_vector(v)
            if stop >= 3:
                flow_vector(v)
            if stop >= 4:
                attention_vector(v, 4, 2)
            if stop >= 5:
                sequence_vector(v)


STOP = 5


def _transforms():
    f = np.arange(256)
    t = np.arange(512)
    ang = 2 * np.pi * (((2 * f[:, None] + 1) * t[None, :]) % 2048) / 2048.0
    cos, sin = np.cos(ang), np.sin(ang)
    fwd = np.zeros((P, 4, 4, P), np.float32)
    inv = np.zeros((P, 2, 2, 2, 256), np.float32)
    for e in range(2):
        for j in range(2):
            tt = 2 * (128 * j + np.arange(P)) + e
            for g in range(2):
                fwd[:, 2 * e + j, 2 * g, :] = cos[g * P:(g + 1) * P, tt].T
                fwd[:, 2 * e + j, 2 * g + 1, :] = -sin[g * P:(g + 1) * P, tt].T
        tt = 2 * np.arange(256) + e
        for g in range(2):
            inv[:, e, g, 0, :] = cos[g * P:(g + 1) * P, tt] / 512.0
            inv[:, e, g, 1, :] = -sin[g * P:(g + 1) * P, tt] / 512.0
    return fwd, inv


def _rows(w, pad=None):
    w = np.asarray(w)
    if pad and w.shape[0] < pad:
        w = np.concatenate([w, np.zeros((pad - w.shape[0],) + w.shape[1:], w.dtype)])
    return np.ascontiguousarray(w.reshape(-1, P, *w.shape[1:]).swapaxes(0, 1))


def _attention(wq, wk, wv, wout):
    pairs = wq.shape[1] // P
    w = np.zeros((pairs + 1, P, 6, P), np.float32)
    for n, m in enumerate((wq, wk, wv)):
        r = _rows(m, 256)
        w[:pairs, :, 2 * n:2 * n + 2, :] = r.reshape(P, 2, pairs, P).transpose(2, 0, 1, 3)
    return w, np.ascontiguousarray(wout.reshape(pairs, P, D).swapaxes(0, 1))


def _experts(w1, b1, w2):
    e, _, f = w1.shape
    one = w1.reshape(e, DK, P, f).transpose(0, 2, 1, 3).reshape(e, P, DK * f)
    bias = b1.reshape(e, f // P, P).transpose(0, 2, 1)
    two = w2.reshape(e, f // P, P, D).transpose(0, 2, 1, 3)
    return np.ascontiguousarray(np.concatenate([one, bias], 2)), np.ascontiguousarray(two)


def layouts(x, ctx_768, **W):
    a = {}
    order = np.concatenate([np.arange(0, L, 2), np.arange(1, L, 2)])
    xo = np.asarray(x)[:, order, :].reshape(T, D)
    a["x_tok"] = np.ascontiguousarray(xo.reshape(NT, P, D).transpose(1, 0, 2))
    a["x_feat"] = _rows(xo.T)
    a["ctx_feat"] = _rows(np.asarray(ctx_768).reshape(T, DC).T, 256)
    a["hy_win"] = _rows(W["L0_attn_W_in"].T)
    a["hy_wout"] = _rows(W["L0_attn_W_out"].T)
    time = np.linspace(0.0, 1.0, L, dtype=np.float32)[order]
    a["time"] = np.ascontiguousarray(np.broadcast_to(time, (P, L)))
    a["f_w1"] = np.ascontiguousarray(W["L0_attn_f_w1"][:, :, 0].T)
    a["f_b1"] = np.ascontiguousarray(W["L0_attn_f_b1"].T)
    a["f_w2b"] = np.ascontiguousarray(np.concatenate(
        [W["L0_attn_f_w2"].transpose(2, 0, 1), W["L0_attn_f_b2"][None]]))
    a["dft_fwd"], a["dft_inv"] = _transforms()
    a["ident"] = np.eye(P, dtype=np.float32)
    a["head_mask"] = np.kron(np.eye(8), np.ones((16, 16))).astype(np.float32)
    a["rank8"] = np.ascontiguousarray(np.broadcast_to(8 - np.arange(8, dtype=np.float32), (P, 8)))
    a["bias_row"] = np.ascontiguousarray(np.broadcast_to(np.stack(
        [W["L0_xattn_b_out"], W["L1_attn_bo"], W["L1_xattn_bo"]]), (P, 3, D)))
    a["gb_row"] = np.ascontiguousarray(np.broadcast_to(np.stack(
        [W["L1_ffn_gamma"], W["L1_ffn_beta"]]), (P, 2, D)))
    kv = W["L0_xattn_w_kv"]
    a["at1_w"], a["at1_wout"] = _attention(W["L0_xattn_w_q"], kv[:, :1024], kv[:, 1024:], W["L0_xattn_w_out"])
    a["at4_w"], a["at4_wout"] = _attention(W["L1_xattn_Wq"].T, W["L1_xattn_Wk"].T, W["L1_xattn_Wv"].T,
                                           W["L1_xattn_Wo"].T)
    a["mo_wg"] = _rows(W["L0_ffn_Wg"])
    a["mo_w1"] = np.ascontiguousarray(W["L0_ffn_W1"].reshape(E8, DK, P, FF0).transpose(2, 0, 1, 3).reshape(P, E8, -1))
    a["mo_w2"] = np.ascontiguousarray(W["L0_ffn_W2"].reshape(E8, 4, P, D).transpose(2, 0, 1, 3).reshape(P, E8, -1))
    spread = lambda x: np.ascontiguousarray(np.broadcast_to(x, (P,) + x.shape))
    a["mo_b1"], a["mo_b2"] = spread(W["L0_ffn_b1"]), spread(W["L0_ffn_b2"])
    a["mo_lt8"] = spread(np.tril(np.ones((E8, E8), np.float32), -1))
    a["mo_step128"] = spread(np.arange(16, dtype=np.float32) * P)
    a["mo_iota"] = spread(np.arange(SLOT_TILES, dtype=np.float32))
    a["mo_before"] = np.triu(np.ones((P, P), np.float32), 1)
    a["fl_w"] = np.ascontiguousarray(np.stack([_rows(W[f"L1_attn_W{n}"].T) for n in "qkvo"], 1))
    a["fl_bias"] = np.ascontiguousarray(np.stack([W[f"L1_attn_b{n}"].reshape(DK, P).T for n in "qkv"], 1))
    a["se_wr"] = _rows(W["L1_ffn_Wr"])
    a["se_br"] = np.ascontiguousarray(np.broadcast_to(W["L1_ffn_br"], (P, E8)))
    a["se_w1"], w2 = _experts(W["L1_ffn_W1"], W["L1_ffn_b1"], W["L1_ffn_W2"])
    a["se_w2"] = np.ascontiguousarray(np.concatenate(
        [w2.reshape(E8, P, -1), np.broadcast_to(W["L1_ffn_b2"][:, None, :], (E8, P, D))], 2))
    return a


def program(nc, arrays):
    I = {n: nc.dram_tensor("in_" + n, a.shape, mybir.dt.from_np(a.dtype), kind="ExternalInput").ap() for n, a in arrays.items()}
    out = nc.dram_tensor("out", (B, L, D), F32, kind="ExternalOutput").ap()
    build(nc, I, out)


def kernel(**inputs):
    import concourse.bacc as _bacc
    from concourse.bass_utils import run_bass_kernel_spmd as _run

    nc = _bacc.Bacc("TRN2", target_bir_lowering=False, num_devices=1)
    arrays = layouts(**{k: np.asarray(v) for k, v in inputs.items()})
    program(nc, arrays)
    r = _run(nc, [{"in_" + k: v for k, v in arrays.items()}], core_ids=[0])
    return r.results[0]["out"]
```

```python
from contextlib import ExitStack

import numpy as np

import concourse.bass as bass
from concourse import mybir

F32 = mybir.dt.float32
F32R = mybir.dt.float32r
I32 = mybir.dt.int32
ALU = mybir.AluOpType
ACT = mybir.ActivationFunctionType
AX = mybir.AxisListType

P = 128
B, L, D = 4, 512, 256
T = B * L
NT = T // P
DK = D // P
DC = 192
E8 = 8
HID = 64
DH = 64
FF0, FF1 = 512, 1024
SLOT_TILES = 2 * T // P + E8
LN_EPS = 1e-5
FLOW_EPS = 1e-6
ROW = D + 1


def build(nc, I, out):
    with ExitStack() as ctx:
        def sb(name, shape, dt=F32):
            return ctx.enter_context(nc.sbuf_tensor(name, shape, dt))

        def sem(name):
            return ctx.enter_context(nc.semaphore(name))

        x_wide = sb("x_wide", [P, NT, D + 4])
        x_tok = x_wide[:, :, 0:D]
        x_feat = sb("x_feat", [P, DK, T])
        ident = sb("ident", [P, P])
        head_mask = sb("head_mask", [P, P])
        rank8 = sb("rank8", [P, E8])
        bias_row = sb("bias_row", [P, 3, D])
        gb_row = sb("gb_row", [P, 2, D])
        ones = sb("ones", [P, P])
        ln_stat = sb("ln_stat", [P, NT, 6])
        ln_mv = sb("ln_mv", [P, NT, 2])
        ln_std = sb("ln_std", [P, NT])
        ln_rstd = sb("ln_rstd", [P, NT])
        eps_col = sb("eps_col", [P, 1])
        at_negmax = sb("at_negmax", [P, 2])
        se_wr = sb("se_wr", [P, DK, E8])
        se_br = sb("se_br", [P, E8])
        REGION, SHARED, SPLIT = 42720, 24288, 18432
        base = -(-nc.sbuf_base // 64) * 64
        sb("region", [P, REGION + 16])

        def place(name, at, shape, dt=F32):
            return nc.alloc_sbuf_tensor_at(name, shape, dt, offset=base + 4 * at)

        hyena_mem = place("hyena_mem", 0, [P, REGION])
        shared_mem = place("shared_mem", 0, [P, SHARED])
        late_mem = place("late_mem", SHARED, [P, SPLIT])
        tail_mem = place("tail_mem", 4096, [P, REGION - 4096])
        psum = ctx.enter_context(nc.psum_tensor("psum", [P, 8, 512], F32))

        class Carve:
            def __init__(self, mem, at=0):
                self.mem, self.at = mem, at

            def __call__(self, *dims):
                n = int(np.prod(dims))
                a = self.mem[:, self.at:self.at + n]
                self.at += n
                assert self.at <= self.mem.shape[1], self.at
                if len(dims) > 1:
                    names = "abcdef"[:len(dims)]
                    a = a.rearrange(f"p ({' '.join(names)}) -> p {' '.join(names)}",
                                    **{k: v for k, v in zip(names, dims)})
                return a

        c = Carve(hyena_mem)
        hy_gate1 = c(4, B, D)
        hy_v = c(4, B, D)
        hy_gate2 = c(DK, T)
        hy_xs = c(2, 2, 2, 512)
        hy_a = c(2, 2, 512)
        hy_b = c(2, 2, 512)
        hy_odd = c(2, 512)
        hy_sd = c(2, 2, 2, 2, 512)
        hy_spec = c(2, 2, 2, 512)
        hy_fwd = c(4, 4, P)
        hy_inv = c(2, 2, 2, D)
        hy_win = c(DK, 3 * D)
        hy_wout = c(DK, D)
        hy_end = c.at
        c = Carve(hyena_mem, 3 * 4096 + 4 * 2048 + 1024)
        hy_time = c(L)
        hy_phi = c(2, L)
        hy_sig = c(2, L)
        hy_w1 = c(2)
        hy_b1 = c(2)
        hy_w2 = c(2, D)
        hy_h = c(4, 2 * D)

        ctx_feat = Carve(shared_mem)(DK, T)
        c = Carve(shared_mem, 4096)
        at_wout = c(8, D)
        at_w = c(6, P)
        at_p = c(4, L)
        at_ot = c(2, L)
        at_oc = c(L)
        at_sum = c(16)
        at_rinv = c(16)
        at_end = c.at
        spl = [SHARED]

        def split_mem(name, *dims):
            n = int(np.prod(dims))
            t = place(name, spl[0], [P, *dims], F32R)
            spl[0] += n
            assert spl[0] <= REGION
            return t

        at_qn = split_mem("at_qn", 2, L)
        at_kn = split_mem("at_kn", 2, L)
        at_qd = split_mem("at_qd", 2, 2, L)
        at_kd = split_mem("at_kd", 2, 2, 2, L)
        at_vd = split_mem("at_vd", 2, 4, 4, DH)
        at_ph = split_mem("at_ph", 2, 4, L)
        at_pl = split_mem("at_pl", 2, 4, L)

        c = Carve(shared_mem, at_end)
        mo_w1 = c(E8, DK * FF0)
        mo_b1 = c(E8, FF0)
        mo_wg = c(DK, E8)
        mo_lt8 = c(E8, E8)
        mo_step128 = c(16)
        mo_iota = c(SLOT_TILES)
        mo_number = c(NT)
        mo_spare = c(SLOT_TILES)
        mo_before = c(P)
        c = Carve(late_mem)
        mo_w2 = c(E8, 4 * D)
        mo_b2 = c(E8, D)
        mo_x = c(2, ROW)
        mo_xt = c(2, D)
        mo_h = c(2, FF0)
        mo_ht = c(2, FF0)
        mo_y = c(2, D)
        mo_yg = c(2, 8, D)
        zero_row = Carve(hyena_mem, REGION - ROW)(ROW)
        c = Carve(shared_mem, 4096)
        mo_logit = c(NT, E8)
        mo_z = c(NT, E8)
        mo_e = c(NT, E8)
        mo_pr = c(NT, E8)
        mo_oh1 = c(NT, E8)
        mo_oh2 = c(NT, E8)
        mo_t = c(NT, E8)
        mo_both_pad = c(2 * NT, E8)
        mo_both = mo_both_pad[:, NT:2 * NT, :]
        mo_pos = c(NT, E8)
        mo_m = c(6, NT)
        mo_s = c(2, NT)
        mo_mine = c(E8)
        mo_cmp = c(E8, 16)
        mo_tiles = c(E8)
        mo_ltt = c(E8, E8)
        mo_base = c(E8)
        mo_end8 = c(E8)
        mo_base128 = c(E8)
        mo_geq = c(SLOT_TILES, E8)
        mo_te = c(SLOT_TILES)
        mo_posf = c(2, NT)
        assert c.at <= at_end
        mo_tei = sb("mo_tei", [P, SLOT_TILES], I32)
        mo_posi = sb("mo_posi", [P, 2, NT], I32)
        mo_dest = sb("mo_dest", [P, SLOT_TILES], I32)

        c = Carve(tail_mem)
        fl_w = c(4, DK, D)
        fl_bias = c(3, DK)
        fl_k = c(DK, T)
        fl_q = c(DK, T)
        fl_v = c(DK, T)
        fl_ke = c(DK, T)
        fl_qe = c(DK, T)
        fl_alloc = c(DK, T)
        fl_mask = c(8, 4, P)
        fl_spread = c(16, P)
        fl_rec = c(512)
        fl_sum = c(8, 4)
        fl_sume = c(8, 4)
        fl_clip = c(2, 512)
        fl_col = c(8, 4)
        fl_ktok = c(2, 512)
        fl_vtok = c(2, 512)
        fl_kv = c(2, P)
        c = Carve(tail_mem)
        se_h = c(2, 8, 512)
        se_w1 = c(2, DK * FF1 + 8)
        se_w2 = c(2, 2, 8 * D + D)
        se_mean = c(DK, B)
        se_logit = c(B, E8)
        se_z = c(B, E8)
        se_e = c(B, E8)
        se_pr = c(B, E8)
        se_oh1 = c(B, E8)
        se_oh2 = c(B, E8)
        se_t = c(B, E8)
        se_m = c(8, B)
        se_pick = c(B, 2)
        se_picki = sb("se_picki", [P, B * 2], I32)
        se_cw = c(B, 2)
        se_cwb = c(B, 2)
        se_bias = c(2, D)
        se_t4 = c(DK, B)
        se_keep = c(NT, D)
        se_cwc = c(2)
        se_xs = place("se_xs", 0, [P, 2, 2, DK, L], F32R)
        SE_SPLIT = REGION - 4 * DK * FF1
        assert 4096 + c.at <= SE_SPLIT
        se_ws = place("se_ws", SE_SPLIT, [P, 2, 2, DK * FF1], F32R)

        ld_const, ld_x, ld_hy, ld_ctx = (sem(n) for n in ("ld_const", "ld_x", "ld_hy", "ld_ctx"))
        S = {}

        def sems(stage, names):
            for n in names.split():
                S[stage, n] = sem(f"{stage}_{n}")

        sems("hy", "time phi filt filtcopy proj projcopy gate2 gate2copy dft odd prodim dve dvex inv gated1 sd sdsum gated2 outmm added step")
        sems("ln", "stat aggr sqrt rstd norm turn feat")
        ln_done = lambda n: NT * (n + 1)
        for n in (1, 4):
            sems(f"at{n}", "w wout q k v qh kh vh ql kl vl qd kd s max exp rinv pn turn ph pl av oc ot y add")
        sems("mo", "fill w wlate rl step exp both rank place scatter x0 x1 dest xturn xt h hb hturn relu y y2 ys0 ys1 g0 g1 mix")
        sems("fl", "w step q sig k v den recip vec col con alloc clip max smx rsum comp turn kcopy vcopy kv kvm out gated outmm added")
        sems("se", "w0 w1 u0 u1 step mean rl exp pick cwmm cwc hi lo h gelu y bias add affine")
        biased = sem("biased")
        store = sem("store")

        block = ctx.enter_context(nc.Block())

        sorted_x = nc.dram_tensor("sorted_x", (SLOT_TILES * P, ROW), F32).ap()


        def sync_hyena(sp):
            sp.dma_start(hy_time, I["time"]).then_inc(ld_hy, 16)
            for dst, name in ((hy_w1, "f_w1"), (hy_b1, "f_b1")):
                sp.dma_start(dst[0:HID, :], I[name]).then_inc(ld_hy, 16)
            sp.dma_start(hy_w2[0:HID + 1], I["f_w2b"]).then_inc(ld_hy, 16)
            sp.dma_start(hy_win, I["hy_win"]).then_inc(ld_x, 16)
            sp.dma_start(x_feat[:, :, :], I["x_feat"]).then_inc(ld_x, 16)
            sp.dma_start(hy_fwd, I["dft_fwd"]).then_inc(ld_const, 16)
            sp.dma_start(hy_inv, I["dft_inv"]).then_inc(ld_const, 16)
            sp.dma_start(x_tok[:, :, :], I["x_tok"]).then_inc(ld_const, 16)
            sp.dma_start(hy_wout, I["hy_wout"]).then_inc(ld_const, 16)
            sp.dma_start(ident[:, :], I["ident"]).then_inc(ld_const, 16)
            sp.dma_start(head_mask[:, :], I["head_mask"]).then_inc(ld_const, 16)
            sp.dma_start(rank8[:, :], I["rank8"]).then_inc(ld_const, 16)
            sp.dma_start(bias_row[:, :, :], I["bias_row"]).then_inc(ld_const, 16)
            sp.dma_start(gb_row[:, :, :], I["gb_row"]).then_inc(ld_const, 16)
            sp.dma_start(se_wr[:, :, :], I["se_wr"]).then_inc(ld_const, 16)
            sp.dma_start(se_br[:, :], I["se_br"]).then_inc(ld_const, 16)
            sp.wait_ge(S["hy", "dve"], 1)
            sp.dma_start(sorted_x.rearrange("(i p) d -> p i d", p=P),
                         zero_row.unsqueeze(1).broadcast_to([P, SLOT_TILES, ROW])).then_inc(S["mo", "fill"], 16)
            sp.wait_ge(S["hy", "gated1"], 8)
            sp.dma_start(ctx_feat, I["ctx_feat"]).then_inc(ld_ctx, 16)

        ALL_CONST = 11 * 16

        def hold(eng, sem, count):
            if not isinstance(count, int) or count > 0:
                eng.wait_ge(sem, count)

        TAIL = 17
        PARTS = {"q": 2, "k": 2, "v": 8}
        PROJECT = {0: ("k", [0]), 1: ("k", [1]), 3: ("q", [0]), 4: ("q", [1]), 6: ("v", [0, 1, 2, 3]), 7: ("v", [4, 5, 6, 7])}

        def over_pairs(eng, pairs, steps):
            steps(0, range(32), True, False)
            with eng.Fori(1, pairs) as i:
                steps(i, range(32), False, False)
            steps(pairs, range(TAIL), False, True)

        def back(s, by, first, last):
            m = s - by
            return None if (first and m < 0) or (last and m >= 0) else m

        def attention_sync(sp, n, pairs):
            s = lambda k: S[f"at{n}", k]

            def stack(u, slot):
                sp.wait_ge(s("kl"), u + 1)
                for h in range(2):
                    for half in range(2):
                        sp.dma_start(at_kd[half * DH:(half + 1) * DH, slot, h, :, :].bitcast(F32),
                                     at_kn[h * DH:(h + 1) * DH, :, :].bitcast(F32)).then_inc(s("kd"), 16)
                sp.wait_ge(s("ql"), u + 1)
                for h in range(2):
                    for part in range(2):
                        sp.dma_start(at_qd[part * DH:(part + 1) * DH, slot, h, :].bitcast(F32),
                                     at_qn[h * DH:(h + 1) * DH, part, :].bitcast(F32)).then_inc(s("qd"), 16)

            stack(0, 0)
            with sp.Fori(0, pairs) as i:
                for b in range(B):
                    stack(4 * i + (b + 1), (b + 1) % 2)
            sp.wait_ge(s("qd"), 64 * (4 * pairs + 1))
            sp.wait_ge(s("kd"), 64 * (4 * pairs + 1))

        def attention_gpsimd(gp, n, w, wout, pairs):
            s = lambda k: S[f"at{n}", k]

            def load(what, pair, before):
                at = {"q": 0, "k": 2, "v": 4}[what]
                hold(gp, s("w"), before)
                gp.dma_start(at_w[:, at:at + 2, :], w[pair, :, at:at + 2, :]).then_inc(s("w"), 16)

            if n == 1:
                gp.wait_ge(S["hy", "dft"], 10)
            else:
                gp.wait_ge(S["fl", "turn"], 16)
            for j, what in enumerate("kqv"):
                load(what, 0, 16 * j)
            if n == 4:
                gp.wait_ge(S["fl", "outmm"], NT // 2)
            gp.dma_start(at_wout[:, 0:pairs, :], wout).then_inc(s("wout"), 16)

            def steps(i, span, first, last):
                for st in span:
                    m = back(st, 2, first, last)
                    if m is not None:
                        gp.wait_ge(s("rinv"), 32 * i + (m + 1))
                        gp.tensor_tensor(at_p[:, m % 4, :], at_p[:, m % 4, :], at_rinv[:, m % 16:m % 16 + 1].broadcast_to([P, L]),
                                         ALU.mult).then_inc(s("pn"), 1)
                    if not last and st in (18, 21, 24):
                        j = (st - 18) // 3
                        gp.wait_ge(s("kqv"[j]), 4 * i + 4)
                        load("kqv"[j], i + 1, 48 * i + (48 + 16 * j))

            over_pairs(gp, pairs, steps)

        def norm_stats(v, t0, c0, added=lambda v, t: None):
            s = lambda k: S["ln", k]
            for t in range(t0, t0 + 4):
                added(v, t)
                v.bn_stats(ln_stat[:, t, :], x_tok[:, t, :]).then_inc(s("stat"), 1)
            for t in range(t0, t0 + 4):
                v.wait_ge(s("stat"), c0 + t % 4 + 1)
                v.bn_aggr(ln_mv[:, t, :], ln_stat[:, t, :]).then_inc(s("aggr"), 1)

        def norm_apply(v, t0, r0):
            s = lambda k: S["ln", k]
            v.wait_ge(s("sqrt"), r0 + 1)
            v.reciprocal(ln_rstd[:, t0:t0 + 4], ln_std[:, t0:t0 + 4]).then_inc(s("rstd"), 1)
            v.wait_ge(s("rstd"), r0 + 1)
            for t in range(t0, t0 + 4):
                v.tensor_scalar(x_tok[:, t, :], x_tok[:, t, :], ln_mv[:, t, 0:1], ln_rstd[:, t:t + 1],
                                ALU.subtract, ALU.mult).then_inc(s("norm"), 1)

        def norm_vector(v, n, added=lambda v, t: None):
            for g in range(NT // 4 + 1):
                if g < NT // 4:
                    norm_stats(v, 4 * g, NT * n + 4 * g, added)
                if g >= 1:
                    norm_apply(v, 4 * g - 4, 4 * n + g - 1)

        def norm_tensor(pe, n, g):
            s = lambda k: S["ln", k]
            c0 = NT * n
            for t in range(4 * g, 4 * g + 4, 2):
                if t >= 4:
                    pe.wait_ge(s("feat"), c0 + t - 2)
                for h in range(2):
                    pe.wait_ge(s("norm"), c0 + t + h + 1)
                    for k in range(DK):
                        mm = pe.transpose(psum[:, 6 + t // 2 % 2, (2 * h + k) * P:(2 * h + k + 1) * P],
                                          x_tok[:, t + h, k * P:(k + 1) * P], ident[:, :])
                mm.then_inc(s("turn"), 2)

        def norm_scalar(a, n):
            s = lambda k: S["ln", k]
            c0 = NT * n

            def root(g):
                a.wait_ge(s("aggr"), c0 + 4 * g + 4)
                a.activation(ln_std[:, 4 * g:4 * g + 4], ln_mv[:, 4 * g:4 * g + 4, 1], ACT.Sqrt,
                             bias=eps_col[:, 0:1]).then_inc(s("sqrt"), 1)

            root(0)
            for g in range(NT // 4):
                if g < 3:
                    root(g + 1)
                for t in range(4 * g, 4 * g + 4, 2):
                    a.wait_ge(s("turn"), c0 + t + 2)
                    a.activation(x_feat[:, :, t * P:(t + 2) * P].rearrange("p k (h c) -> p k h c", h=2),
                                 psum[:, 6 + t // 2 % 2, :].rearrange("p (h k c) -> p k h c", h=2, k=DK),
                                 ACT.Copy).then_inc(s("feat"), 2)

        def project_out(pe, g, feat, w, outmm, added):
            for p in (2 * g, 2 * g + 1):
                if p >= 2:
                    pe.wait_ge(added, p - 1)
                for h in range(2):
                    t = 2 * p + h
                    for k in range(DK):
                        mm = pe.matmul(psum[:, 4 + p % 2, h * D:(h + 1) * D], feat[:, k, t * P:(t + 1) * P], w[:, k, :],
                                       start=k == 0, stop=k == DK - 1)
                mm.then_inc(outmm, 1)

        def add_out(v, t, outmm, added):
            if t % 4 == 0:
                for p in (t // 2, t // 2 + 1):
                    v.wait_ge(outmm, p + 1)
                    v.tensor_tensor(x_tok[:, 2 * p:2 * p + 2, :], psum[:, 4 + p % 2, :].rearrange("p (t d) -> p t d", t=2),
                                    x_tok[:, 2 * p:2 * p + 2, :], ALU.add).then_inc(added, 1)
            v.wait_ge(added, t // 2 + 1)

        def hyena_tensor(pe):
            s = lambda k: S["hy", k]
            pe.wait_ge(ld_hy, 64)
            pe.wait_ge(s("phi"), 3)
            for ej in range(4):
                for o in range(2):
                    mm = pe.matmul(psum[:, ej, o * D:(o + 1) * D], hy_phi[0:HID + 1, o, ej * P:(ej + 1) * P],
                                   hy_w2[0:HID + 1, o, :], start=True, stop=True)
                mm.then_inc(s("filt"), 1)
            pe.wait_ge(ld_x, 32)
            for t in range(NT):
                if t >= 4:
                    pe.wait_ge(s("projcopy"), t - 3)
                for k in range(DK):
                    mm = pe.matmul(psum[:, 4 + t % 4, :], x_feat[:, k, t * P:(t + 1) * P], hy_win[:, k, 0:512],
                                   start=k == 0, stop=k == DK - 1)
                mm.then_inc(s("proj"), 1)
            def second_gate(m):
                for b in range(B):
                    for k in range(DK):
                        mm = pe.matmul(psum[:, b, :], hy_win[:, k, 512 + m * P:512 + (m + 1) * P],
                                       x_feat[:, k, b * L:(b + 1) * L], start=k == 0, stop=k == DK - 1)
                    mm.then_inc(s("gate2"), 1)

            pe.wait_ge(ld_const, ALL_CONST)
            pe.wait_ge(s("filtcopy"), 4)
            pe.wait_ge(s("projcopy"), NT)

            def forward(job, src, g):
                bank = 4 * (job % 2)
                if job >= 2:
                    pe.wait_ge(s("dvex"), 2 * (job - 1))
                for e in range(2):
                    for part in range(2):
                        for j in range(2):
                            mm = pe.matmul(psum[:, bank + 2 * e + part, :], hy_fwd[:, 2 * e + j, 2 * g + part, :],
                                           src(2 * e + j), start=j == 0, stop=j == 1)
                mm.then_inc(s("dft"), 1)

            for g in range(2):
                forward(g, lambda ej: hy_h[:, ej, :], g)
            job = 2
            for o in range(2):
                for half in range(2):
                    for g in range(2):
                        if o == 1:
                            pe.wait_ge(s("gated1"), 4 if half + g == 0 else 8)
                        if job == 6:
                            pe.wait_ge(s("gate2copy"), 4)
                        forward(job, lambda ej: hy_v[:, ej, 2 * half:2 * half + 2, :], g)
                        job += 1
                pe.wait_ge(s("dvex"), 2 * (job - 1))
                second_gate(o)
                if o == 0:
                    for half in range(2):
                        pe.wait_ge(s("sd"), 2 * half + 2)
                        pe.wait_ge(s("sdsum"), 2 * half + 2)
                        if half == 0:
                            pe.wait_ge(s("dvex"), 2 * job)
                        for ej in range(4):
                            n = 4 * half + ej
                            e, j = ej // 2, ej % 2
                            if n >= 4:
                                pe.wait_ge(s("gated1"), n - 3)
                            for g in range(2):
                                for part in range(2):
                                    mm = pe.matmul(psum[:, 4 + n % 4, :], hy_inv[:, e, g, part, j * P:(j + 1) * P],
                                                   hy_sd[:, half, e, g, part, :], start=g + part == 0, stop=g + part == 2)
                            mm.then_inc(s("inv"), 1)
                else:
                    for half in range(2):
                        pe.wait_ge(s("sd"), 4 + 2 * half + 2)
                        pe.wait_ge(s("sdsum"), 4 + 2 * half + 2)
                        if half == 0:
                            pe.wait_ge(s("gate2copy"), 8)
                        for b2 in range(2):
                            for m in range(DK):
                                n = 4 * half + 2 * b2 + m
                                if n >= 4:
                                    pe.wait_ge(s("gated2"), n - 3)
                                col = b2 * D + m * P
                                for e in range(2):
                                    for g in range(2):
                                        for part in range(2):
                                            mm = pe.matmul(psum[:, n % 4, e * D:(e + 1) * D],
                                                           hy_sd[:, half, e, g, part, col:col + P],
                                                           hy_inv[:, e, g, part, :], start=g + part == 0, stop=g + part == 2)
                                mm.then_inc(s("inv"), 1)
            for g in range(4):
                pe.wait_ge(s("gated2"), 2 * g + 2)
                project_out(pe, g, hy_gate2, hy_wout, s("outmm"), s("added"))
                if g >= 1:
                    norm_tensor(pe, 0, g - 1)
            norm_tensor(pe, 0, 3)

        def hyena_scalar(a):
            s = lambda k: S["hy", k]
            a.wait_ge(ld_hy, 64)
            for o in range(2):
                a.activation(hy_phi[0:HID, o, :], hy_time[0:HID], ACT.Identity, bias=hy_b1[0:HID, o:o + 1],
                             scale=hy_w1[0:HID, o:o + 1]).then_inc(s("time"), 1)
                a.activation(hy_sig[0:HID, o, :], hy_time[0:HID], ACT.Sigmoid, bias=hy_b1[0:HID, o:o + 1],
                             scale=hy_w1[0:HID, o:o + 1]).then_inc(s("time"), 1)
            for ej in range(4):
                a.wait_ge(s("filt"), ej + 1)
                a.activation(hy_h[:, ej, :], psum[:, ej, :], ACT.Copy).then_inc(s("filtcopy"), 1)
            for job in range(10):
                a.wait_ge(s("dft"), job + 1)
                if job >= 1:
                    a.wait_ge(s("dvex"), 2 * job)
                bank = 4 * (job % 2)
                a.activation(hy_odd, psum[:, bank + 2:bank + 4, :], ACT.Copy).then_inc(s("odd"), 1)
                if job in (5, 9):
                    m = (job - 5) // 4
                    for b in range(B):
                        a.wait_ge(s("gate2"), 4 * m + b + 1)
                        a.activation(hy_gate2[:, m, b * L:(b + 1) * L], psum[:, b, :], ACT.Copy).then_inc(s("gate2copy"), 1)
            norm_scalar(a, 0)

        def over_seq(x):
            return x.rearrange("p r (b c) -> p r b c", b=2)

        def filter_part(g, i, part, o):
            f = hy_spec[:, g, i, part, o * D:(o + 1) * D]
            return f.unsqueeze(1).unsqueeze(1).broadcast_to([P, 2, 2, D])

        def hyena_gpsimd(gp):
            s = lambda k: S["hy", k]
            for n in range(8):
                o, half, g = n // 4, n // 2 % 2, n % 2
                hy_x = hy_xs[:, n % 2]
                if n >= 1:
                    gp.wait_ge(s("step"), n)
                for i in range(2):
                    gp.wait_ge(s("dvex"), 2 * (n + 2) + i + 1)
                    gp.tensor_tensor(over_seq(hy_b[:, i]), over_seq(hy_x[:, i]), filter_part(g, i, 1, o),
                                     ALU.mult).then_inc(s("prodim"), 1)
                gp.wait_ge(s("step"), n + 1)
                if o == 1:
                    gp.wait_ge(s("inv"), 8)
                gp.tensor_tensor(hy_sd[:, half, 0, g], hy_x[:, 0], hy_x[:, 1], ALU.add).then_inc(s("sdsum"), 1)

        def hyena_vector(v):
            s = lambda k: S["hy", k]
            steps = [0]

            def step(ins):
                steps[0] += 1
                ins.then_inc(s("step"), 1)
                v.wait_ge(s("step"), steps[0])

            v.memset(zero_row[:, 0:D], 0.0)
            v.memset(zero_row[:, D:ROW], float(2 * T + SLOT_TILES * P))
            v.memset(eps_col[:, :], LN_EPS)
            v.memset(ones[:, :], 1.0).then_inc(s("dve"), 1)
            v.memset(hy_phi[HID:HID + 1, :, :], 1.0).then_inc(s("phi"), 1)
            for o in range(2):
                v.wait_ge(s("time"), 2 * o + 2)
                v.tensor_tensor(hy_phi[0:HID, o, :], hy_phi[0:HID, o, :], hy_sig[0:HID, o, :], ALU.mult).then_inc(s("phi"), 1)
            for t in range(NT):
                v.wait_ge(s("proj"), t + 1)
                b, ej = t // 4, t % 4
                v.tensor_copy(hy_v[:, ej, b, :], psum[:, 4 + t % 4, 0:D])
                v.tensor_copy(hy_gate1[:, ej, b, :], psum[:, 4 + t % 4, D:2 * D]).then_inc(s("projcopy"), 1)

            def spectrum(job, dst):
                bank = 4 * (job % 2)
                v.wait_ge(s("odd"), job + 1)
                v.tensor_tensor(dst[:, 0], psum[:, bank:bank + 2, :], hy_odd, ALU.add).then_inc(s("dvex"), 1)
                v.tensor_tensor(dst[:, 1], psum[:, bank:bank + 2, :], hy_odd, ALU.subtract).then_inc(s("dvex"), 1)

            for g in range(2):
                spectrum(g, hy_spec[:, g])
            v.wait_ge(s("dvex"), 4)
            job = 2
            v.wait_ge(s("dft"), 2)
            for o in range(2):
                for half in range(2):
                    for g in range(2):
                        n = job - 2
                        hy_x = hy_xs[:, n % 2]
                        if n >= 2:
                            v.wait_ge(s("sdsum"), n - 1)
                        spectrum(job, hy_x)
                        job += 1
                        for i in range(2):
                            v.wait_ge(s("dvex"), 2 * job - 1 + i)
                            v.tensor_tensor(over_seq(hy_a[:, i]), over_seq(hy_x[:, i]), filter_part(g, i, 0, o),
                                            ALU.mult).then_inc(s("dve"), 1)
                        v.wait_ge(s("dve"), 1 + 2 * n + 2)
                        v.wait_ge(s("prodim"), 2 * n + 2)
                        v.tensor_tensor(hy_x[:, :, 0], hy_a[:, :, 0], hy_b[:, :, 1], ALU.subtract)
                        step(v.tensor_tensor(hy_x[:, :, 1], hy_a[:, :, 1], hy_b[:, :, 0], ALU.add))
                        if o == 1:
                            v.wait_ge(s("inv"), 8)
                        v.tensor_tensor(hy_sd[:, half, 1, g], hy_x[:, 0], hy_x[:, 1], ALU.subtract).then_inc(s("sd"), 1)
                        v.wait_ge(s("sd"), n + 1)
                for n in range(8):
                    v.wait_ge(s("inv"), 8 * o + n + 1)
                    if o == 0:
                        half, ej = n // 4, n % 4
                        v.tensor_tensor(hy_v[:, ej, 2 * half:2 * half + 2, :],
                                        psum[:, 4 + n % 4, :].rearrange("p (b c) -> p b c", b=2),
                                        hy_gate1[:, ej, 2 * half:2 * half + 2, :], ALU.mult).then_inc(s("gated1"), 1)
                    else:
                        v.wait_ge(s("gate2copy"), 8)
                        b, m = n // 2, n % 2
                        z = hy_gate2[:, m, b * L:(b + 1) * L]
                        v.tensor_tensor(z, psum[:, n % 4, :], z, ALU.mult).then_inc(s("gated2"), 1)
            v.wait_ge(ld_const, ALL_CONST)

            norm_vector(v, 0, lambda v, t: add_out(v, t, s("outmm"), s("added")))

        def attention_tensor(pe, n, pairs):
            s = lambda k: S[f"at{n}", k]

            def project(what, u, b, parts):
                cols = slice(b * L, (b + 1) * L)
                if parts[0] == 0:
                    pe.wait_ge(s("w"), u * 12 + (16 * ("kqv".index(what) + 1) - 12 * b))
                    if what == "k":
                        hold(pe, s("vl"), u)
                    else:
                        pe.wait_ge(s("kl" if what == "q" else "ql"), u + 1)
                for part in parts:
                    if what == "q":
                        mm = pe.matmul(psum[:, 5, :], at_w[:, part, :], x_feat[:, part, cols], start=part == 0, stop=part == 1)
                    elif what == "k":
                        mm = pe.matmul(psum[:, 5, :], at_w[:, 2 + part, :], ctx_feat[:, part, cols],
                                       start=part == 0, stop=part == 1)
                    else:
                        kt, k = part // 2, part % 2
                        mm = pe.matmul(psum[:, 5, kt * P:(kt + 1) * P],
                                       ctx_feat[:, k, b * L + kt * P:b * L + (kt + 1) * P], at_w[:, 4 + k, :],
                                       start=k == 0, stop=k == 1)
                if parts[-1] == PARTS[what] - 1:
                    mm.then_inc(s(what), 1)

            def steps(i, span, first, last):
                for st in span:
                    m = back(st, 0, first, last)
                    if m is not None:
                        b, h, qt = m // 8, m // 4 % 2, m % 4
                        if m % 8 == 0:
                            pe.wait_ge(s("qd"), 64 * 4 * i + 64 * (b + 1))
                            pe.wait_ge(s("kd"), 64 * 4 * i + 64 * (b + 1))
                        hold(pe, s("exp"), 32 * i + (m - 1))
                        for part in range(2):
                            mm = pe.matmul(psum[:, m % 2, :], at_qd[:, b % 2, h, qt * P:(qt + 1) * P],
                                           at_kd[:, b % 2, h, part, :], start=part == 0, stop=part == 1)
                        mm.then_inc(s("s"), 1)
                    g = st // 4 - 2
                    if st % 4 < 3 and not (first and g < 0) and not (last and g >= 0):
                        h = g % 2
                        bank = 7 if h else 4
                        if st % 4 == 0:
                            pe.wait_ge(s("pl"), 32 * i + (4 * g + 4))
                            pe.wait_ge(s("vl"), 4 * i + (g // 2 + 1))
                            hold(pe, s("ot"), 8 * i + (g - 1))
                        for n8 in ((0, 1, 2), (3, 4, 5), (6, 7))[st % 4]:
                            kt, part = n8 // 2, (at_ph, at_pl)[n8 % 2]
                            mm = pe.matmul(psum[:, bank, :],
                                           at_vd[:, g // 2 % 2, kt, 2 * h:2 * h + 2, :].rearrange("p a d -> p (a d)"),
                                           part[:, h, kt, :], start=n8 == 0, stop=n8 == 7)
                        if st % 4 == 2:
                            mm.then_inc(s("av"), 1)
                    u = st // 8 - 2
                    if st % 4 == 3 and not (first and u < 0) and not (last and u >= 0):
                        half = st // 4 % 2
                        pe.wait_ge(s("ot"), 8 * i + (2 * u + 2))
                        hold(pe, s("add"), 8 * i + (2 * u + half))
                        pair = i if u >= 0 else i - 1
                        rhs = at_wout[:, pair, :] if isinstance(pair, int) else at_wout[:, bass.ds(pair, 1), :]
                        for n2 in range(2):
                            qt = 2 * half + n2
                            mm = pe.matmul(psum[:, 6, n2 * D:(n2 + 1) * D], at_ot[:, u % 2, qt * P:(qt + 1) * P], rhs,
                                           start=True, stop=True)
                        mm.then_inc(s("y"), 1)
                    if not last and st % 8 in PROJECT:
                        what, parts = PROJECT[st % 8]
                        project(what, 4 * i + (st // 8 + 1), (st // 8 + 1) % 4, parts)
                    m = back(st, 3, first, last)
                    if m is not None:
                        pe.wait_ge(s("pn"), 32 * i + (m + 1))
                        hold(pe, s("pl"), 32 * i + (m - 1))
                        for kt in range(4):
                            mm = pe.transpose(psum[:, 2 + m % 2, kt * P:(kt + 1) * P], at_p[:, m % 4, kt * P:(kt + 1) * P],
                                              ident[:, :])
                        mm.then_inc(s("turn"), 1)

            pe.wait_ge(S["ln", "feat"], ln_done(n - 1))
            pe.wait_ge(ld_ctx, 16)
            for what in "kqv":
                project(what, 0, 0, range(PARTS[what]))
            pe.wait_ge(s("wout"), 16)
            over_pairs(pe, pairs, steps)

        def attention_scalar(a, n, pairs):
            s = lambda k: S[f"at{n}", k]

            def high(what, u, slot, used):
                a.wait_ge(s(what), u + 1)
                if what == "q":
                    hold(a, s("qd"), 64 * u)
                    a.activation(at_qn[:, 0, :], psum[:, 5, :], ACT.Copy, scale=DH ** -0.5).then_inc(s("qh"), 1)
                elif what == "k":
                    hold(a, s("kd"), 64 * u)
                    a.activation(at_kn[:, 0, :], psum[:, 5, :], ACT.Copy).then_inc(s("kh"), 1)
                else:
                    hold(a, s("av"), used)
                    a.activation(at_vd[:, slot, :, 0:4:3, :], psum[:, 5, :].rearrange("p (t h d) -> p t h d", t=4, h=2),
                                 ACT.Copy).then_inc(s("vh"), 1)

            def steps(i, span, first, last):
                for st in span:
                    m = back(st, 0, first, last)
                    if m is not None:
                        a.wait_ge(s("max"), 32 * i + (m + 1))
                        hold(a, s("turn"), 32 * i + (m - 3))
                        hold(a, s("rinv"), 32 * i + (m - 15))
                        a.activation(at_p[:, m % 4, :], psum[:, m % 2, :], ACT.Exp, bias=at_negmax[:, m % 2:m % 2 + 1],
                                     accum_out=at_sum[:, m % 16:m % 16 + 1]).then_inc(s("exp"), 1)
                    m = back(st, 3, first, last)
                    if m is not None:
                        qt = m % 4
                        a.wait_ge(s("turn"), 32 * i + (m + 1))
                        hold(a, s("av"), 8 * i + (m // 4 - 1))
                        a.activation(at_ph[:, m // 4 % 2, :, qt * P:(qt + 1) * P],
                                     psum[:, 2 + m % 2, :].rearrange("p (t q) -> p t q", t=4), ACT.Copy).then_inc(s("ph"), 1)
                    if not last and st % 8 in (1, 4, 7):
                        u = st // 8 + 1
                        high({1: "k", 4: "q", 7: "v"}[st % 8], 4 * i + u, u % 2, 8 * i + 2 * (u - 1))
                    m = back(st, 11, first, last)
                    if m is not None and m % 4 == 0:
                        g = m // 4
                        h = g % 2
                        a.wait_ge(s("av"), 8 * i + (g + 1))
                        hold(a, s("ot"), 8 * i + (g - 1))
                        a.activation(at_oc[h * DH:(h + 1) * DH, :], psum[(1 - h) * DH:(2 - h) * DH, 7 if h else 4, :],
                                     ACT.Copy).then_inc(s("oc"), 1)

            if n == 1:
                a.wait_ge(S["mo", "fill"], 16)
            for what in "kqv":
                high(what, 0, 0, 0)
            over_pairs(a, pairs, steps)
            norm_scalar(a, n)

        def attention_vector(v, n, pairs):
            s = lambda k: S[f"at{n}", k]

            def low(what, u, slot):
                v.wait_ge(s(what + "h"), u + 1)
                if what == "q":
                    v.scalar_tensor_tensor(at_qn[:, 1, :], psum[:, 5, :], DH ** -0.5, at_qn[:, 0, :],
                                           ALU.mult, ALU.subtract).then_inc(s("ql"), 1)
                elif what == "k":
                    v.tensor_tensor(at_kn[:, 1, :], psum[:, 5, :], at_kn[:, 0, :], ALU.subtract).then_inc(s("kl"), 1)
                else:
                    v.tensor_tensor(at_vd[:, slot, :, 1:3, :], psum[:, 5, :].rearrange("p (t h d) -> p t h d", t=4, h=2),
                                    at_vd[:, slot, :, 0:4:3, :], ALU.subtract).then_inc(s("vl"), 1)

            def steps(i, span, first, last):
                for st in span:
                    if not last and st % 8 == 0:
                        low("v", 4 * i + st // 8, st // 8 % 2)
                    m = back(st, 0, first, last)
                    if m is not None:
                        v.wait_ge(s("s"), 32 * i + (m + 1))
                        hold(v, s("exp"), 32 * i + (m - 1))
                        v.tensor_reduce(at_negmax[:, m % 2:m % 2 + 1], psum[:, m % 2, :], AX.X, ALU.max,
                                        negate=True).then_inc(s("max"), 1)
                    if not last and st % 8 in (2, 5):
                        low({2: "k", 5: "q"}[st % 8], 4 * i + (st // 8 + 1), 0)
                    m = back(st, 1, first, last)
                    if m is not None:
                        v.wait_ge(s("exp"), 32 * i + (m + 1))
                        c = slice(m % 16, m % 16 + 1)
                        hold(v, s("pn"), 32 * i + (m - 15))
                        v.reciprocal(at_rinv[:, c], at_sum[:, c]).then_inc(s("rinv"), 1)
                    m = back(st, 4, first, last)
                    if m is not None:
                        qt = m % 4
                        v.wait_ge(s("ph"), 32 * i + (m + 1))
                        p = (slice(None), m // 4 % 2, slice(None), slice(qt * P, (qt + 1) * P))
                        v.tensor_tensor(at_pl[p], psum[:, 2 + m % 2, :].rearrange("p (t q) -> p t q", t=4), at_ph[p],
                                        ALU.subtract).then_inc(s("pl"), 1)
                    m = back(st, 12, first, last)
                    if m is not None and m % 4 == 0:
                        g = m // 4
                        rows = slice(g % 2 * DH, (g % 2 + 1) * DH)
                        v.wait_ge(s("oc"), 8 * i + (g + 1))
                        hold(v, s("y"), 8 * i + 2 * (g // 2 - 1))
                        v.tensor_tensor(at_ot[rows, g // 2 % 2, :], psum[rows, 7 if g % 2 else 4, :], at_oc[rows, :],
                                        ALU.add).then_inc(s("ot"), 1)
                    u, half = (st // 8 - 2, 0) if st % 8 == 4 else (st // 8 - 3, 1)
                    if st % 4 == 0 and not (first and u < 0) and not (last and u >= 0):
                        v.wait_ge(s("y"), 8 * i + (2 * u + half + 1))
                        t = 4 * (u % 4) + 2 * half
                        v.tensor_tensor(x_tok[:, t:t + 2, :], psum[:, 6, :].rearrange("p (t d) -> p t d", t=2),
                                        x_tok[:, t:t + 2, :], ALU.add).then_inc(s("add"), 1)

            v.wait_ge(S["ln", "turn"], ln_done(n - 1))
            v.tensor_tensor(x_tok[:, :, :], x_tok[:, :, :],
                            bias_row[:, 0 if n == 1 else 2, :].unsqueeze(1).broadcast_to([P, NT, D]),
                            ALU.add).then_inc(biased, 1)
            for what in "kq":
                low(what, 0, 0)
            v.wait_ge(biased, 1 if n == 1 else 3)
            over_pairs(v, pairs, steps)
            v.wait_ge(s("add"), 8 * pairs)
            norm_vector(v, n)

        def top2_vector(v, stage, rows, G, logit, z, e, pr, oh1, oh2, t, m):
            n = [0]

            def step(ins):
                n[0] += 1
                ins.then_inc(S[stage, "step"], 1)
                v.wait_ge(S[stage, "step"], n[0])

            r = lambda x: x[rows]
            over = lambda x: x[rows].unsqueeze(2).broadcast_to([x[rows].shape[0], G, E8])
            rank = rank8[rows].unsqueeze(1).broadcast_to([rank8[rows].shape[0], G, E8])
            m = [m[:, i, :] for i in range(m.shape[1])]
            step(v.tensor_reduce(r(m[0]), r(logit), AX.X, ALU.max))
            step(v.tensor_tensor(r(z), r(logit), over(m[0]), ALU.subtract))
            v.wait_ge(S[stage, "exp"], 1)
            step(v.tensor_reduce(r(m[1]), r(e), AX.X, ALU.add))
            step(v.reciprocal(r(m[2]), r(m[1])))
            step(v.tensor_tensor(r(pr), r(e), over(m[2]), ALU.mult))
            for k, oh in enumerate((oh1, oh2)):
                step(v.tensor_reduce(r(m[k]), r(pr), AX.X, ALU.max))
                step(v.tensor_tensor(r(t), r(pr), over(m[k]), ALU.is_equal))
                step(v.tensor_tensor(r(t), r(t), rank, ALU.mult))
                step(v.tensor_reduce(r(m[2 + k]), r(t), AX.X, ALU.max))
                step(v.tensor_tensor(r(oh), rank, over(m[2 + k]), ALU.is_equal))
                if k == 0:
                    step(v.scalar_tensor_tensor(r(pr), r(oh), -2.0, r(pr), ALU.mult, ALU.add))
            return step

        results = nc.dram_tensor("results", (2 * T + SLOT_TILES * P, D), F32).ap()
        UNROLL = 4

        def over_tiles(eng, steps):
            steps(0, range(UNROLL), True, False)
            with eng.Fori(1, SLOT_TILES // UNROLL) as i:
                steps(i, range(UNROLL), False, False)
            steps(SLOT_TILES // UNROLL, range(3), False, True)


        def tokens_sync(sp):
            s = lambda k: S["mo", k]
            for dst, name in ((mo_wg, "mo_wg"), (mo_lt8, "mo_lt8"), (mo_step128, "mo_step128"), (mo_iota, "mo_iota"),
                              (mo_number, "mo_number"), (mo_spare, "mo_spare"), (mo_before, "mo_before")):
                sp.dma_start(dst, I[name]).then_inc(s("w"), 16)
            for dst, name in ((mo_w1, "mo_w1"), (mo_b1, "mo_b1")):
                sp.dma_start(dst, I[name]).then_inc(s("wlate"), 16)
            sp.wait_ge(S["ln", "norm"], NT + 4)
            for dst, name in ((mo_b2, "mo_b2"), (mo_w2, "mo_w2")):
                sp.dma_start(dst, I[name]).then_inc(s("wlate"), 16)
            sp.wait_ge(s("scatter"), 2 * NT * 16)
            for q in range(2):
                sp.dma_start(mo_x[:, q, :], sorted_x[q * P:(q + 1) * P, :]).then_inc(s(f"x{q}"), 16)
            with sp.Fori(1, SLOT_TILES // 2) as m:
                for q in range(2):
                    sp.wait_ge(s("dest"), 2 * m + (q - 1))
                    sp.dma_start(mo_x[:, q, :], sorted_x[bass.ds(m * (2 * P) + q * P, P), :]).then_inc(s(f"x{q}"), 16)
            for q in range(2):
                sp.wait_ge(s(f"ys{q}"), 8 * SLOT_TILES)
            for g in range(NT // 4):
                if g >= 2:
                    sp.wait_ge(s("mix"), 8 * (g - 1))
                for k in range(2):
                    row = k * T + g * 4 * P
                    sp.dma_start(mo_yg[:, k, 4 * (g % 2):4 * (g % 2) + 4, :],
                                 results[row:row + 4 * P, :].rearrange("(t p) d -> p t d", p=P)).then_inc(s(f"g{g % 2}"), 16)

        def tokens_gpsimd(gp):
            s = lambda k: S["mo", k]
            gp.wait_ge(s("fill"), 16)
            for k in range(2):
                gp.wait_ge(s("place"), k + 1)
                for t in range(NT):
                    gp.indirect_dma_start(out=sorted_x, out_offset=bass.IndirectOffsetOnAxis(mo_posi[:, k, t:t + 1], 0),
                                          in_=x_wide[:, t, 0:ROW], in_offset=None).then_inc(s("scatter"), 16)
            for m in range(SLOT_TILES):
                gp.wait_ge(s("y2"), m + 1)
                gp.indirect_dma_start(out=results, out_offset=bass.IndirectOffsetOnAxis(mo_dest[:, m:m + 1], 0),
                                      in_=mo_y[:, m % 2, :], in_offset=None).then_inc(s(f"ys{m % 2}"), 16)

        def tokens_tensor(pe):
            s = lambda k: S["mo", k]
            pe.wait_ge(s("w"), 7 * 16)
            for g in range(NT // 4 + 1):
                if g < NT // 4:
                    norm_tensor(pe, 1, g)
                if g >= 1:
                    pe.wait_ge(S["ln", "feat"], NT + 4 * g)
                    for t in range(4 * g - 4, 4 * g):
                        for k in range(DK):
                            mm = pe.matmul(psum[:, 0, t * E8:(t + 1) * E8], x_feat[:, k, t * P:(t + 1) * P], mo_wg[:, k, :],
                                           start=k == 0, stop=k == DK - 1)
            mm.then_inc(s("rl"), 1)
            pe.wait_ge(s("both"), 2)
            pad = mo_both_pad.rearrange("p t e -> p (t e)")
            pe.matmul(psum[:, 1, 0:P], mo_before, pad[:, P:2 * P], start=True, stop=False)
            for d in range(1, NT):
                mm = pe.matmul(psum[:, 1, 0:P], ones[:, :], pad[:, P - d * E8:2 * P - d * E8],
                               start=False, stop=d == NT - 1)
            mm.then_inc(s("rank"), 1)
            pe.matmul(psum[:, 2, 0:E8], ones[:, :], mo_mine, start=True, stop=True).then_inc(s("rank"), 1)
            pe.wait_ge(s("place"), 1)
            pe.wait_ge(s("wlate"), 4 * 16)
            def steps(i, span, first, last):
                for step in span:
                    m = back(step, 0, first, last)
                    if m is not None:
                        pe.wait_ge(s(f"x{m % 2}"), 8 * UNROLL * i + (8 * (m - m % 2) + 16))
                        hold(pe, s("xt"), UNROLL * i + (m - 1))
                        for k in range(DK):
                            mm = pe.transpose(psum[:, m % 2, k * P:(k + 1) * P], mo_x[:, m % 2, k * P:(k + 1) * P], ident[:, :])
                        mm.then_inc(s("xturn"), 1)
                    m = back(step, 1, first, last)
                    if m is not None:
                        e = pe.value_load(mo_tei[0:1, bass.ds(UNROLL * i + m, 1)], min_val=0, max_val=E8 - 1)
                        pe.wait_ge(s("xt"), UNROLL * i + (m + 1))
                        hold(pe, s("hb"), UNROLL * i + (m - 1))
                        for k in range(DK):
                            mm = pe.matmul(psum[:, 2 + m % 2, :], mo_xt[:, m % 2, k * P:(k + 1) * P],
                                           mo_w1[:, bass.ds(e, 1), k * FF0:(k + 1) * FF0], start=k == 0, stop=k == DK - 1)
                        mm.then_inc(s("h"), 1)
                    m = back(step, 2, first, last)
                    if m is not None:
                        pe.wait_ge(s("hb"), UNROLL * i + (m + 1))
                        hold(pe, s("relu"), UNROLL * i + (m - 1))
                        for ht in range(4):
                            mm = pe.transpose(psum[:, 4 + m % 2, ht * P:(ht + 1) * P], mo_h[:, m % 2, ht * P:(ht + 1) * P],
                                              ident[:, :])
                        mm.then_inc(s("hturn"), 1)
                    m = back(step, 3, first, last)
                    if m is not None:
                        e = pe.value_load(mo_tei[0:1, bass.ds(UNROLL * i + m, 1)], min_val=0, max_val=E8 - 1)
                        pe.wait_ge(s("relu"), UNROLL * i + (m + 1))
                        hold(pe, s("y2"), UNROLL * i + (m - 1))
                        for ht in range(4):
                            mm = pe.matmul(psum[:, 6 + m % 2, 0:D], mo_ht[:, m % 2, ht * P:(ht + 1) * P],
                                           mo_w2[:, bass.ds(e, 1), ht * D:(ht + 1) * D], start=ht == 0, stop=ht == 3)
                        mm.then_inc(s("y"), 1)

            over_tiles(pe, steps)
            for g in range(4):
                norm_tensor(pe, 2, g)

        def tokens_scalar(a):
            s = lambda k: S["mo", k]
            a.wait_ge(s("step"), 2)
            a.activation(mo_e, mo_z, ACT.Exp).then_inc(s("exp"), 1)
            def steps(i, span, first, last):
                for step in span:
                    m = back(step, 0, first, last)
                    if m is not None:
                        a.wait_ge(s("xturn"), UNROLL * i + (m + 1))
                        hold(a, s("h"), UNROLL * i + (m - 1))
                        a.activation(mo_xt[:, m % 2, :], psum[:, m % 2, 0:D], ACT.Copy).then_inc(s("xt"), 1)
                    m = back(step, 2, first, last)
                    if m is not None:
                        a.wait_ge(s("hturn"), UNROLL * i + (m + 1))
                        hold(a, s("y"), UNROLL * i + (m - 1))
                        a.activation(mo_ht[:, m % 2, :], psum[:, 4 + m % 2, :], ACT.Relu).then_inc(s("relu"), 1)

            over_tiles(a, steps)
            norm_scalar(a, 2)

        def tokens_vector(v):
            s = lambda k: S["mo", k]
            v.wait_ge(s("rl"), 1)
            v.memset(mo_both_pad[:, 0:NT, :], 0.0)
            v.tensor_copy(mo_logit, psum[:, 0, 0:NT * E8].rearrange("p (t e) -> p t e", e=E8)).then_inc(s("both"), 1)
            v.wait_ge(s("both"), 1)
            step = top2_vector(v, "mo", slice(0, P), NT, mo_logit, mo_z, mo_e, mo_pr, mo_oh1, mo_oh2, mo_t, mo_m)
            step(v.tensor_tensor(mo_both, mo_oh1, mo_oh2, ALU.add))
            v.tensor_reduce(mo_mine, mo_both.rearrange("p t e -> p e t"), AX.X, ALU.add).then_inc(s("both"), 1)
            step(v.tensor_tensor(mo_m[:, 4, :], mo_m[:, 0, :], mo_m[:, 1, :], ALU.add))
            step(v.reciprocal(mo_m[:, 5, :], mo_m[:, 4, :]))
            for k in range(2):
                step(v.tensor_tensor(mo_s[:, k, :], mo_m[:, k, :], mo_m[:, 5, :], ALU.mult))
            v.wait_ge(s("rank"), 2)
            step(v.tensor_tensor(mo_cmp, psum[:, 2, 0:E8].unsqueeze(2).broadcast_to([P, E8, 16]),
                                 mo_step128.unsqueeze(1).broadcast_to([P, E8, 16]), ALU.is_gt))
            step(v.tensor_reduce(mo_tiles, mo_cmp, AX.X, ALU.add))
            step(v.tensor_tensor(mo_ltt, mo_lt8, mo_tiles.unsqueeze(1).broadcast_to([P, E8, E8]), ALU.mult))
            step(v.tensor_reduce(mo_base, mo_ltt, AX.X, ALU.add))
            step(v.tensor_tensor(mo_end8, mo_base, mo_tiles, ALU.add))
            step(v.tensor_scalar(mo_base128, mo_base, float(P), None, ALU.mult))
            step(v.tensor_tensor(mo_geq, mo_iota.unsqueeze(2).broadcast_to([P, SLOT_TILES, E8]),
                                 mo_end8.unsqueeze(1).broadcast_to([P, SLOT_TILES, E8]), ALU.is_ge))
            step(v.tensor_reduce(mo_te, mo_geq, AX.X, ALU.add))
            v.tensor_scalar(mo_tei[:, :], mo_te, float(E8 - 1), None, ALU.min)
            step(v.tensor_tensor(mo_pos, psum[:, 1, 0:P].rearrange("p (t e) -> p t e", e=E8),
                                 mo_base128.unsqueeze(1).broadcast_to([P, NT, E8]), ALU.add))
            for k, oh in enumerate((mo_oh1, mo_oh2)):
                step(v.tensor_tensor(oh, oh, mo_pos, ALU.mult))
                step(v.tensor_reduce(mo_posf[:, k, :], oh, AX.X, ALU.add))
            v.tensor_copy(x_wide[:, :, D], mo_number)
            v.tensor_copy(mo_posi[:, :, :], mo_posf).then_inc(s("place"), 1)
            v.wait_ge(s("scatter"), NT * 16)
            v.tensor_scalar(x_wide[:, :, D], mo_number, float(T), None, ALU.add).then_inc(s("place"), 1)
            def steps(i, span, first, last):
                for step in span:
                    m = back(step, 1, first, last)
                    if m is not None:
                        v.wait_ge(s("xturn"), UNROLL * i + (m + 1))
                        at = bass.ds(UNROLL * i + m, 1)
                        v.tensor_tensor(mo_dest[:, at], mo_x[:, m % 2, D:ROW], mo_spare[:, at], ALU.min).then_inc(s("dest"), 1)
                    m = back(step, 1, first, last)
                    if m is not None:
                        e = v.value_load(mo_tei[0:1, bass.ds(UNROLL * i + m, 1)], min_val=0, max_val=E8 - 1)
                        v.wait_ge(s("h"), UNROLL * i + (m + 1))
                        hold(v, s("hturn"), UNROLL * i + (m - 1))
                        v.tensor_tensor(mo_h[:, m % 2, :], psum[:, 2 + m % 2, :],
                                        mo_b1[:, bass.ds(e, 1), :].rearrange("p o n -> p (o n)"), ALU.add).then_inc(s("hb"), 1)
                    m = back(step, 3, first, last)
                    if m is not None:
                        e = v.value_load(mo_tei[0:1, bass.ds(UNROLL * i + m, 1)], min_val=0, max_val=E8 - 1)
                        v.wait_ge(s("y"), UNROLL * i + (m + 1))
                        hold(v, s(f"ys{m % 2}"), 8 * UNROLL * i + 8 * (m - m % 2))
                        v.tensor_tensor(mo_y[:, m % 2, :], psum[:, 6 + m % 2, 0:D],
                                        mo_b2[:, bass.ds(e, 1), :].rearrange("p o n -> p (o n)"), ALU.add).then_inc(s("y2"), 1)

            over_tiles(v, steps)
            for t in range(NT):
                for k in range(2):
                    v.wait_ge(s(f"g{t // 4 % 2}"), 32 * (t // 8) + 32)
                    if k:
                        v.wait_ge(s("mix"), 2 * t + 1)
                    v.scalar_tensor_tensor(x_tok[:, t, :], mo_yg[:, k, t % 8, :], mo_s[:, k, t:t + 1], x_tok[:, t, :],
                                           ALU.mult, ALU.add).then_inc(s("mix"), 1)

            def added(v, t):
                v.wait_ge(s("mix"), 2 * t + 2)

            norm_vector(v, 2, added)

        COMBOS = [(m, b) for m in range(DK) for b in range(B)]

        def flow_sync(sp):
            s = lambda k: S["fl", k]
            sp.wait_ge(S["ln", "feat"], ln_done(2))
            sp.dma_start(fl_w, I["fl_w"]).then_inc(s("w"), 16)
            sp.dma_start(fl_bias, I["fl_bias"]).then_inc(s("w"), 16)
            sp.dma_start(fl_spread, I["fl_spread"]).then_inc(s("w"), 16)

        def flow_tensor(pe):
            s = lambda k: S["fl", k]
            pe.wait_ge(s("w"), 48)
            for j, (m, b) in enumerate(COMBOS):
                for n, name in enumerate(("q", "k", "v")):
                    if j >= 2:
                        pe.wait_ge(s("sig"), 3 * (j - 2) + n + 1)
                    for k in range(DK):
                        mm = pe.matmul(psum[:, 2 * n + j % 2, :], fl_w[:, n, k, m * P:(m + 1) * P],
                                       x_feat[:, k, b * L:(b + 1) * L], start=k == 0, stop=k == DK - 1)
                    mm.then_inc(s(name), 1)
            pe.wait_ge(s("sig"), 24)
            for j, (m, b) in enumerate(COMBOS):
                pe.wait_ge(s("vec"), 2 * j + 2)
                cols = slice(b * L, (b + 1) * L)
                pe.matmul(psum[:, 0, :], fl_mask[:, j, 0, :], fl_qe[:, m, cols], start=j == 0, stop=False)
                mm = pe.matmul(psum[:, 0, :], fl_mask[:, j, 1, :], fl_ke[:, m, cols], start=False, stop=j == 7)
            mm.then_inc(s("den"), 1)
            pe.wait_ge(s("recip"), 1)
            for j in range(8):
                if j >= 2:
                    pe.wait_ge(s("recip"), 1 + 2 * j - 2)
                for n in range(2):
                    pe.matmul(psum[:, 2 * n + j % 2, :], fl_spread[:, 2 * j + n, :], fl_rec, start=True,
                              stop=True).then_inc(s("den"), 1)
            for j, (m, b) in enumerate(COMBOS):
                pe.wait_ge(s("col"), j + 1)
                if j >= 2:
                    pe.wait_ge(s("alloc"), j - 1)
                    pe.wait_ge(s("clip"), j - 1)
                cols = slice(b * L, (b + 1) * L)
                pe.matmul(psum[:, 4 + j % 2, :], fl_mask[:, j, 2, :], fl_qe[:, m, cols], start=True, stop=True).then_inc(s("con"), 1)
                pe.matmul(psum[:, 6 + j % 2, :], fl_mask[:, j, 3, :], fl_ke[:, m, cols], start=True, stop=True).then_inc(s("con"), 1)
            pe.wait_ge(s("recip"), 17)
            for j in range(9):
                if j < 8:
                    m, b = COMBOS[j]
                    pe.wait_ge(s("comp"), j + 1)
                    if j >= 1:
                        pe.wait_ge(s("kcopy"), j)
                        pe.wait_ge(s("vcopy"), j)
                    for n, src in enumerate((fl_k, fl_v)):
                        for tt in range(4):
                            mm = pe.transpose(psum[:, n, tt * P:(tt + 1) * P],
                                              src[:, m, b * L + tt * P:b * L + (tt + 1) * P], ident[:, :])
                        mm.then_inc(s("turn"), 1)
                if j >= 1:
                    i = j - 1
                    m, b = COMBOS[i]
                    pe.wait_ge(s("kcopy"), i + 1)
                    pe.wait_ge(s("vcopy"), i + 1)
                    if i >= 1:
                        pe.wait_ge(s("kvm"), i)
                    for tt in range(4):
                        mm = pe.matmul(psum[:, 2, 0:P], fl_ktok[:, i % 2, tt * P:(tt + 1) * P],
                                       fl_vtok[:, i % 2, tt * P:(tt + 1) * P], start=tt == 0, stop=tt == 3)
                    mm.then_inc(s("kv"), 1)
                    pe.wait_ge(s("kvm"), i + 1)
                    if i >= 1:
                        pe.wait_ge(s("gated"), i)
                    pe.matmul(psum[:, 3, :], fl_kv[:, i % 2, :], fl_q[:, m, b * L:(b + 1) * L],
                              start=True, stop=True).then_inc(s("out"), 1)
            pe.wait_ge(s("gated"), 8)
            for g in range(4):
                project_out(pe, g, fl_v, fl_w[:, 3], s("outmm"), s("added"))
                if g >= 1:
                    norm_tensor(pe, 3, g - 1)
            norm_tensor(pe, 3, 3)

        def flow_scalar(a):
            s = lambda k: S["fl", k]
            a.wait_ge(s("w"), 48)
            for j, (m, b) in enumerate(COMBOS):
                cols = slice(b * L, (b + 1) * L)
                a.wait_ge(s("q"), j + 1)
                a.activation(fl_q[:, m, cols], psum[:, j % 2, :], ACT.Sigmoid, bias=fl_bias[:, 0, m:m + 1],
                             accum_out=fl_sum[:, j, 1:2]).then_inc(s("sig"), 1)
                a.wait_ge(s("k"), j + 1)
                a.activation(fl_k[:, m, cols], psum[:, 2 + j % 2, :], ACT.Sigmoid, bias=fl_bias[:, 1, m:m + 1],
                             accum_out=fl_sum[:, j, 0:1]).then_inc(s("sig"), 1)
                a.wait_ge(s("v"), j + 1)
                a.activation(fl_v[:, m, cols], psum[:, 4 + j % 2, :], ACT.Identity,
                             bias=fl_bias[:, 2, m:m + 1]).then_inc(s("sig"), 1)
            for j, (m, b) in enumerate(COMBOS):
                cols = slice(b * L, (b + 1) * L)
                a.wait_ge(s("con"), 2 * j + 1)
                a.activation(fl_alloc[:, m, cols], psum[:, 4 + j % 2, :], ACT.Sigmoid).then_inc(s("alloc"), 1)
            for j, (m, b) in enumerate(COMBOS):
                cols = slice(b * L, (b + 1) * L)
                a.wait_ge(s("max"), j + 1)
                a.activation(fl_ke[:, m, cols], fl_ke[:, m, cols], ACT.Exp, bias=fl_col[:, j, 0:1],
                             accum_out=fl_col[:, j, 1:2]).then_inc(s("smx"), 1)
            for j in range(8):
                a.wait_ge(s("turn"), 2 * j + 1)
                if j >= 2:
                    a.wait_ge(s("kv"), j - 1)
                a.activation(fl_ktok[:, j % 2, :], psum[:, 0, :], ACT.Copy).then_inc(s("kcopy"), 1)
            norm_scalar(a, 3)

        def flow_vector(v):
            s = lambda k: S["fl", k]
            v.wait_ge(S["ln", "turn"], ln_done(2))
            v.tensor_tensor(x_tok[:, :, :], x_tok[:, :, :], bias_row[:, 1, :].unsqueeze(1).broadcast_to([P, NT, D]),
                            ALU.add).then_inc(biased, 1)
            for j, (m, b) in enumerate(COMBOS):
                cols = slice(b * L, (b + 1) * L)
                v.wait_ge(s("sig"), 3 * j + 3)
                if j == 0:
                    v.memset(fl_mask[:, :, 0:2, :], 0.0).then_inc(s("step"), 1)
                v.tensor_scalar(fl_sume[:, j, 0:2], fl_sum[:, j, 0:2], FLOW_EPS, None, ALU.add).then_inc(s("step"), 1)
                v.tensor_scalar(fl_qe[:, m, cols], fl_q[:, m, cols], FLOW_EPS, None, ALU.add)
                v.tensor_scalar(fl_ke[:, m, cols], fl_k[:, m, cols], FLOW_EPS, None, ALU.add)
                v.wait_ge(s("step"), j + 2)
                for n in range(2):
                    row = 8 * (2 * j + n)
                    v.tensor_scalar(fl_mask[:, j, n, row:row + 8], head_mask[:, 0:P:16], fl_sume[:, j, n:n + 1], None,
                                    ALU.mult).then_inc(s("vec"), 1)
            v.wait_ge(s("den"), 1)
            v.reciprocal(fl_rec, psum[:, 0, :]).then_inc(s("recip"), 1)
            for j, (m, b) in enumerate(COMBOS):
                cols = slice(b * L, (b + 1) * L)
                v.wait_ge(s("den"), 2 * j + 2)
                v.tensor_tensor_reduce(fl_q[:, m, cols], fl_q[:, m, cols], psum[:, j % 2, :], 1.0, 0.0, ALU.mult, ALU.add,
                                       fl_sum[:, j, 3:4]).then_inc(s("recip"), 1)
                v.wait_ge(s("den"), 2 * j + 3)
                v.tensor_tensor_reduce(fl_clip[:, j % 2, :], fl_k[:, m, cols], psum[:, 2 + j % 2, :], 1.0, 0.0, ALU.mult, ALU.add,
                                       fl_sum[:, j, 2:3]).then_inc(s("recip"), 1)
                v.wait_ge(s("recip"), 2 * j + 3)
                v.tensor_scalar(fl_sume[:, j, 2:4], fl_sum[:, j, 2:4], FLOW_EPS, None, ALU.add).then_inc(s("step"), 1)
                v.wait_ge(s("step"), 9 + j + 1)
                v.tensor_scalar(fl_mask[:, j, 2, :], head_mask[:, :], fl_sume[:, j, 2:3], None, ALU.mult)
                v.tensor_scalar(fl_mask[:, j, 3, :], head_mask[:, :], fl_sume[:, j, 3:4], None, ALU.mult).then_inc(s("col"), 1)
            for j, (m, b) in enumerate(COMBOS):
                cols = slice(b * L, (b + 1) * L)
                v.wait_ge(s("con"), 2 * j + 2)
                v.tensor_scalar(fl_ke[:, m, cols], psum[:, 6 + j % 2, :], 1.0, -1.0, ALU.min, ALU.max).then_inc(s("clip"), 1)
                v.wait_ge(s("clip"), j + 1)
                v.tensor_reduce(fl_col[:, j, 0:1], fl_ke[:, m, cols], AX.X, ALU.max, negate=True).then_inc(s("max"), 1)
            for j, (m, b) in enumerate(COMBOS):
                cols = slice(b * L, (b + 1) * L)
                v.wait_ge(s("smx"), j + 1)
                v.reciprocal(fl_col[:, j, 2:3], fl_col[:, j, 1:2]).then_inc(s("rsum"), 1)
                v.wait_ge(s("rsum"), 2 * j + 1)
                v.tensor_scalar(fl_col[:, j, 3:4], fl_col[:, j, 2:3], float(L), None, ALU.mult).then_inc(s("rsum"), 1)
                v.wait_ge(s("rsum"), 2 * j + 2)
                v.scalar_tensor_tensor(fl_v[:, m, cols], fl_ke[:, m, cols], fl_col[:, j, 3:4], fl_v[:, m, cols],
                                       ALU.mult, ALU.mult).then_inc(s("comp"), 1)
            for j in range(9):
                if j < 8:
                    v.wait_ge(s("turn"), 2 * j + 2)
                    if j >= 2:
                        v.wait_ge(s("kv"), j - 1)
                    v.tensor_copy(fl_vtok[:, j % 2, :], psum[:, 1, :]).then_inc(s("vcopy"), 1)
                if j >= 1:
                    i = j - 1
                    m, b = COMBOS[i]
                    cols = slice(b * L, (b + 1) * L)
                    v.wait_ge(s("kv"), i + 1)
                    if i >= 2:
                        v.wait_ge(s("out"), i - 1)
                    v.tensor_tensor(fl_kv[:, i % 2, :], psum[:, 2, 0:P], head_mask[:, :], ALU.mult).then_inc(s("kvm"), 1)
                    v.wait_ge(s("out"), i + 1)
                    v.wait_ge(s("alloc"), i + 1)
                    v.tensor_tensor(fl_v[:, m, cols], psum[:, 3, :], fl_alloc[:, m, cols], ALU.mult).then_inc(s("gated"), 1)
            v.wait_ge(biased, 2)

            norm_vector(v, 3, lambda v, t: add_out(v, t, s("outmm"), s("added")))

        def sequence_sync(sp):
            s = lambda k: S["se", k]
            sp.wait_ge(S["ln", "feat"], ln_done(3))
            sp.wait_ge(s("pick"), 1)

            for b in range(B):
                if b >= 2:
                    sp.wait_ge(s("bias"), 2 * b - 1)
                for m in range(2):
                    if b >= 1:
                        sp.wait_ge(s(f"w{m}"), 16 * b)
                        sp.wait_ge(s(f"u{m}"), 16 * b)
                        sp.wait_ge(s("gelu"), 16 * b - 8 + 8 * m)
                    if b >= 2:
                        sp.wait_ge(s("y"), 8 * b - 12 + 4 * m)
                    e = sp.value_load(se_picki[0:1, bass.ds(2 * b + m, 1)], min_val=0, max_val=E8 - 1)
                    sp.dma_start(se_w1[:, m], I["se_w1"][bass.ds(e, 1)].rearrange("o p n -> (o p) n")).then_inc(s(f"w{m}"), 16)
                    sp.dma_start(se_w2[:, b % 2, m], I["se_w2"][bass.ds(e, 1)].rearrange("o p n -> (o p) n")).then_inc(s(f"u{m}"), 16)

        def sequence_tensor(pe):
            s = lambda k: S["se", k]
            pe.wait_ge(S["ln", "feat"], ln_done(4))
            pe.wait_ge(s("mean"), B + 1)
            for b in range(B):
                for k in range(DK):
                    mm = pe.matmul(psum[0:1, 0, b * E8:(b + 1) * E8], se_mean[:, k, b:b + 1], se_wr[:, k, :],
                                   start=k == 0, stop=k == DK - 1)
            mm.then_inc(s("rl"), 1)
            pe.wait_ge(s("pick"), 2)
            pe.matmul(psum[:, 1, 0:2 * B], ones[0:1, :], se_cw[0:1].rearrange("p b s -> p (b s)"),
                      start=True, stop=True).then_inc(s("cwmm"), 1)
            pe.wait_ge(s("bias"), 1)
            for b in range(B):
                par = b % 2
                for step in range(3):
                    if step < 2:
                        pe.wait_ge(s("lo"), 3 * b + 2 + step)
                        for ft in range(8):
                            if b + step + ft // 4 >= 1:
                                pe.wait_ge(s("gelu"), 16 * b + 8 * step + ft - 3)
                            for k in range(DK):
                                for wp, xp in ((0, 0), (0, 1), (1, 0)):
                                    mm = pe.matmul(psum[:, ft % 4, :], se_ws[:, step, wp, k * FF1 + ft * P:k * FF1 + (ft + 1) * P],
                                                   se_xs[:, par, xp, k, :], start=k + wp + xp == 0, stop=k * wp == 1)
                            mm.then_inc(s("h"), 1)
                    if step >= 1:
                        m = step - 1
                        pe.wait_ge(s("gelu"), 16 * b + 8 * m + 8)
                        pe.wait_ge(s(f"u{m}"), 16 * b + 16)
                        for tt in range(4):
                            if b + m >= 1:
                                pe.wait_ge(s("add"), 12 * b + (4 if m else -4) + tt + 1)
                            for ft in range(8):
                                mm = pe.matmul(psum[:, 4 + tt, 0:D], se_h[:, m, ft, tt * P:(tt + 1) * P],
                                               se_w2[:, par, m, ft * D:(ft + 1) * D], start=ft == 0, stop=ft == 7)
                            mm.then_inc(s("y"), 1)

        def sequence_scalar(a):
            s = lambda k: S["se", k]
            a.wait_ge(s("step"), 2)
            a.activation(se_e[0:1], se_z[0:1], ACT.Exp).then_inc(s("exp"), 1)
            a.wait_ge(s("pick"), 1)
            a.activation(se_m[0:1, 5, :], se_m[0:1, 4, :], ACT.Exp).then_inc(s("exp"), 1)

            def root(b, n):
                a.wait_ge(S["ln", "aggr"], NT * 5 + 8 * b + 4 * (n - 4))
                a.activation(ln_std[:, 4 * b:4 * b + 4], ln_mv[:, 4 * b:4 * b + 4, 1], ACT.Sqrt,
                             bias=eps_col[:, 0:1]).then_inc(S["ln", "sqrt"], 1)

            def high(what, b):
                if what == "x":
                    a.activation(se_xs[:, b % 2, 0], x_feat[:, :, b * L:(b + 1) * L], ACT.Copy).then_inc(s("hi"), 1)
                else:
                    a.wait_ge(s(f"w{what}"), 16 * b + 16)
                    a.activation(se_ws[:, what, 0, :], se_w1[:, what, 0:DK * FF1], ACT.Copy).then_inc(s("hi"), 1)

            for what in ("x", 0, 1):
                high(what, 0)
            for b in range(B):
                for m in range(2):
                    for ft in range(8):
                        a.wait_ge(s("h"), 16 * b + 8 * m + ft + 1)
                        if b and ft == 0:
                            a.wait_ge(s("y"), 8 * b + 4 * m - 4)
                        b1 = se_w1[:, m, DK * FF1 + ft:DK * FF1 + ft + 1]
                        a.activation(se_h[:, m, ft, :], psum[:, ft % 4, :], ACT.Gelu, bias=b1).then_inc(s("gelu"), 1)
                        if b and m == 0 and ft in (3, 6):
                            root(b - 1, 5 if ft == 3 else 6)
                        if b < B - 1 and m == 1 and ft in (1, 5):
                            high("x" if ft == 1 else 0, b + 1)
                if b < B - 1:
                    high(1, b + 1)
            for n in (5, 6):
                root(B - 1, n)

        def sequence_vector(v):
            s = lambda k: S["se", k]
            v.wait_ge(S["at4", "qd"], 64 * 9)
            v.wait_ge(S["at4", "kd"], 64 * 9)
            for b in range(B):
                v.wait_ge(S["ln", "feat"], NT * 4 + 4 * b + 4)
                v.tensor_reduce(se_t4[:, :, b], x_feat[:, :, b * L:(b + 1) * L], AX.X, ALU.add).then_inc(s("mean"), 1)
            v.wait_ge(s("mean"), B)
            v.tensor_scalar(se_mean, se_t4, 1.0 / L, None, ALU.mult).then_inc(s("mean"), 1)
            v.wait_ge(s("rl"), 1)
            one = slice(0, 1)
            v.tensor_tensor(se_logit[one], psum[0:1, 0, 0:B * E8].rearrange("p (b e) -> p b e", e=E8),
                            se_br[one].unsqueeze(1).broadcast_to([1, B, E8]), ALU.add).then_inc(s("mean"), 1)
            v.wait_ge(s("mean"), B + 2)
            step = top2_vector(v, "se", one, B, se_logit, se_z, se_e, se_pr, se_oh1, se_oh2, se_t, se_m)
            step(v.tensor_scalar(se_pick[one, :, 0], se_m[one, 2, :], -1.0, float(E8), ALU.mult, ALU.add))
            step(v.tensor_scalar(se_pick[one, :, 1], se_m[one, 3, :], -1.0, float(E8), ALU.mult, ALU.add))
            step(v.tensor_tensor(se_m[one, 4, :], se_m[one, 1, :], se_m[one, 0, :], ALU.subtract))
            v.tensor_copy(se_picki[0:1, :], se_pick[one].rearrange("p b s -> p (b s)")).then_inc(s("pick"), 1)
            v.wait_ge(s("exp"), 2)
            step(v.tensor_scalar(se_m[one, 6, :], se_m[one, 5, :], 1.0, None, ALU.add))
            step(v.reciprocal(se_cw[one, :, 0], se_m[one, 6, :]))
            v.tensor_tensor(se_cw[one, :, 1], se_cw[one, :, 0], se_m[one, 5, :], ALU.mult).then_inc(s("pick"), 1)
            v.wait_ge(s("cwmm"), 1)
            v.tensor_copy(se_cwb, psum[:, 1, 0:2 * B].rearrange("p (b s) -> p b s", s=2)).then_inc(s("bias"), 1)

            def low(what, b):
                v.wait_ge(s("hi"), 3 * b + {"x": 1, 0: 2, 1: 3}[what])
                if what == "x":
                    v.tensor_tensor(se_xs[:, b % 2, 1], x_feat[:, :, b * L:(b + 1) * L], se_xs[:, b % 2, 0],
                                    ALU.subtract).then_inc(s("lo"), 1)
                else:
                    v.tensor_tensor(se_ws[:, what, 1, :], se_w1[:, what, 0:DK * FF1], se_ws[:, what, 0, :],
                                    ALU.subtract).then_inc(s("lo"), 1)

            low("x", 0)
            v.tensor_tensor(se_keep, x_tok[:, :, :], gb_row[:, 1, :].unsqueeze(1).broadcast_to([P, NT, D]),
                            ALU.add).then_inc(s("mean"), 1)
            v.wait_ge(s("bias"), 1)
            v.wait_ge(s("mean"), B + 3)
            for what in range(2):
                low(what, 0)
            for b in range(B):
                par = b % 2
                for m in range(2):
                    v.wait_ge(s(f"u{m}"), 16 * b + 16)
                v.tensor_copy(se_cwc, se_cwb[:, b, :]).then_inc(s("cwc"), 1)
                v.wait_ge(s("cwc"), 3 * b + 1)
                v.tensor_scalar(se_bias[:, 0, :], se_w2[:, par, 0, 8 * D:9 * D], se_cwc[:, 0:1], None, ALU.mult).then_inc(s("cwc"), 1)
                v.wait_ge(s("cwc"), 3 * b + 2)
                v.scalar_tensor_tensor(se_bias[:, 1, :], se_w2[:, par, 1, 8 * D:9 * D], se_cwc[:, 1:2], se_bias[:, 0, :],
                                       ALU.mult, ALU.add).then_inc(s("cwc"), 1)
                v.wait_ge(s("cwc"), 3 * b + 3)
                v.sem_inc(s("bias"), 2)
                for tt in range(4):
                    v.tensor_tensor(x_tok[:, 4 * b + tt, :], x_tok[:, 4 * b + tt, :], se_bias[:, 1, :],
                                    ALU.add).then_inc(s("add"), 1)
                for m in range(2):
                    if b < B - 1:
                        for what in (("x", 0), (1,))[m]:
                            low(what, b + 1)
                    for tt in range(4):
                        x = x_tok[:, 4 * b + tt, :]
                        v.wait_ge(s("y"), 8 * b + 4 * m + tt + 1)
                        v.wait_ge(s("add"), 12 * b + 4 * m + tt + 1)
                        v.scalar_tensor_tensor(x, psum[:, 4 + tt, 0:D], se_cwc[:, m:m + 1], x,
                                               ALU.mult, ALU.add).then_inc(s("add"), 1)
                v.wait_ge(s("add"), 12 * b + 12)
                c0, r0 = NT * 5 + 8 * b, 4 * 5 + 2 * b
                norm_stats(v, 4 * b, c0)
                norm_apply(v, 4 * b, r0)
                for j in range(4):
                    x = x_tok[:, 4 * b + j, :]
                    v.wait_ge(S["ln", "norm"], c0 + j + 1)
                    v.tensor_tensor(x, x, gb_row[:, 0, :], ALU.mult).then_inc(s("affine"), 1)
                for j in range(4):
                    x = x_tok[:, 4 * b + j, :]
                    v.wait_ge(s("affine"), 8 * b + j + 1)
                    v.tensor_tensor(x, x, se_keep[:, 4 * b + j, :], ALU.add).then_inc(s("affine"), 1)
                v.wait_ge(s("affine"), 8 * b + 8)
                norm_stats(v, 4 * b, c0 + 4)
                norm_apply(v, 4 * b, r0 + 1)

        @block.sync
        def _(sp):
            sync_hyena(sp)
            attention_sync(sp, 1, 8)
            tokens_sync(sp)
            flow_sync(sp)
            attention_sync(sp, 4, 2)
            sequence_sync(sp)
            for b in range(B):
                sp.wait_ge(S["ln", "norm"], NT * 5 + 8 * b + 8)
                for e in range(2):
                    sp.dma_start(out[b].rearrange("(j p e) d -> e p j d", j=2, e=2)[e],
                                 x_tok[:, 4 * b + 2 * e:4 * b + 2 * e + 2, :]).then_inc(store, 16)
            sp.wait_ge(store, 16 * 2 * B)

        @block.tensor
        def _(pe):
            hyena_tensor(pe)
            attention_tensor(pe, 1, 8)
            tokens_tensor(pe)
            flow_tensor(pe)
            attention_tensor(pe, 4, 2)
            for g in range(4):
                norm_tensor(pe, 4, g)
            sequence_tensor(pe)

        @block.gpsimd
        def _(gp):
            hyena_gpsimd(gp)
            attention_gpsimd(gp, 1, I["at1_w"], I["at1_wout"], 8)
            tokens_gpsimd(gp)
            attention_gpsimd(gp, 4, I["at4_w"], I["at4_wout"], 2)

        @block.scalar
        def _(a):
            hyena_scalar(a)
            attention_scalar(a, 1, 8)
            tokens_scalar(a)
            flow_scalar(a)
            attention_scalar(a, 4, 2)
            sequence_scalar(a)

        @block.vector
        def _(v):
            hyena_vector(v)
            attention_vector(v, 1, 8)
            tokens_vector(v)
            flow_vector(v)
            attention_vector(v, 4, 2)
            sequence_vector(v)


def _transforms():
    f = np.arange(256)
    t = np.arange(512)
    ang = 2 * np.pi * (((2 * f[:, None] + 1) * t[None, :]) % 2048) / 2048.0
    cos, sin = np.cos(ang), np.sin(ang)
    fwd = np.zeros((P, 4, 4, P), np.float32)
    inv = np.zeros((P, 2, 2, 2, 256), np.float32)
    for e in range(2):
        for j in range(2):
            tt = 2 * (128 * j + np.arange(P)) + e
            for g in range(2):
                fwd[:, 2 * e + j, 2 * g, :] = cos[g * P:(g + 1) * P, tt].T
                fwd[:, 2 * e + j, 2 * g + 1, :] = -sin[g * P:(g + 1) * P, tt].T
        tt = 2 * np.arange(256) + e
        for g in range(2):
            inv[:, e, g, 0, :] = cos[g * P:(g + 1) * P, tt] / 512.0
            inv[:, e, g, 1, :] = -sin[g * P:(g + 1) * P, tt] / 512.0
    return fwd, inv


def _rows(w, pad=None):
    w = np.asarray(w)
    if pad and w.shape[0] < pad:
        w = np.concatenate([w, np.zeros((pad - w.shape[0],) + w.shape[1:], w.dtype)])
    return np.ascontiguousarray(w.reshape(-1, P, *w.shape[1:]).swapaxes(0, 1))


def _attention(wq, wk, wv, wout):
    pairs = wq.shape[1] // P
    w = np.zeros((pairs + 1, P, 6, P), np.float32)
    for n, m in enumerate((wq, wk, wv)):
        r = _rows(m, 256)
        w[:pairs, :, 2 * n:2 * n + 2, :] = r.reshape(P, 2, pairs, P).transpose(2, 0, 1, 3)
    return w, np.ascontiguousarray(wout.reshape(pairs, P, D).swapaxes(0, 1))


def _experts(w1, b1, w2):
    e, _, f = w1.shape
    one = w1.reshape(e, DK, P, f).transpose(0, 2, 1, 3).reshape(e, P, DK * f)
    bias = b1.reshape(e, f // P, P).transpose(0, 2, 1)
    two = w2.reshape(e, f // P, P, D).transpose(0, 2, 1, 3)
    return np.ascontiguousarray(np.concatenate([one, bias], 2)), np.ascontiguousarray(two)


def layouts(x, ctx_768, **W):
    a = {}
    order = np.concatenate([np.arange(0, L, 2), np.arange(1, L, 2)])
    xo = np.asarray(x)[:, order, :].reshape(T, D)
    a["x_tok"] = np.ascontiguousarray(xo.reshape(NT, P, D).transpose(1, 0, 2))
    a["x_feat"] = _rows(xo.T)
    a["ctx_feat"] = _rows(np.asarray(ctx_768).reshape(T, DC).T, 256)
    a["hy_win"] = _rows(W["L0_attn_W_in"].T)
    a["hy_wout"] = _rows(W["L0_attn_W_out"].T)
    time = np.linspace(0.0, 1.0, L, dtype=np.float32)[order]
    a["time"] = np.ascontiguousarray(np.broadcast_to(time, (P, L)))
    a["f_w1"] = np.ascontiguousarray(W["L0_attn_f_w1"][:, :, 0].T)
    a["f_b1"] = np.ascontiguousarray(W["L0_attn_f_b1"].T)
    a["f_w2b"] = np.ascontiguousarray(np.concatenate(
        [W["L0_attn_f_w2"].transpose(2, 0, 1), W["L0_attn_f_b2"][None]]))
    a["dft_fwd"], a["dft_inv"] = _transforms()
    a["ident"] = np.eye(P, dtype=np.float32)
    a["head_mask"] = np.kron(np.eye(8), np.ones((16, 16))).astype(np.float32)
    a["rank8"] = np.ascontiguousarray(np.broadcast_to(8 - np.arange(8, dtype=np.float32), (P, 8)))
    a["bias_row"] = np.ascontiguousarray(np.broadcast_to(np.stack(
        [W["L0_xattn_b_out"], W["L1_attn_bo"], W["L1_xattn_bo"]]), (P, 3, D)))
    a["gb_row"] = np.ascontiguousarray(np.broadcast_to(np.stack(
        [W["L1_ffn_gamma"], W["L1_ffn_beta"]]), (P, 2, D)))
    kv = W["L0_xattn_w_kv"]
    a["at1_w"], a["at1_wout"] = _attention(W["L0_xattn_w_q"], kv[:, :1024], kv[:, 1024:], W["L0_xattn_w_out"])
    a["at4_w"], a["at4_wout"] = _attention(W["L1_xattn_Wq"].T, W["L1_xattn_Wk"].T, W["L1_xattn_Wv"].T,
                                           W["L1_xattn_Wo"].T)
    a["mo_wg"] = _rows(W["L0_ffn_Wg"])
    a["mo_w1"] = np.ascontiguousarray(W["L0_ffn_W1"].reshape(E8, DK, P, FF0).transpose(2, 0, 1, 3).reshape(P, E8, -1))
    a["mo_w2"] = np.ascontiguousarray(W["L0_ffn_W2"].reshape(E8, 4, P, D).transpose(2, 0, 1, 3).reshape(P, E8, -1))
    spread = lambda x: np.ascontiguousarray(np.broadcast_to(x, (P,) + x.shape))
    a["mo_b1"], a["mo_b2"] = spread(W["L0_ffn_b1"]), spread(W["L0_ffn_b2"])
    a["mo_lt8"] = spread(np.tril(np.ones((E8, E8), np.float32), -1))
    a["mo_step128"] = spread(np.arange(16, dtype=np.float32) * P)
    a["mo_iota"] = spread(np.arange(SLOT_TILES, dtype=np.float32))
    a["mo_number"] = (np.arange(P)[:, None] + P * np.arange(NT)[None]).astype(np.float32)
    a["mo_spare"] = (2 * T + np.arange(P)[:, None] + P * np.arange(SLOT_TILES)[None]).astype(np.float32)
    a["mo_before"] = np.triu(np.ones((P, P), np.float32), 1)
    a["fl_w"] = np.ascontiguousarray(np.stack([_rows(W[f"L1_attn_W{n}"].T) for n in "qkvo"], 1))
    spread8 = np.zeros((16, 8, 16, P), np.float32)
    for n in range(16):
        spread8[n, :, n] = np.kron(np.eye(8), np.ones((1, 16)))
    a["fl_spread"] = spread8.reshape(P, 16, P)
    a["fl_bias"] = np.ascontiguousarray(np.stack([W[f"L1_attn_b{n}"].reshape(DK, P).T for n in "qkv"], 1))
    a["se_wr"] = _rows(W["L1_ffn_Wr"])
    a["se_br"] = np.ascontiguousarray(np.broadcast_to(W["L1_ffn_br"], (P, E8)))
    a["se_w1"], w2 = _experts(W["L1_ffn_W1"], W["L1_ffn_b1"], W["L1_ffn_W2"])
    a["se_w2"] = np.ascontiguousarray(np.concatenate(
        [w2.reshape(E8, P, -1), np.broadcast_to(W["L1_ffn_b2"][:, None, :], (E8, P, D))], 2))
    return a


def program(nc, arrays):
    I = {n: nc.dram_tensor("in_" + n, a.shape, mybir.dt.from_np(a.dtype), kind="ExternalInput").ap() for n, a in arrays.items()}
    out = nc.dram_tensor("out", (B, L, D), F32, kind="ExternalOutput").ap()
    build(nc, I, out)


def kernel(**inputs):
    import concourse.bacc as _bacc
    from concourse.bass_utils import run_bass_kernel_spmd as _run

    nc = _bacc.Bacc("TRN2", target_bir_lowering=False, num_devices=1)
    arrays = layouts(**{k: np.asarray(v) for k, v in inputs.items()})
    program(nc, arrays)
    r = _run(nc, [{"in_" + k: v for k, v in arrays.items()}], core_ids=[0])
    return r.results[0]["out"]
```
